# Optimizing a Trainium2 kernel written in Bass

```python
import numpy as np
import jax
import jax.numpy as jnp

def _softmax(x, axis=-1):
    return jax.nn.softmax(x, axis=axis)

def _gelu(x):
    return jax.nn.gelu(x, approximate=True)

def _silu(x):
    return jax.nn.silu(x)

def _sigmoid(x):
    return jax.nn.sigmoid(x)

def _layernorm(x, axis=-1, eps=1e-05):
    m = jnp.mean(x, axis=axis, keepdims=True)
    v = jnp.var(x, axis=axis, keepdims=True)
    return (x - m) / jnp.sqrt(v + eps)

def _scatter_add(tgt, idx, src, axis=0):
    return tgt.at[idx].add(src)

def _segment_sum(src, seg, n):
    return jax.ops.segment_sum(src, seg, n)
kernel_name = 'mk_flamingo_gated_d2_seqx_r8_a36678'

def setup_inputs(seed: int=0):
    np.random.seed(seed)
    _w = jnp.asarray

    def _rec_inputs():
        import jax
        import jax.numpy as jnp
        _rk = jax.random.key(seed)
        x = -0.0002928 + 1 * jax.random.normal(jax.random.fold_in(_rk, 1), (16, 128, 128), jnp.float32)
        _lenS = 128 - jax.random.randint(jax.random.fold_in(_rk, 7), (16,), 0, max(1, 128 // 4) + 1, jnp.int32)
        _lenS2 = 128 - jax.random.randint(jax.random.fold_in(_rk, 8), (16,), 0, max(1, 128 // 4) + 1, jnp.int32)
        _ctx_1024P = jax.random.normal(jax.random.fold_in(_rk, 11), (16, 16, 128), jnp.float32)
        _ctx_1024c = jax.random.dirichlet(jax.random.fold_in(_rk, 511), 0.3 * jnp.ones((16,), jnp.float32), (16, 128))
        _ctx_1024t = jnp.einsum('bsk,bkd->bsd', _ctx_1024c, _ctx_1024P)
        _ctx_1024t = _ctx_1024t * jax.lax.rsqrt(jnp.mean(jnp.square(_ctx_1024t)) + 1e-12) * 0.953939
        ctx_1024 = -1.39393e-06 + 0.999914 * (_ctx_1024t + 0.3 * jax.random.normal(jax.random.fold_in(_rk, 611), (16, 128, 128), jnp.float32))
        fside_BxSx4_0 = jax.random.uniform(jax.random.fold_in(_rk, 12), (16, 128, 4), jnp.float32, 0.0, 0.999884)
        _validS = jnp.arange(128)[None, :] < _lenS[:, None]
        _validS2 = jnp.arange(128)[None, :] < _lenS2[:, None]
        _causal = jnp.tril(jnp.ones((128, 128), dtype=bool))
        mask_Bx1x1xS2_ik0 = jnp.where(jnp.broadcast_to(_validS2[:, None, None, :], (16, 1, 1, 128)), 0, 1).astype(jnp.int32)
        _g = jax.random.normal(jax.random.fold_in(_rk, 9001), (2, 2), jnp.float32)
        _g = jnp.sign(_g) * jnp.maximum(jnp.abs(_g), 1.0) + (_g == 0) * 1.0
        g_xattn = _g[0]
        g_ffn = _g[1]
        return (x, ctx_1024, fside_BxSx4_0, mask_Bx1x1xS2_ik0, g_xattn, g_ffn)
    x, ctx_1024, fside_BxSx4_0, mask_Bx1x1xS2_ik0, g_xattn, g_ffn = _rec_inputs()

    def _L0_xattn_setup():
        import jax, jax.numpy as jnp
        import numpy as np
        D_MODEL = 128
        H = 16
        D_K = 64
        D_V = 64
        D_G = D_MODEL // H
        WAVE_LEN = 1000.0
        B = 8
        N = 64

        def box_relational_embedding(boxes, dim_g=D_G):
            x_min, y_min, x_max, y_max = jnp.split(boxes, 4, axis=-1)
            cx = (x_min + x_max) * 0.5
            cy = (y_min + y_max) * 0.5
            w = x_max - x_min + 1.0
            h = y_max - y_min + 1.0
            delta_x = jnp.log(jnp.clip(jnp.abs((cx - jnp.swapaxes(cx, 1, 2)) / w), 0.001, None))
            delta_y = jnp.log(jnp.clip(jnp.abs((cy - jnp.swapaxes(cy, 1, 2)) / h), 0.001, None))
            delta_w = jnp.log(w / jnp.swapaxes(w, 1, 2))
            delta_h = jnp.log(h / jnp.swapaxes(h, 1, 2))
            pos = jnp.stack([delta_x, delta_y, delta_w, delta_h], axis=-1)
            n_freq = dim_g // 8
            feat_range = jnp.arange(n_freq, dtype=jnp.float32)
            dim_mat = 1.0 / WAVE_LEN ** (feat_range / n_freq)
            mul = (100.0 * pos)[..., None] * dim_mat
            b, n = (pos.shape[0], pos.shape[1])
            mul = mul.reshape(b, n, n, 4 * n_freq)
            return jnp.concatenate([jnp.sin(mul), jnp.cos(mul)], axis=-1)
        key = jax.random.key(seed)
        ks = jax.random.split(key, 12)
        s = 0.02
        inp = {'queries': jax.random.normal(ks[0], (B, N, D_MODEL), jnp.float32), 'keys': jax.random.normal(ks[1], (B, N, D_MODEL), jnp.float32), 'values': jax.random.normal(ks[2], (B, N, D_MODEL), jnp.float32), 'boxes': jax.random.uniform(ks[3], (B, N, 4), jnp.float32), 'Wq': jax.random.normal(ks[4], (H * D_K, D_MODEL), jnp.float32) * s, 'bq': jnp.zeros((H * D_K,), jnp.float32), 'Wk': jax.random.normal(ks[5], (H * D_K, D_MODEL), jnp.float32) * s, 'bk': jnp.zeros((H * D_K,), jnp.float32), 'Wv': jax.random.normal(ks[6], (H * D_V, D_MODEL), jnp.float32) * s, 'bv': jnp.zeros((H * D_V,), jnp.float32), 'Wo': jax.random.normal(ks[7], (D_MODEL, H * D_V), jnp.float32) * s, 'bo': jnp.zeros((D_MODEL,), jnp.float32), 'Wg': jax.random.normal(ks[8], (H, D_G), jnp.float32) * s, 'bg': jnp.zeros((H,), jnp.float32)}
        return inp
    _L0_xattn_all = _L0_xattn_setup()
    _L0_xattn_in = {k: v for k, v in _L0_xattn_all.items() if k in ('Wq', 'bq', 'Wk', 'bk', 'Wv', 'bv', 'Wo', 'bo', 'Wg', 'bg')}
    del _L0_xattn_all

    def _L0_ffn_setup():
        import jax, jax.numpy as jnp
        import numpy as np
        B, T, D, E, H = (4, 256, 128, 4, 8)
        EPS = 1e-05

        def _uniform(k, shape, bound):
            return jax.random.uniform(k, shape, jnp.float32, -bound, bound)

        def _layernorm(x, w, b):
            mu = jnp.mean(x, axis=-1, keepdims=True)
            var = jnp.mean(jnp.square(x - mu), axis=-1, keepdims=True)
            return (x - mu) * jax.lax.rsqrt(var + EPS) * w + b
        key = jax.random.key(seed)
        ks = jax.random.split(key, 12)
        wb = np.sqrt(6.0 / D) / np.sqrt(6.0)
        wb = 1.0 / np.sqrt(D)
        return {'x': jax.random.normal(ks[0], (B, T, D), jnp.float32), 'router_prob': jax.random.uniform(ks[1], (B, T, E), jnp.float32), 'norm_w': jnp.ones((D,), jnp.float32), 'norm_b': jnp.zeros((D,), jnp.float32), 'q_w': _uniform(ks[2], (D, D), wb), 'q_b': _uniform(ks[3], (D,), wb), 'k_w': _uniform(ks[4], (D, D), wb), 'k_b': _uniform(ks[5], (D,), wb), 'v_w': _uniform(ks[6], (D, D), wb), 'v_b': _uniform(ks[7], (D,), wb), 'o_w': _uniform(ks[8], (D, D), wb), 'o_b': _uniform(ks[9], (D,), wb)}
    _L0_ffn_all = _L0_ffn_setup()
    _L0_ffn_in = {k: v for k, v in _L0_ffn_all.items() if k in ('router_prob', 'norm_w', 'norm_b', 'q_w', 'q_b', 'k_w', 'k_b', 'v_w', 'v_b', 'o_w', 'o_b')}
    del _L0_ffn_all

    def _L1_xattn_setup():
        import jax, jax.numpy as jnp
        import numpy as np
        D_MODEL = 128
        NUM_HEADS = 16
        D_K = D_MODEL // NUM_HEADS
        MAX_REL = 128
        key = jax.random.key(seed)
        ks = jax.random.split(key, 16)
        B, S = (4, 256)
        s = 1.0 / np.sqrt(D_MODEL)
        inp = {'query': jax.random.normal(ks[0], (B, S, D_MODEL), jnp.float32), 'key': jax.random.normal(ks[1], (B, S, D_MODEL), jnp.float32), 'value': jax.random.normal(ks[2], (B, S, D_MODEL), jnp.float32), 'mask': jax.random.randint(ks[3], (B, 1, 1, S), 0, 2, jnp.int32), 'Wq': jax.random.normal(ks[4], (D_MODEL, D_MODEL), jnp.float32) * s, 'bq': jax.random.normal(ks[5], (D_MODEL,), jnp.float32) * 0.02, 'Wk': jax.random.normal(ks[6], (D_MODEL, D_MODEL), jnp.float32) * s, 'bk': jax.random.normal(ks[7], (D_MODEL,), jnp.float32) * 0.02, 'Wv': jax.random.normal(ks[8], (D_MODEL, D_MODEL), jnp.float32) * s, 'bv': jax.random.normal(ks[9], (D_MODEL,), jnp.float32) * 0.02, 'Wo': jax.random.normal(ks[10], (D_MODEL, D_MODEL), jnp.float32) * s, 'bo': jax.random.normal(ks[11], (D_MODEL,), jnp.float32) * 0.02, 'rel_emb': jax.random.normal(ks[12], (2 * MAX_REL + 1, NUM_HEADS), jnp.float32) * 0.02}
        return inp
    _L1_xattn_all = _L1_xattn_setup()
    _L1_xattn_in = {k: v for k, v in _L1_xattn_all.items() if k in ('Wq', 'bq', 'Wk', 'bk', 'Wv', 'bv', 'Wo', 'bo', 'rel_emb')}
    del _L1_xattn_all

    def _L1_ffn_setup():
        import jax, jax.numpy as jnp
        import numpy as np
        B, T = (2, 256)
        D_MODEL, D_HIDDEN = (128, 256)
        N_EXPERTS, TOP_K = (8, 2)
        N_TOKENS = B * T
        CAPACITY = 2 * N_TOKENS * TOP_K // N_EXPERTS
        key = jax.random.key(seed)
        k_x, k_rw, k_w, k_v, k_o = jax.random.split(key, 5)
        x = jax.random.normal(k_x, (B, T, D_MODEL), jnp.float32)
        router_w = jax.random.normal(k_rw, (N_EXPERTS, D_MODEL), jnp.float32) * D_MODEL ** (-0.5)
        router_b = jnp.zeros((N_EXPERTS,), jnp.float32)
        W = jax.random.normal(k_w, (N_EXPERTS, D_MODEL, D_HIDDEN), jnp.float32) * D_MODEL ** (-0.5)
        V = jax.random.normal(k_v, (N_EXPERTS, D_MODEL, D_HIDDEN), jnp.float32) * D_MODEL ** (-0.5)
        W_out = jax.random.normal(k_o, (N_EXPERTS, D_HIDDEN, D_MODEL), jnp.float32) * D_HIDDEN ** (-0.5)
        return {'x': x, 'router_w': router_w, 'router_b': router_b, 'W': W, 'V': V, 'W_out': W_out}
    _L1_ffn_all = _L1_ffn_setup()
    _L1_ffn_in = {k: v for k, v in _L1_ffn_all.items() if k in ('router_w', 'router_b', 'W', 'V', 'W_out')}
    del _L1_ffn_all
    return {'x': x, 'ctx_1024': ctx_1024, 'fside_BxSx4_0': fside_BxSx4_0, 'mask_Bx1x1xS2_ik0': mask_Bx1x1xS2_ik0, 'g_xattn': g_xattn, 'g_ffn': g_ffn, 'L0_xattn_Wq': _L0_xattn_in['Wq'], 'L0_xattn_bq': _L0_xattn_in['bq'], 'L0_xattn_Wk': _L0_xattn_in['Wk'], 'L0_xattn_bk': _L0_xattn_in['bk'], 'L0_xattn_Wv': _L0_xattn_in['Wv'], 'L0_xattn_bv': _L0_xattn_in['bv'], 'L0_xattn_Wo': _L0_xattn_in['Wo'], 'L0_xattn_bo': _L0_xattn_in['bo'], 'L0_xattn_Wg': _L0_xattn_in['Wg'], 'L0_xattn_bg': _L0_xattn_in['bg'], 'L0_ffn_router_prob': _L0_ffn_in['router_prob'], 'L0_ffn_norm_w': _L0_ffn_in['norm_w'], 'L0_ffn_norm_b': _L0_ffn_in['norm_b'], 'L0_ffn_q_w': _L0_ffn_in['q_w'], 'L0_ffn_q_b': _L0_ffn_in['q_b'], 'L0_ffn_k_w': _L0_ffn_in['k_w'], 'L0_ffn_k_b': _L0_ffn_in['k_b'], 'L0_ffn_v_w': _L0_ffn_in['v_w'], 'L0_ffn_v_b': _L0_ffn_in['v_b'], 'L0_ffn_o_w': _L0_ffn_in['o_w'], 'L0_ffn_o_b': _L0_ffn_in['o_b'], 'L1_xattn_Wq': _L1_xattn_in['Wq'], 'L1_xattn_bq': _L1_xattn_in['bq'], 'L1_xattn_Wk': _L1_xattn_in['Wk'], 'L1_xattn_bk': _L1_xattn_in['bk'], 'L1_xattn_Wv': _L1_xattn_in['Wv'], 'L1_xattn_bv': _L1_xattn_in['bv'], 'L1_xattn_Wo': _L1_xattn_in['Wo'], 'L1_xattn_bo': _L1_xattn_in['bo'], 'L1_xattn_rel_emb': _L1_xattn_in['rel_emb'], 'L1_ffn_router_w': _L1_ffn_in['router_w'], 'L1_ffn_router_b': _L1_ffn_in['router_b'], 'L1_ffn_W': _L1_ffn_in['W'], 'L1_ffn_V': _L1_ffn_in['V'], 'L1_ffn_W_out': _L1_ffn_in['W_out']}

def reference(x, ctx_1024, fside_BxSx4_0, mask_Bx1x1xS2_ik0, g_xattn, g_ffn, L0_xattn_Wq, L0_xattn_bq, L0_xattn_Wk, L0_xattn_bk, L0_xattn_Wv, L0_xattn_bv, L0_xattn_Wo, L0_xattn_bo, L0_xattn_Wg, L0_xattn_bg, L0_ffn_router_prob, L0_ffn_norm_w, L0_ffn_norm_b, L0_ffn_q_w, L0_ffn_q_b, L0_ffn_k_w, L0_ffn_k_b, L0_ffn_v_w, L0_ffn_v_b, L0_ffn_o_w, L0_ffn_o_b, L1_xattn_Wq, L1_xattn_bq, L1_xattn_Wk, L1_xattn_bk, L1_xattn_Wv, L1_xattn_bv, L1_xattn_Wo, L1_xattn_bo, L1_xattn_rel_emb, L1_ffn_router_w, L1_ffn_router_b, L1_ffn_W, L1_ffn_V, L1_ffn_W_out):
    import jax
    import jax.numpy as jnp

    def _L0_xattn_ref(queries, keys, values, boxes, Wq, bq, Wk, bk, Wv, bv, Wo, bo, Wg, bg):
        import jax, jax.numpy as jnp
        import numpy as np
        D_MODEL = 128
        H = 16
        D_K = 64
        D_V = 64
        D_G = D_MODEL // H
        WAVE_LEN = 1000.0
        B = 8
        N = 64

        def box_relational_embedding(boxes, dim_g=D_G):
            x_min, y_min, x_max, y_max = jnp.split(boxes, 4, axis=-1)
            cx = (x_min + x_max) * 0.5
            cy = (y_min + y_max) * 0.5
            w = x_max - x_min + 1.0
            h = y_max - y_min + 1.0
            delta_x = jnp.log(jnp.clip(jnp.abs((cx - jnp.swapaxes(cx, 1, 2)) / w), 0.001, None))
            delta_y = jnp.log(jnp.clip(jnp.abs((cy - jnp.swapaxes(cy, 1, 2)) / h), 0.001, None))
            delta_w = jnp.log(w / jnp.swapaxes(w, 1, 2))
            delta_h = jnp.log(h / jnp.swapaxes(h, 1, 2))
            pos = jnp.stack([delta_x, delta_y, delta_w, delta_h], axis=-1)
            n_freq = dim_g // 8
            feat_range = jnp.arange(n_freq, dtype=jnp.float32)
            dim_mat = 1.0 / WAVE_LEN ** (feat_range / n_freq)
            mul = (100.0 * pos)[..., None] * dim_mat
            b, n = (pos.shape[0], pos.shape[1])
            mul = mul.reshape(b, n, n, 4 * n_freq)
            return jnp.concatenate([jnp.sin(mul), jnp.cos(mul)], axis=-1)
        b, nq, _ = queries.shape
        nk = keys.shape[1]
        emb = box_relational_embedding(boxes)
        g = jax.nn.relu(jnp.einsum('bnmd,hd->bhnm', emb, Wg) + bg[None, :, None, None])
        q = (queries @ Wq.T + bq).reshape(b, nq, H, D_K).transpose(0, 2, 1, 3)
        k = (keys @ Wk.T + bk).reshape(b, nk, H, D_K).transpose(0, 2, 1, 3)
        v = (values @ Wv.T + bv).reshape(b, nk, H, D_V).transpose(0, 2, 1, 3)
        a = jnp.einsum('bhqd,bhkd->bhqk', q, k) / jnp.sqrt(jnp.float32(D_K))
        mn = jax.nn.softmax(jnp.log(jnp.clip(g, 1e-06, None)) + a, axis=-1)
        out = jnp.einsum('bhqk,bhkd->bqhd', mn, v).reshape(b, nq, H * D_V)
        return out @ Wo.T + bo

    def _L0_ffn_ref(x, router_prob, norm_w, norm_b, q_w, q_b, k_w, k_b, v_w, v_b, o_w, o_b):
        import jax, jax.numpy as jnp
        import numpy as np
        B, T, D, E, H = (4, 256, 128, 4, 8)
        EPS = 1e-05

        def _uniform(k, shape, bound):
            return jax.random.uniform(k, shape, jnp.float32, -bound, bound)

        def _layernorm(x, w, b):
            mu = jnp.mean(x, axis=-1, keepdims=True)
            var = jnp.mean(jnp.square(x - mu), axis=-1, keepdims=True)
            return (x - mu) * jax.lax.rsqrt(var + EPS) * w + b
        e_cnt = router_prob.shape[2]
        b, t, d = x.shape
        n = t // e_cnt
        h = H
        scale = d ** (-0.5)
        qs, ks_, vs = ([], [], [])
        for e in range(e_cnt):
            xe = x[:, e * n:(e + 1) * n, :]
            xn = _layernorm(xe, norm_w, norm_b)
            m = d // 2 ** e
            xm = xn[..., :m]
            qs.append(jnp.einsum('bnm,dm->bnd', xm, q_w[:, :m]) + q_b)
            ks_.append(jnp.einsum('bnm,dm->bnd', xm, k_w[:, :m]) + k_b)
            vs.append(jnp.einsum('bnm,dm->bnd', xm, v_w[:, :m]) + v_b)
        q = jnp.concatenate(qs, axis=1)
        k = jnp.concatenate(ks_, axis=1)
        v = jnp.concatenate(vs, axis=1)
        dh = d // h
        q = q.reshape(b, t, h, dh).transpose(0, 2, 1, 3)
        k = k.reshape(b, t, h, dh).transpose(0, 2, 1, 3)
        v = v.reshape(b, t, h, dh).transpose(0, 2, 1, 3)
        attn = jnp.einsum('bhqd,bhkd->bhqk', q, k) * scale
        attn = jax.nn.softmax(attn, axis=-1)
        attn_out = jnp.einsum('bhqk,bhkd->bhqd', attn, v)
        attn_out = attn_out.transpose(0, 2, 1, 3).reshape(b, t, d)
        outs = []
        for e in range(e_cnt):
            sl = slice(e * n, (e + 1) * n)
            m = d // 2 ** e
            xm = attn_out[:, sl, :m]
            out = jnp.einsum('bnm,om->bno', xm, o_w[:m, :m]) + o_b[:m]
            pad = d - m
            if pad:
                out = jnp.pad(out, ((0, 0), (0, 0), (0, pad)))
            outs.append(out + x[:, sl, :])
        return jnp.concatenate(outs, axis=1)

    def _L1_xattn_ref(query, key, value, mask, Wq, bq, Wk, bk, Wv, bv, Wo, bo, rel_emb):
        import jax, jax.numpy as jnp
        import numpy as np
        D_MODEL = 128
        NUM_HEADS = 16
        D_K = D_MODEL // NUM_HEADS
        MAX_REL = 128
        B, S, D = query.shape
        H, dk = (NUM_HEADS, D_K)

        def proj(x, W, b):
            return (x @ W.T + b).reshape(B, S, H, dk).transpose(0, 2, 1, 3)
        Q = proj(query, Wq, bq)
        K = proj(key, Wk, bk)
        V = proj(value, Wv, bv)
        scores = jnp.einsum('bhqd,bhkd->bhqk', Q, K) / jnp.sqrt(jnp.float32(dk))
        pos = jnp.arange(S)
        rel = jnp.clip(pos[None, :] - pos[:, None], -MAX_REL, MAX_REL) + MAX_REL
        bias = rel_emb[rel].transpose(2, 0, 1)
        scores = scores + bias[None]
        scores = jnp.where(mask == 0, -jnp.inf, scores)
        weights = jax.nn.softmax(scores, axis=-1)
        weights = jnp.nan_to_num(weights, nan=0.0)
        context = jnp.einsum('bhqk,bhkd->bhqd', weights, V)
        context = context.transpose(0, 2, 1, 3).reshape(B, S, D)
        return context @ Wo.T + bo

    def _L1_ffn_ref(x, router_w, router_b, W, V, W_out):
        import jax, jax.numpy as jnp
        import numpy as np
        B, T = (2, 256)
        D_MODEL, D_HIDDEN = (128, 256)
        N_EXPERTS, TOP_K = (8, 2)
        N_TOKENS = B * T
        CAPACITY = 2 * N_TOKENS * TOP_K // N_EXPERTS
        Bq, Tq, D = x.shape
        N = Bq * Tq
        x_flat = x.reshape(N, D)
        router_logits = x_flat @ router_w.T + router_b
        top_vals, top_ids = jax.lax.top_k(router_logits, TOP_K)
        top_probs = jax.nn.softmax(top_vals, axis=-1)
        x_pad = jnp.concatenate([x_flat, jnp.zeros((1, D), x_flat.dtype)], axis=0)
        probs_pad = jnp.concatenate([top_probs, jnp.zeros((1, TOP_K), top_probs.dtype)], axis=0)
        out = jnp.zeros((N + 1, D), x_flat.dtype)
        for e in range(N_EXPERTS):
            tok, slot = jnp.nonzero(top_ids == e, size=CAPACITY, fill_value=(N, 0))
            w = probs_pad[tok, slot][:, None]
            xin = x_pad[tok]
            a = xin @ W[e]
            b = xin @ V[e]
            y = a * (b * jax.nn.sigmoid(b)) @ W_out[e]
            out = out.at[tok].add(y * w)
        return out[:N].reshape(Bq, Tq, D)
    x = x + jnp.tanh(g_xattn[0]) * _L0_xattn_ref(_layernorm(x, axis=-1), ctx_1024, ctx_1024, fside_BxSx4_0, L0_xattn_Wq, L0_xattn_bq, L0_xattn_Wk, L0_xattn_bk, L0_xattn_Wv, L0_xattn_bv, L0_xattn_Wo, L0_xattn_bo, L0_xattn_Wg, L0_xattn_bg)
    x = x + jnp.tanh(g_ffn[0]) * _L0_ffn_ref(_layernorm(x, axis=-1), L0_ffn_router_prob, L0_ffn_norm_w, L0_ffn_norm_b, L0_ffn_q_w, L0_ffn_q_b, L0_ffn_k_w, L0_ffn_k_b, L0_ffn_v_w, L0_ffn_v_b, L0_ffn_o_w, L0_ffn_o_b)
    x = x + jnp.tanh(g_xattn[1]) * _L1_xattn_ref(_layernorm(x, axis=-1), ctx_1024, ctx_1024, mask_Bx1x1xS2_ik0, L1_xattn_Wq, L1_xattn_bq, L1_xattn_Wk, L1_xattn_bk, L1_xattn_Wv, L1_xattn_bv, L1_xattn_Wo, L1_xattn_bo, L1_xattn_rel_emb)
    x = x + jnp.tanh(g_ffn[1]) * _L1_ffn_ref(_layernorm(x, axis=-1), L1_ffn_router_w, L1_ffn_router_b, L1_ffn_W, L1_ffn_V, L1_ffn_W_out)
    return x

_drawn_inputs = setup_inputs


def setup_inputs(seed=0):
    import zlib

    import numpy as np

    out = dict(_drawn_inputs(seed))
    spreads = {'g_ffn': (-1.0, 0.2),
     'L0_xattn_bq': (0.0, 0.8),
     'L0_xattn_bk': (0.0, 0.8),
     'L0_xattn_bv': (0.0, 0.1),
     'L0_xattn_bo': (0.0, 0.1),
     'L0_xattn_bg': (0.0, 0.1),
     'L0_ffn_norm_w': (1.0, 0.6),
     'L0_ffn_norm_b': (0.0, 0.1),
     'L1_ffn_router_b': (0.0, 0.1)}
    factors = {'L0_xattn_Wq': 8.0,
     'L0_xattn_Wk': 4.652,
     'L0_ffn_q_b': 4.66,
     'L0_ffn_k_w': 3.158,
     'L0_ffn_k_b': 8.0,
     'L1_xattn_bk': 8.0}
    for name, (base, spread) in spreads.items():
        noise = np.random.default_rng([zlib.crc32(name.encode()), seed]).standard_normal(out[name].shape)
        drawn = base * np.exp(spread * noise) if base else spread * noise
        out[name] = jnp.asarray(drawn.astype(out[name].dtype))
    for name, factor in factors.items():
        out[name] = (out[name] * factor).astype(out[name].dtype)
    return out
```

```python
import math
from contextlib import ExitStack

import numpy as np
import concourse.bass as bass
from concourse import mybir

F32 = mybir.dt.float32
I32 = mybir.dt.int32
U32 = mybir.dt.uint32
ALU = mybir.AluOpType
ACT = mybir.ActivationFunctionType
AX = mybir.AxisListType

B, S, D = 16, 128, 128
NH, DK = 16, 64
PAIRS = NH * DK // 128
NF, NPF = 8, 16
NC = S // NPF
EPS = 1e-5
GMIN = 1e-6
NEG = -1e30
TWO_PI = 2.0 * math.pi
PI_HI = 6.28125
PI_LO = TWO_PI - PI_HI
ROUND = 1.5 * 2.0 ** 23
PI_SAFE = 3.1415925
NE, HID, CAP = 8, 256, 256
SLOTS = NE * CAP
LAST = B - 1


def wait(eng, sem, value):
    if isinstance(value, int) and value <= 0:
        return
    eng.wait_ge(sem, value)


def over_batches(eng, body, tail=1):
    body(0, 0, 0, 0)
    body(1, 1, 1, 0)
    with eng.Fori(1, B // 2 - tail) as it:
        body(it * 2, 0, None, it)
        body(it * 2 + 1, 1, None, it)
    for b in range(B - 2 * tail, B):
        body(b, b % 2, b, b // 2)


class Stage:

    def __init__(self, sem, name, slots, width, nested):
        self.name = name
        self.NS = slots
        self.dh = width
        self.nested = nested
        self.OJ = slots + 2
        self.primed = 4
        self.s_S = sem(f"s_S_{name}")
        self.s_mx = sem(f"s_mx_{name}")
        self.s_exp = sem(f"s_exp_{name}")
        self.s_T = sem(f"s_T_{name}")
        self.s_Te = sem(f"s_Te_{name}")
        self.s_Of = sem(f"s_Of_{name}")
        self.s_Oe = sem(f"s_Oe_{name}")
        self.s_qk = sem(f"s_qk_{name}")
        self.s_qke = sem(f"s_qke_{name}")
        self.s_kz = sem(f"s_kz_{name}")
        self.s_V = sem(f"s_V_{name}")
        self.s_Ve = sem(f"s_Ve_{name}")
        self.s_st = sem(f"s_st_{name}")
        self.s_mv = sem(f"s_mv_{name}")
        self.s_var = sem(f"s_var_{name}")
        self.s_rstd = sem(f"s_rstd_{name}")
        self.s_h = sem(f"s_h_{name}")
        self.s_rs = sem(f"s_rs_{name}")
        self.s_rsr = sem(f"s_rsr_{name}")
        self.s_x = sem(f"s_x_{name}")
        self.s_w = sem(f"s_w_{name}")
        self.s_cst = sem(f"s_cst_{name}")
        if nested:
            self.s_h1 = sem(f"s_h1_{name}")
            self.s_st2 = sem(f"s_st2_{name}")
            self.s_mv2 = sem(f"s_mv2_{name}")
            self.s_var2 = sem(f"s_var2_{name}")
            self.s_rstd2 = sem(f"s_rstd2_{name}")
            self.s_xn = sem(f"s_xn_{name}")
            self.s_xnw = sem(f"s_xnw_{name}")
            self.s_res = sem(f"s_res_{name}")
        else:
            self.s_add = sem(f"s_add_{name}")
            self.s_bm = sem(f"s_bm_{name}")
            self.s_ctx = [sem(f"s_ctx{i}_{name}") for i in range(2)]

    def pv_done(self, b, g):
        while g < 0:
            g += self.NS
            b = b - 1
        if g < self.NS - 2:
            return b * self.OJ + (4 + g + 1)
        return (b + 1) * self.OJ + (g - (self.NS - 2) + 1)

    def at(self, g, par):
        return g if self.NS == 4 else 2 * par + g

    @staticmethod
    def vjob(b, i):
        return 2 + i if isinstance(b, int) and b < 0 else b * 2 + (3 + i)


def build_program(nc, A, out, stop=99):
    ctx = ExitStack()
    with ctx:
        def sb(name, shape, dt=F32):
            return ctx.enter_context(nc.sbuf_tensor(name, shape, dt))

        def sem(name):
            return ctx.enter_context(nc.semaphore(name))

        banks = {n: ctx.enter_context(nc.psum_tensor(n, [128, 512], F32))
                 for n in ("S0", "S1", "T0", "T1", "A0", "D0", "D1", "O0")}
        bS = [banks["S0"], banks["S1"]]
        bT = [banks["T0"], banks["T1"]]
        bA, bG, bV, bO = banks["A0"], banks["D0"], banks["D1"], banks["O0"]

        X = sb("X", [128, B, D])
        ident = sb("ident", [128, 128])
        gates = sb("gates", [128, 4])
        graw = sb("graw", [128, 4])
        mhalf = sb("mhalf", [128, 1])
        epst = sb("epst", [128, 1])
        spare = sb("spare", [128, 2])
        E = sb("E", [128, B, NC, S])
        KR = sb("KR", [128, 2, NC * S])
        Wblk = sb("Wblk", [128, 2, 8, NPF])
        wrep = sb("wrep", [128, NH])
        delta = sb("delta", [128, NPF])
        bgp = sb("bgp", [128, 2])
        phase = sb("phase", [128, 4])
        valM = sb("valM", [128, B, S])
        rowM = sb("rowM", [128, B, S])
        pn = sb("pn", [128, 2, B, NC])
        valN = sb("valN", [128, B, NC])
        scl = sb("scl", [128, B, NC])
        G = [sb(f"G{i}", [128, NH, S]) for i in range(2)]
        Gc = [sb(f"Gc{i}", [128, NC, S]) for i in range(2)]
        WqT = sb("WqT", [128, NH * DK])
        WkT = sb("WkT", [128, NH * DK])
        WvT = sb("WvT", [128, NH * DK])
        WoT = sb("WoT", [128, PAIRS, 128])
        bq = sb("bq", [128, PAIRS])
        bk = sb("bk", [128, PAIRS])
        bvb = sb("bvb", [128, NH * DK])
        bob = sb("bob", [128, 128])
        ctxS = [sb(f"ctxS{i}", [128, 128]) for i in range(2)]
        qS = [sb(f"qS{i}", [128, PAIRS, 128]) for i in range(2)]
        kZ = [sb(f"kZ{i}", [128, PAIRS, 2, 128]) for i in range(2)]
        Vs = [sb(f"Vs{i}", [128, NH * DK]) for i in range(2)]
        st6 = sb("st6", [128, 2, 6])
        mv = sb("mv", [128, 2, 2])
        rstd = sb("rstd", [128, 2])
        hS = [sb(f"hS{i}", [128, 128]) for i in range(2)]
        hTs = [sb(f"hTs{i}", [128, 128]) for i in range(2)]
        Pe = [sb(f"Pe{i}", [128, 4, 128]) for i in range(2)]
        PT = [sb(f"PT{i}", [128, 4, 128]) for i in range(2)]
        nmx = sb("nmx", [128, 2, 4])
        sums = sb("sums", [128, 4, 4])
        rs = sb("rs", [128, 4, 4])
        Os = sb("Os", [128, NH, DK])
        OTs = sb("OTs", [128, PAIRS, 128])

        s_ld = sem("s_ld"); s_ldx = sem("s_ldx"); s_ldb = sem("s_ldb"); s_ldw = sem("s_ldw")
        s_c = sem("s_c")
        s_a = sem("s_a")
        s_const = sem("s_const")
        s_row = sem("s_row"); s_lnw = sem("s_lnw")
        s_sub = sem("s_sub"); s_scl = sem("s_scl"); s_abs = sem("s_abs"); s_absb = sem("s_absb"); s_ln = sem("s_ln")
        s_red = sem("s_red"); s_redc = sem("s_redc"); s_sin = sem("s_sin")
        s_xb = sem("s_xb"); s_wb = sem("s_wb")
        s_S = sem("s_S"); s_mx = sem("s_mx"); s_exp = sem("s_exp"); s_P = sem("s_P")
        s_T = sem("s_T"); s_Te = sem("s_Te"); s_Of = sem("s_Of"); s_Oe = sem("s_Oe")
        s_qk = sem("s_qk"); s_qke = sem("s_qke"); s_ke = sem("s_ke"); s_G = sem("s_G"); s_Ge = sem("s_Ge")
        s_V = sem("s_V"); s_Ve = sem("s_Ve"); s_st = sem("s_st"); s_mv = sem("s_mv"); s_var = sem("s_var")
        s_rstd = sem("s_rstd"); s_h = sem("s_h"); s_ctx = [sem("s_ctx0"), sem("s_ctx1")]
        s_rs = sem("s_rs")
        s_gd = [sem("s_gd0"), sem("s_gd1")]
        s_x1 = sem("s_x1")
        s_out = sem("s_out")

        NEST, REL = Stage(sem, "nest", 2, 16, True), Stage(sem, "rel", 4, 8, False)
        Eflat = E[:].rearrange("p b c m -> p (b c m)")

        def unit(i, shape):
            v = Eflat[:, 2048 * i:2048 * i + shape[0] * shape[1]]
            return v.rearrange("p (a m) -> p a m", a=shape[0])

        for st in (NEST, REL):
            n = st.name
            heads = 4 * st.NS
            st.KZ = [unit(i, [heads, 128]) for i in range(2)]
            st.W = [sb(f"W{x}_{n}", [128, 128]) for x in "qkvo"]
            st.bq, st.bk = sb(f"bq_{n}", [128, 1]), sb(f"bk_{n}", [128, 1])
            st.bv, st.bo = sb(f"bv_{n}", [128, 128]), sb(f"bo_{n}", [128, 128])
            st.hm = sb(f"hm_{n}", [128, heads])
        BM = [unit(2 + i, [NH, 128]) for i in range(2)]
        bias1 = unit(4, [NH, 128])
        mneg = unit(5, [B, 128])
        mrow = unit(6, [B, 128])
        valid = sb("valid", [128, B])
        mv2 = sb("mv2", [128, 2, 2])
        st62 = sb("st62", [128, 2, 6])
        rstd2 = sb("rstd2", [128, 2])
        q2, k2, V2, h1 = ([valM[:, 2 * i + j, :] for j in range(2)] for i in range(4))
        O2, OT2, tmpx, tmpy = (valM[:, 8 + i, :] for i in range(4))
        gob = valM[:, 12, :]
        gwide = valM[:, 13, :]
        nw = sb("nw", [128, 128]); nb = sb("nb", [128, 128])
        wide = sb("wide", [128, 128])

        xg = nc.dram_tensor("slot_rows", (SLOTS, D), F32).ap()
        yg = nc.dram_tensor("slot_results", (SLOTS, D), F32).ap()
        zeroS = sb("zeroS", [128, 64])
        Hall = rowM
        We, Ve, Wout = G[0], G[1], kZ[0]

        def tile(i):
            return KR[:, i // 8, 128 * (i % 8):128 * (i % 8) + 128]

        def by_expert(i):
            return tile(i).rearrange("p (n e) -> p n e", e=NE)
        logits, top8, cnt, pos, base, one0, one1, picked = (by_expert(i) for i in range(8))
        idx8 = by_expert(8).bitcast(U32)
        small = tile(9)
        eid = small[:, 0:32].rearrange("p (k n) -> p k n", k=2)
        place = small[:, 32:64].rearrange("p (k n) -> p k n", k=2)
        full = small[:, 64:96].rearrange("p (k n) -> p k n", k=2)
        slot = small[:, 96:128].rearrange("p (k n) -> p k n", k=2)
        small2 = tile(10)
        weight = small2[:, 0:32].rearrange("p (k n) -> p k n", k=2)
        slot_u = small2[:, 32:64].rearrange("p (k n) -> p k n", k=2).bitcast(U32)
        gap = small2[:, 64:80]
        rstd_all = small2[:, 80:96]
        iota8 = small2[:, 96:104]
        rb = small2[:, 104:112]
        rwT = small2[:, 112:120]
        st_all = tile(11)[:, 0:96].rearrange("p (n s) -> p n s", s=6)
        mv_all = tile(11)[:, 96:128].rearrange("p (n s) -> p n s", s=2)
        ustrict, ones = valM[:, 14, :], valM[:, 15, :]
        Yg = Eflat[:, 0:4096].rearrange("p (k n d) -> p k n d", k=2, n=B)
        xTs = [Eflat[:, 4096 + 256 * i:4352 + 256 * i] for i in range(2)]
        sil = [Eflat[:, 5120 + 512 * i:5632 + 512 * i] for i in range(2)]
        hid = [Eflat[:, 6144 + 512 * i:6656 + 512 * i] for i in range(2)]
        Ys = [Eflat[:, 7168 + 256 * i:7424 + 256 * i] for i in range(2)]
        Xs = Eflat[:, 8192:10240].rearrange("p (t d) -> p t d", t=SLOTS // 128)
        m_w = sem("m_w"); m_st = sem("m_st"); m_mv = sem("m_mv"); m_rstd = sem("m_rstd"); m_h = sem("m_h")
        m_T = sem("m_T"); m_Te = sem("m_Te"); m_L = sem("m_L"); m_Le = sem("m_Le"); m_all = sem("m_all")
        m_cnt = sem("m_cnt"); m_pre = sem("m_pre"); m_gap = sem("m_gap"); m_exp = sem("m_exp")
        m_slot = sem("m_slot"); m_zero = sem("m_zero"); m_fill = sem("m_fill"); m_put = sem("m_put")
        m_xs = [sem(f"m_xs{i}") for i in range(NE)]
        m_xT = sem("m_xT"); m_xTe = sem("m_xTe"); m_ab = sem("m_ab"); m_sil = sem("m_sil"); m_hid = sem("m_hid")
        m_y = sem("m_y"); m_ye = sem("m_ye"); m_yd = [sem("m_yd0"), sem("m_yd1")]
        m_get = [sem(f"m_get{n}") for n in range(4)]
        m_x = sem("m_x"); m_clear = sem("m_clear")
        bAB = [(bS[0], bS[1]), (bT[0], bT[1])]
        bXT = [bA, bO]
        bY = [bG, bV]

        GD = 16 * 8

        block = ctx.enter_context(nc.Block())

        def vjob(b, i):
            return 2 + i if isinstance(b, int) and b < 0 else b * 5 + (6 + i)

        OJ = 7

        def pv_done(b, g):
            while g < 0:
                g += 4
                b = b - 1
            return (b * OJ + (5 + g) + 1) if g < 2 else ((b + 1) * OJ + (g - 2) + 1)


        def xrow(n):
            return X[:, bass.ds(n, 1), :].rearrange("p a d -> p (a d)")

        def small_pool(pool, st, before):
            def std(n, par, s_mv, s_var, s_rstd, mvt, r):
                pool.wait_ge(s_mv, n + 1)
                nc.gpsimd.tensor_tensor(r[:, par:par + 1], mvt[:, par, 1:2], epst[:], ALU.add).then_inc(s_var, 1)
                pool.wait_ge(s_var, n + 1)
                nc.gpsimd.tensor_tensor(r[:, par:par + 1], r[:, par:par + 1], mhalf[:], ALU.pow).then_inc(s_rstd, 1)

            def scale_norm(n, par):
                pool.wait_ge(st.s_xn, n + 1)
                nc.gpsimd.tensor_tensor(hS[par][:], hS[par][:], nw[:], ALU.mult).then_inc(st.s_xnw, 1)
                wait(pool, st.s_res, n * 2)
                nc.gpsimd.tensor_tensor(tmpx, h1[par], gates[:, 1:2].to_broadcast([128, 128]), ALU.mult).then_inc(st.s_xnw, 1)
                pool.wait_ge(st.s_xnw, n * 2 + 2)
                nc.gpsimd.tensor_tensor(hS[par][:], hS[par][:], nb[:], ALU.add).then_inc(st.s_h, 1)
                nc.gpsimd.tensor_tensor(tmpx, tmpx, gob, ALU.add).then_inc(st.s_res, 1)
                pool.wait_ge(st.s_res, n * 2 + 1)
                nc.gpsimd.tensor_tensor(xrow(n), xrow(n), tmpx, ALU.add).then_inc(st.s_res, 1)

            def keys(n, par):
                pool.wait_ge(st.s_qke, n + 1)
                wait(pool, st.s_S, (n - 1) * st.NS)
                heads = 4 * st.NS
                nc.gpsimd.tensor_tensor(st.KZ[par], k2[par].unsqueeze(1).to_broadcast([128, heads, 128]),
                                        st.hm[:].unsqueeze(2).to_broadcast([128, heads, 128]), ALU.mult).then_inc(st.s_kz, 1)

            def bias(n, par):
                wait(pool, st.s_add, (n - 1) * st.NS)
                nc.gpsimd.tensor_tensor(BM[par], bias1, mneg[:, bass.ds(n, 1), :].to_broadcast([128, NH, 128]),
                                        ALU.add).then_inc(st.s_bm, 1)

            pool.wait_ge(before, B)
            pool.wait_ge(st.s_cst, 1)
            std1 = (st.s_mv, st.s_var, st.s_rstd, mv, rstd)
            if st.nested:
                std2 = (st.s_mv2, st.s_var2, st.s_rstd2, mv2, rstd2)
                for n in range(3):
                    std(n, n % 2, *std1)
                    std(n, n % 2, *std2)
                    if n < 2:
                        scale_norm(n, n % 2)
            else:
                std(0, 0, *std1)
                std(1, 1, *std1)
                bias(0, 0)
            keys(0, 0)

            def body(b, par, known, it):
                if st.nested:
                    if known is None or known + 2 <= LAST:
                        scale_norm(b + 2, par)
                    if known is None or known + 3 <= LAST:
                        std(b + 3, 1 - par, *std1)
                        std(b + 3, 1 - par, *std2)
                elif known is None or known + 2 <= LAST:
                    std(b + 2, par, *std1)
                if known is None or known < LAST:
                    keys(b + 1, 1 - par)
                    if not st.nested:
                        bias(b + 1, 1 - par)
            over_batches(pool, body, 2 if st.nested else 1)

        def small_act(act, st, before):
            def evict_qk(n, par):
                act.wait_ge(st.s_qk, n + 1)
                scale = D ** -0.5 if st.nested else st.dh ** -0.5
                nc.scalar.activation(q2[par], bA[:, 0:128], ACT.Identity, bias=st.bq[:], scale=scale)
                if not isinstance(n, int) or n >= 2:
                    act.wait_ge(st.s_kz, n - 1)
                nc.scalar.activation(k2[par], bA[:, 128:256], ACT.Identity, bias=st.bk[:]).then_inc(st.s_qke, 1)

            act.wait_ge(before, B)
            act.wait_ge(st.s_cst, 1)
            evict_qk(0, 0)

            def body(b, par, known, it):
                for g in range(st.NS):
                    u = b * st.NS + g
                    act.wait_ge(st.s_mx, u + 1)
                    if st.nested:
                        wait(act, st.s_T, u - 1)
                    if known != 0 or g >= 1:
                        wait(act, st.s_rs, u)
                    for j in range(4):
                        src = bS[g % 2][:, 128 * j:128 * j + 128] if st.nested else Pe[g % 2][:, j, :]
                        last = nc.scalar.activation(Pe[g % 2][:, j, :], src, ACT.Exp, bias=nmx[:, g % 2, j:j + 1],
                                                    accum_out=sums[:, st.at(g, par), j:j + 1])
                    last.then_inc(st.s_exp, 1)
                    if g == 0 and (known is None or known < LAST):
                        evict_qk(b + 1, 1 - par)
            over_batches(act, body, 2 if st.nested else 1)

        def small_dve(dve, st, before, link):
            V_ = nc.vector
            NS, OJ = st.NS, st.OJ
            dve.wait_ge(before, B)
            dve.wait_ge(st.s_w, 16 * (12 if st.nested else 11))
            link(V_.tensor_scalar(st.bq[:], st.bq[:], D ** -0.5 if st.nested else st.dh ** -0.5, None, ALU.mult))
            if st.nested:
                link(V_.tensor_tensor(nw[:], nw[:], wide[:], ALU.mult))
                link(V_.tensor_tensor(nb[:], nb[:], wide[:], ALU.mult))
                link(V_.tensor_scalar(gwide, wide[:], gates[:, 1:2], None, ALU.mult))
                V_.tensor_tensor(gob, gwide, st.bo[:], ALU.mult).then_inc(st.s_cst, 1)
            else:
                link(V_.tensor_scalar(st.bo[:], st.bo[:], gates[:, 2:3], None, ALU.mult))
                link(V_.tensor_scalar(mneg, mrow.bitcast(I32), 0, NEG, ALU.is_equal, ALU.mult))
                link(V_.tensor_reduce(valid[:], mneg, AX.X, ALU.max))
                V_.tensor_scalar(valid[:], valid[:], 0.5 * NEG, None, ALU.is_gt).then_inc(st.s_cst, 1)

            def stats(n, par, src, six, out2, s_st, s_mv):
                V_.bn_stats(six[:, par, :], src).then_inc(s_st, 1)
                dve.wait_ge(s_st, n + 1)
                V_.memset(spare[:, par:par + 1], 0.0)
                V_.bn_aggr(out2[:, par, :], six[:, par, :]).then_inc(s_mv, 1)

            def stats1(n, par):
                stats(n, par, xrow(n), st6, mv, st.s_st, st.s_mv)

            def norm1(n, par, dst, s_done):
                dve.wait_ge(st.s_rstd, n + 1)
                V_.tensor_scalar(dst, xrow(n), mv[:, par, 0:1], rstd[:, par:par + 1], ALU.subtract,
                                 ALU.mult).then_inc(s_done, 1)

            def inner_stats(n, par):
                if not isinstance(n, int) or n >= 2:
                    dve.wait_ge(st.s_res, (n - 1) * 2)
                norm1(n, par, h1[par], st.s_h1)
                dve.wait_ge(st.s_h1, n + 1)
                stats(n, par, h1[par], st62, mv2, st.s_st2, st.s_mv2)

            def inner_norm(n, par):
                dve.wait_ge(st.s_rstd2, n + 1)
                if not isinstance(n, int) or n >= 2:
                    dve.wait_ge(st.s_V, st.vjob(n - 4, 1) + 1 if not isinstance(n, int) or n > 3 else n - 1)
                V_.tensor_scalar(hS[par][:], h1[par], mv2[:, par, 0:1], rstd2[:, par:par + 1], ALU.subtract,
                                 ALU.mult).then_inc(st.s_xn, 1)

            def evict_h(par, job):
                dve.wait_ge(st.s_V, job + 1)
                V_.tensor_copy(hTs[par][:], bV[:, 0:128]).then_inc(st.s_Ve, 1)

            def evict_v(par, job):
                dve.wait_ge(st.s_V, job + 1)
                V_.tensor_tensor(V2[par], bV[:, 0:128], st.bv[:], ALU.add).then_inc(st.s_Ve, 1)

            def evict_o(b, g, par):
                while g < 0:
                    g += NS
                    b = b - 1
                    par = 1 - par
                at = st.at(g, par)
                dve.wait_ge(st.s_Of, st.pv_done(b, g))
                dve.wait_ge(st.s_rs, b * NS + (g + 1))
                w = 4 * st.dh
                V_.tensor_tensor(O2[:, w * g:w * g + w].rearrange("p (j d) -> p j d", j=4),
                                 bO[:, 0:w].rearrange("p (j d) -> p j d", j=4),
                                 rs[:, at, :].unsqueeze(2).to_broadcast([128, 4, st.dh]), ALU.mult).then_inc(st.s_Oe, 1)

            def evict_ot(b):
                dve.wait_ge(st.s_Of, b * OJ + 3)
                V_.tensor_copy(OT2, bO[:, 0:128]).then_inc(st.s_Oe, 1)

            def evict_y(b):
                dve.wait_ge(st.s_Of, b * OJ + 4)
                if st.nested:
                    if not isinstance(b, int) or b >= 2:
                        dve.wait_ge(st.s_x, b - 1)
                    V_.tensor_tensor(tmpy, bO[:, 0:128], gwide, ALU.mult).then_inc(st.s_Oe, 1)
                    dve.wait_ge(st.s_res, b * 2)
                    dve.wait_ge(st.s_Oe, b * OJ + 4)
                    V_.tensor_tensor(xrow(b - 1), xrow(b - 1), tmpy, ALU.add).then_inc(st.s_x, 1)
                else:
                    V_.scalar_tensor_tensor(xrow(b - 1), bO[:, 0:128], gates[:, 2:3], xrow(b - 1), ALU.mult,
                                            ALU.add).then_inc(st.s_Oe, 1)
                    dve.wait_ge(st.s_Oe, b * OJ + 4)
                    V_.tensor_tensor(xrow(b - 1), xrow(b - 1), st.bo[:], ALU.add).then_inc(st.s_x, 1)

            def invert(b, g, par):
                while g < 0:
                    g += NS
                    b = b - 1
                    par = 1 - par
                at = st.at(g, par)
                dve.wait_ge(st.s_exp, b * NS + (g + 1))
                V_.reciprocal(rs[:, at, :], sums[:, at, :]).then_inc(st.s_rsr, 1)
                dve.wait_ge(st.s_rsr, b * NS + (g + 1))
                if st.nested:
                    reach = wide[:].rearrange("p (h d) -> p h d", d=st.dh)[:, 4 * g:4 * g + 4, 0]
                    V_.tensor_tensor(rs[:, at, :], rs[:, at, :], reach, ALU.mult).then_inc(st.s_rs, 1)
                else:
                    V_.tensor_tensor(rs[:, at, :], rs[:, at, :], valid[:, bass.ds(b, 1)].to_broadcast([128, 4]),
                                     ALU.mult).then_inc(st.s_rs, 1)

            def evict_t(b, g):
                while g < 0:
                    g += NS
                    b = b - 1
                u = b * NS + g
                dve.wait_ge(st.s_T, u + 1)
                wait(dve, st.s_Of, st.pv_done(b, g - 2))
                V_.tensor_copy(PT[g % 2][:].rearrange("p j q -> p (j q)"), bT[g % 2][:, :]).then_inc(st.s_Te, 1)

            V_.memset(tmpy, 1.0).then_inc(st.s_Oe, st.primed)
            dve.wait_ge(st.s_Oe, st.primed)
            if st.nested:
                for n in range(3):
                    stats1(n, n % 2)
                    inner_stats(n, n % 2)
                    if n < 2:
                        inner_norm(n, n % 2)
            else:
                for n in range(2):
                    stats1(n, n % 2)
                    norm1(n, n % 2, hS[n % 2][:], st.s_h)
            evict_h(0, 0)
            evict_h(1, 1)
            evict_v(0, 2)

            def body(b, par, known, it):
                first = known == 0
                for g in range(NS):
                    u = b * NS + g
                    dve.wait_ge(st.s_S, u + 1)
                    wait(dve, st.s_exp, u - 1)
                    if st.nested:
                        src = bS[g % 2][:, :].rearrange("p (j k) -> p j k", j=4)
                    else:
                        if g == 0:
                            dve.wait_ge(st.s_bm, b + 1)
                        wait(dve, st.s_T, u - 1)
                        src = Pe[g % 2][:]
                        V_.tensor_tensor(src, bS[g % 2][:, :].rearrange("p (j k) -> p j k", j=4),
                                         BM[par][:, 4 * g:4 * g + 4, :], ALU.add).then_inc(st.s_add, 1)
                        dve.wait_ge(st.s_add, u + 1)
                    V_.tensor_reduce(nmx[:, g % 2, :], src, AX.X, ALU.max, negate=True).then_inc(st.s_mx, 1)
                    if NS == 4 and not (first and g < 3):
                        evict_o(b, g - 3, par)
                    if NS == 2 and g == 1 and not first:
                        evict_o(b, -2, par)
                    if not (first and g == 0):
                        invert(b, g - 1, par)
                        evict_t(b, g - 1)
                    if NS == 4 and g == 2 and not first:
                        evict_ot(b)
                    if g == 0:
                        if st.nested:
                            if known is None or known + 2 <= LAST:
                                inner_norm(b + 2, par)
                            if known is None or known + 3 <= LAST:
                                stats1(b + 3, 1 - par)
                        elif known is None or known + 2 <= LAST:
                            stats1(b + 2, par)
                    if g == 1:
                        if st.nested:
                            if known is None or known + 3 <= LAST:
                                inner_stats(b + 3, 1 - par)
                        elif known is None or known + 2 <= LAST:
                            norm1(b + 2, par, hS[par][:], st.s_h)
                        if known is None or known < LAST:
                            evict_v(1 - par, st.vjob(b, 0))
                    if NS == 4 and g == 2 and not first:
                        evict_y(b)
                if NS == 2 and not first:
                    evict_o(b, -1, par)
                    evict_ot(b)
                    evict_y(b)
                if known is None or known + 2 <= LAST:
                    evict_h(par, st.vjob(b, 1))

            over_batches(dve, body, 2 if st.nested else 1)
            invert(B, -1, 0)
            evict_t(B, -1)
            if NS == 4:
                evict_o(B, -3, 0)
            evict_o(B, -2, 0)
            evict_o(B, -1, 0)
            evict_ot(B)
            evict_y(B)

        def small_pe(pe, st, before):
            NS, OJ = st.NS, st.OJ

            def mm(o, l, r, start=True, stop=True):
                return nc.tensor.matmul(o, l, r, start=start, stop=stop)

            def job_h(n, par, job):
                pe.wait_ge(st.s_h, n + 1)
                wait(pe, st.s_Ve, job)
                nc.tensor.transpose(bV[:, 0:128], hS[par][:], ident[:]).then_inc(st.s_V, 1)

            def source(par):
                return hTs[par] if st.nested else ctxS[par]

            def job_v(n, par, job):
                wait(pe, st.s_Ve, job)
                mm(bV[:, 0:128], source(par)[:], st.W[2][:]).then_inc(st.s_V, 1)

            def job_qk(n, par, hjob, half):
                pe.wait_ge(st.s_Ve, hjob + 1)
                if not st.nested:
                    pe.wait_ge(st.s_ctx[par], (half + 1) * 16)
                wait(pe, st.s_qke, n)
                mm(bA[:, 0:128], st.W[0][:], hTs[par][:])
                mm(bA[:, 128:256], st.W[1][:], source(par)[:]).then_inc(st.s_qk, 1)

            def job_s(b, g, par):
                u = b * NS + g
                if g == 0:
                    pe.wait_ge(st.s_kz, b + 1)
                wait(pe, st.s_exp, u - 1)
                if not st.nested:
                    wait(pe, st.s_add, u - 1)
                mm(bS[g % 2][:, :], q2[par], st.KZ[par][:, 4 * g:4 * g + 4, :].rearrange("p h k -> p (h k)")
                   ).then_inc(st.s_S, 1)

            def job_t(b, g):
                while g < 0:
                    g += NS
                    b = b - 1
                u = b * NS + g
                pe.wait_ge(st.s_exp, u + 1)
                wait(pe, st.s_Te, u - 1)
                for j in range(4):
                    last = nc.tensor.transpose(bT[g % 2][:, 128 * j:128 * j + 128], Pe[g % 2][:, j, :], ident[:])
                last.then_inc(st.s_T, 1)

            def job_pv(b, g, par):
                while g < 0:
                    g += NS
                    b = b - 1
                    par = 1 - par
                pe.wait_ge(st.s_Te, b * NS + (g + 1))
                pe.wait_ge(st.s_Oe, st.pv_done(b, g) - 1)
                if g == 0:
                    wait(pe, st.s_Ve, st.vjob(b - 1, 0) + 1)
                for j in range(4):
                    h = 4 * g + j
                    last = mm(bO[:, st.dh * j:st.dh * j + st.dh], PT[g % 2][:, j, :], V2[par][:, st.dh * h:st.dh * h + st.dh])
                last.then_inc(st.s_Of, 1)

            def job_ot(b):
                pe.wait_ge(st.s_Oe, b * OJ + 2)
                nc.tensor.transpose(bO[:, 0:128], O2, ident[:]).then_inc(st.s_Of, 1)

            def job_y(b):
                pe.wait_ge(st.s_Oe, b * OJ + 3)
                mm(bO[:, 0:128], OT2, st.W[3][:]).then_inc(st.s_Of, 1)

            pe.wait_ge(before, B)
            pe.wait_ge(st.s_Oe, st.primed)
            pe.wait_ge(st.s_cst, 1)
            nc.tensor.transpose(bO[:, 0:128], ident[:], ident[:]).then_inc(st.s_Of, st.primed)
            job_h(0, 0, 0)
            job_h(1, 1, 1)
            job_qk(0, 0, 0, 0)
            job_v(0, 0, 2)

            def body(b, par, known, it):
                first = known == 0
                more = known is None or known < LAST
                for g in range(NS):
                    job_s(b, g, par)
                    if NS == 4 and g == 2 and not first:
                        job_ot(b)
                    if not (first and g == 0):
                        job_t(b, g - 1)
                    if g == 0 and more:
                        job_qk(b + 1, 1 - par, 1 if first else st.vjob(b - 1, 1), it + par)
                    if NS == 4 and g == 2 and not first:
                        job_y(b)
                    if not (first and g < 2):
                        job_pv(b, g - 2, par)
                    if g == 1 and more:
                        job_v(b + 1, 1 - par, st.vjob(b, 0))
                if NS == 2 and not first:
                    job_ot(b)
                    job_y(b)
                if known is None or known + 2 <= LAST:
                    job_h(b + 2, par, st.vjob(b, 1))
            over_batches(pe, body, 2 if st.nested else 1)
            job_t(B, -1)
            job_pv(B, -2, 0)
            job_pv(B, -1, 0)
            job_ot(B)
            job_y(B)


        def experts_sp(sp):
            sp.wait_ge(m_zero, 1)
            sp.dma_start(xg.rearrange("(p a) (c d) -> p (a c) d", p=128, c=2),
                         zeroS[:].unsqueeze(1).to_broadcast([128, 2 * SLOTS // 128, 64])).then_inc(m_fill, 16)
            for e in range(NE):
                if e == 0:
                    sp.wait_ge(m_put, 2 * B * 16)
                sp.dma_start(Xs[:, 2 * e:2 * e + 2, :],
                             xg[CAP * e:CAP * e + CAP, :].rearrange("(t p) d -> p t d", p=128)).then_inc(m_xs[e], 16)
            for e in range(NE):
                sp.wait_ge(m_ye, e + 1)
                sp.dma_start(yg[CAP * e:CAP * e + CAP, :].rearrange("(t p) d -> p t d", p=128),
                             Ys[e % 2].rearrange("p (t d) -> p t d", t=2)).then_inc(m_yd[e % 2], 16)
            for q in range(4):
                sp.wait_ge(m_x, 4 * q + 4)
                sp.dma_start(out[4 * q:4 * q + 4].rearrange("b t d -> t b d"), X[:, 4 * q:4 * q + 4, :]).then_inc(s_out, 16)
            sp.wait_ge(s_out, 64)

        def experts_pool(pool):
            pool.wait_ge(m_mv, 1)
            nc.gpsimd.tensor_scalar(rstd_all, mv_all[:, :, 1], EPS, None, ALU.add).then_inc(m_all, 1)
            pool.wait_ge(m_all, 1)
            nc.gpsimd.tensor_tensor(rstd_all, rstd_all, mhalf[:].to_broadcast([128, B]), ALU.pow).then_inc(m_rstd, 1)
            pool.wait_ge(m_slot, 1)
            pool.wait_ge(m_fill, 16)
            for k in range(2):
                for n in range(B):
                    nc.gpsimd.indirect_dma_start(
                        out=xg, out_offset=bass.IndirectOffsetOnAxis(ap=slot_u[:, k, n:n + 1], axis=0),
                        in_=Hall[:, n, :], in_offset=None, bounds_check=SLOTS - 1, oob_is_err=False).then_inc(m_put, 16)
            pool.wait_ge(m_clear, 1)
            for i in range(2):
                pool.wait_ge(m_yd[i], 16 * NE // 2)
            for n in range(B):
                for k in range(2):
                    nc.gpsimd.indirect_dma_start(
                        out=Yg[:, k, n, :], out_offset=None, in_=yg,
                        in_offset=bass.IndirectOffsetOnAxis(ap=slot_u[:, k, n:n + 1], axis=0),
                        bounds_check=SLOTS - 1, oob_is_err=False).then_inc(m_get[n // 4], 16)

        def experts_act(act):
            act.wait_ge(REL.s_x, B)
            act.wait_ge(m_gap, 1)
            nc.scalar.activation(gap, gap, ACT.Exp).then_inc(m_exp, 1)
            for e in range(NE):
                act.wait_ge(m_ab, e + 1)
                wait(act, m_hid, e - 1)
                nc.scalar.activation(sil[e % 2], bAB[e % 2][1][:, :], ACT.Silu).then_inc(m_sil, 1)
                if e >= 1:
                    evict_result(act, e - 1)
            evict_result(act, NE - 1)

        def evict_result(act, e):
            act.wait_ge(m_y, e + 1)
            wait(act, m_yd[e % 2], 16 * (e // 2))
            nc.scalar.copy(Ys[e % 2], bY[e % 2][:, 0:256]).then_inc(m_ye, 1)

        def experts_dve(dve, link):
            V_ = nc.vector
            dve.wait_ge(REL.s_x, B)
            V_.memset(zeroS[:], 0.0).then_inc(m_zero, 1)
            for n in range(B):
                last = V_.bn_stats(st_all[:, n, :], X[:, n, :])
            last.then_inc(m_st, 1)
            dve.wait_ge(m_st, 1)
            for n in range(B):
                last = V_.bn_aggr(mv_all[:, n, :], st_all[:, n, :])
            last.then_inc(m_mv, 1)
            V_.memset(Yg, 0.0).then_inc(m_clear, 1)
            V_.memset(ones, 1.0)
            dve.wait_ge(m_w, 16 * 7)
            dve.wait_ge(m_rstd, 1)
            for n in range(B + 2):
                if n < B:
                    V_.tensor_scalar(Hall[:, n, :], X[:, n, :], mv_all[:, n, 0:1], rstd_all[:, n:n + 1], ALU.subtract,
                                     ALU.mult).then_inc(m_h, 1)
                if 1 <= n <= B:
                    dve.wait_ge(m_T, n)
                    V_.tensor_copy(hTs[(n - 1) % 2][:], bXT[(n - 1) % 2][:, 0:128]).then_inc(m_Te, 1)
                if n >= 2:
                    dve.wait_ge(m_L, n - 1)
                    V_.tensor_tensor(logits[:, n - 2, :], bY[n % 2][:, 0:NE], rb, ALU.add).then_inc(m_Le, 1)
            dve.wait_ge(m_Le, B)
            for n in range(B):
                last = V_.max(top8[:, n, :], logits[:, n, :])
            link(last)
            for n in range(B):
                last = V_.max_index(idx8[:, n, :], top8[:, n, :], logits[:, n, :])
            V_.tensor_tensor(gap, top8[:, :, 1], top8[:, :, 0], ALU.subtract).then_inc(m_gap, 1)
            link(last)
            link(V_.tensor_copy(eid, idx8[:, :, 0:2].rearrange("p n k -> p k n")))
            for k, one in enumerate((one0, one1)):
                link(V_.tensor_tensor(one, eid[:, k, :].unsqueeze(2).to_broadcast([128, B, NE]),
                                      iota8.unsqueeze(1).to_broadcast([128, B, NE]), ALU.is_equal))
            V_.tensor_tensor(cnt, one0, one1, ALU.add).then_inc(m_cnt, 1)
            V_.memset(base[:, 0, :], 0.0)
            dve.wait_ge(m_exp, 1)
            link(V_.tensor_scalar(weight[:, 0, :], gap, 1.0, None, ALU.add))
            link(V_.reciprocal(weight[:, 0, :], weight[:, 0, :]))
            link(V_.tensor_scalar(weight[:, 0, :], weight[:, 0, :], gates[:, 3:4], None, ALU.mult))
            link(V_.tensor_tensor(weight[:, 1, :], weight[:, 0, :], gap, ALU.mult))
            dve.wait_ge(m_pre, 2)
            for n in range(1, B):
                link(V_.tensor_tensor(base[:, n, :], bS[1][:, NE * (n - 1):NE * n], base[:, n - 1, :], ALU.add))
            link(V_.tensor_tensor(pos, bS[0][:, 0:128].rearrange("p (n e) -> p n e", e=NE), base, ALU.add))
            for k, one in enumerate((one0, one1)):
                link(V_.tensor_tensor(picked, one, pos, ALU.mult))
                link(V_.tensor_reduce(place[:, k, :], picked, AX.X, ALU.add))
            link(V_.tensor_scalar(full, place, float(CAP), None, ALU.is_ge))
            link(V_.scalar_tensor_tensor(slot, eid, float(CAP), place, ALU.mult, ALU.add))
            link(V_.scalar_tensor_tensor(slot, full, float(16 * SLOTS), slot, ALU.mult, ALU.add))
            V_.tensor_copy(slot_u, slot).then_inc(m_slot, 1)
            link(V_.tensor_scalar(full, full, -1.0, 1.0, ALU.mult, ALU.add))
            link(V_.tensor_tensor(weight, weight, full, ALU.mult))
            for e in range(NE + 1):
                if e < NE:
                    dve.wait_ge(m_xT, e + 1)
                    V_.tensor_copy(xTs[e % 2], bXT[e % 2][:, 0:256]).then_inc(m_xTe, 1)
                if e >= 1:
                    dve.wait_ge(m_sil, e)
                    wait(dve, m_y, e - 2)
                    V_.tensor_tensor(hid[(e - 1) % 2], bAB[(e - 1) % 2][0][:, :], sil[(e - 1) % 2],
                                     ALU.mult).then_inc(m_hid, 1)
            for n in range(B):
                dve.wait_ge(m_get[n // 4], 4 * 32)
                link(V_.scalar_tensor_tensor(X[:, n, :], Yg[:, 0, n, :], weight[:, 0, n:n + 1], X[:, n, :], ALU.mult, ALU.add))
                V_.scalar_tensor_tensor(X[:, n, :], Yg[:, 1, n, :], weight[:, 1, n:n + 1], X[:, n, :], ALU.mult,
                                        ALU.add).then_inc(m_x, 1)

        def experts_pe(pe):
            def mm(o, l, r, start=True, stop=True):
                return nc.tensor.matmul(o, l, r, start=start, stop=stop)
            pe.wait_ge(REL.s_x, B)
            pe.wait_ge(m_w, 16 * 7)
            for n in range(B + 1):
                if n < B:
                    pe.wait_ge(m_h, n + 1)
                    wait(pe, m_Te, n - 1)
                    nc.tensor.transpose(bXT[n % 2][:, 0:128], Hall[:, n, :], ident[:]).then_inc(m_T, 1)
                if n >= 1:
                    pe.wait_ge(m_Te, n)
                    wait(pe, m_Le, n - 2)
                    mm(bY[(n - 1) % 2][:, 0:NE], hTs[(n - 1) % 2][:], rwT).then_inc(m_L, 1)
            pe.wait_ge(m_cnt, 1)
            both = cnt.rearrange("p n e -> p (n e)")
            mm(bS[0][:, 0:128], ustrict, both).then_inc(m_pre, 1)
            mm(bS[1][:, 0:128], ones, both).then_inc(m_pre, 1)
            pe.wait_ge(m_slot, 1)

            def result(e):
                pe.wait_ge(m_hid, e + 1)
                wait(pe, m_ye, e - 1)
                for t in range(2):
                    for c in range(2):
                        last = mm(bY[e % 2][:, 128 * t:128 * t + 128], hid[e % 2][:, 256 * c + 128 * t:256 * c + 128 * t + 128],
                                  Wout[:, e, c, :], start=c == 0, stop=c == 1)
                last.then_inc(m_y, 1)

            for e in range(NE):
                pe.wait_ge(m_xs[e], 16)
                wait(pe, m_xTe, e - 1)
                for t in range(2):
                    last = nc.tensor.transpose(bXT[e % 2][:, 128 * t:128 * t + 128], Xs[:, 2 * e + t, :], ident[:])
                last.then_inc(m_xT, 1)
                pe.wait_ge(m_xTe, e + 1)
                wait(pe, m_hid, e - 1)
                for bank, w in zip(bAB[e % 2], (We, Ve)):
                    for c in range(2):
                        last = mm(bank[:, 256 * c:256 * c + 256], w[:, 2 * e + c, :], xTs[e % 2])
                last.then_inc(m_ab, 1)
                if e >= 1:
                    result(e - 1)
            result(NE - 1)

        @block.sync
        def _(sp):
            sp.dma_start(ident[:], A["ident"]).then_inc(s_ld, 16)
            sp.dma_start(graw[:], A["gates"].partition_broadcast(128)).then_inc(s_ld, 16)
            sp.dma_start(pn[:], A["box_pn"]).then_inc(s_ldb, 16)
            sp.dma_start(valM[:], A["box_row"][0]).then_inc(s_ldb, 16)
            sp.dma_start(rowM[:], A["box_row"][1]).then_inc(s_ldb, 16)
            sp.dma_start(phase[:], A["phase"]).then_inc(s_ldb, 16)
            sp.dma_start(X[:], A["x"].rearrange("b t d -> t b d")).then_inc(s_ldx, 16)
            for dst, name in ((wrep, "wg"), (delta, "delta"), (bgp, "bg"), (WqT, "WqT"), (WkT, "WkT"), (WvT, "WvT"),
                              (WoT, "WoT"), (bq, "bq"), (bk, "bk")):
                sp.dma_start(dst[:], A[name]).then_inc(s_ldw, 16)
            sp.dma_start(bvb[:], A["bv"].partition_broadcast(128)).then_inc(s_ldw, 16)
            sp.dma_start(bob[:], A["bo"].partition_broadcast(128)).then_inc(s_ldw, 16)

            for st in (NEST, REL):
                n = st.name
                for dst, name in zip(st.W + [st.bq, st.bk, st.hm], ("Wq", "Wk", "Wv", "Wo", "bq", "bk", "hm")):
                    sp.dma_start(dst[:], A[f"{name}_{n}"]).then_inc(st.s_w, 16)
                for dst, name in ((st.bv, "bv"), (st.bo, "bo")):
                    sp.dma_start(dst[:], A[f"{name}_{n}"].partition_broadcast(128)).then_inc(st.s_w, 16)
            sp.dma_start(nw[:], A["norm_w"].partition_broadcast(128)).then_inc(NEST.s_w, 16)
            sp.dma_start(nb[:], A["norm_b"].partition_broadcast(128)).then_inc(NEST.s_w, 16)
            sp.dma_start(wide[:], A["wide"]).then_inc(NEST.s_w, 16)

            def load_ctx(n, par, known):
                if known is None or known >= 2:
                    wait(sp, s_V, vjob(n - 3, 3) + 1)
                sp.dma_start(ctxS[par][:], A["ctxT"][:, bass.ds(n, 1) if not isinstance(n, int) else slice(n, n + 1), :]
                             .rearrange("d a t -> d (a t)")).then_inc(s_ctx[par], 16)

            def spread(b1, par, known):
                for hg in range(2):
                    wait(sp, s_Ge, b1 * 4 + (2 * hg + 2))
                    wait(sp, s_P, (b1 - 1) * 4)
                    for h in range(8):
                        sp.dma_start(G[par][:, 8 * hg + h, :],
                                     Gc[hg][NPF * h:NPF * h + NPF, :, :].rearrange("n c m -> n (c m)")).then_inc(s_gd[hg], 16)

            load_ctx(0, 0, 0)
            load_ctx(1, 1, 1)

            def body(b, par, known, it):
                spread(b, par, known)
                if known is None or known + 2 <= LAST:
                    load_ctx(b + 2, par, None if known is None else known + 2)
            over_batches(sp, body)

            sp.wait_ge(s_x1, B)
            sp.wait_ge(s_G, 4 * B)
            sp.dma_start(bias1, A["rel_bias"]).then_inc(REL.s_w, 16)
            sp.dma_start(mrow.bitcast(I32), A["mask"].partition_broadcast(128)).then_inc(REL.s_w, 16)

            if stop >= 4:
                for dst, name in ((We, "W_e"), (Ve, "V_e"), (Wout, "W_out"), (rwT, "rwT"), (ustrict, "ustrict")):
                    sp.dma_start(dst[:] if dst in (We, Ve, Wout) else dst, A[name]).then_inc(m_w, 16)
                for dst, name in ((rb, "rb"), (iota8, "iota8")):
                    sp.dma_start(dst, A[name].partition_broadcast(128)).then_inc(m_w, 16)

            def rel_ctx(n, par, known):
                if known is None or known >= 2:
                    wait(sp, REL.s_V, REL.vjob(n - 3, 0) + 1)
                else:
                    sp.wait_ge(s_x1, B)
                sp.dma_start(ctxS[par][:], A["ctxT"][:, bass.ds(n, 1) if not isinstance(n, int) else slice(n, n + 1), :]
                             .rearrange("d a t -> d (a t)")).then_inc(REL.s_ctx[par], 16)
            if stop >= 3:
                rel_ctx(0, 0, 0)
                rel_ctx(1, 1, 1)

                def body(b, par, known, it):
                    if known is None or known + 2 <= LAST:
                        rel_ctx(b + 2, par, None if known is None else known + 2)
                over_batches(sp, body)

            if stop < 4:
                sp.wait_ge([None, s_x1, NEST.s_x, REL.s_x][stop], B)
                sp.dma_start(out.rearrange("b t d -> t b d"), X[:]).then_inc(s_out, 16)
                sp.wait_ge(s_out, 16)
            else:
                experts_sp(sp)

        @block.gpsimd
        def _(pool):
            pool.wait_ge(s_ldb, 64)
            with pool.Fori(0, B) as b:
                pool.wait_ge(s_sub, b + 1)
                Eb = E[:, bass.ds(b, 1), :, :].rearrange("p a c m -> p (a c) m")
                nc.gpsimd.tensor_tensor(Eb, Eb, scl[:, bass.ds(b, 1), :].rearrange("p a c -> p (a c)").unsqueeze(2)
                                        .to_broadcast([128, NC, S]), ALU.mult).then_inc(s_scl, 1)

            def prep(n, par):
                pool.wait_ge(s_mv, n + 1)
                nc.gpsimd.tensor_tensor(rstd[:, par:par + 1], mv[:, par, 1:2], epst[:], ALU.add).then_inc(s_var, 1)
                pool.wait_ge(s_var, n + 1)
                nc.gpsimd.tensor_tensor(rstd[:, par:par + 1], rstd[:, par:par + 1], mhalf[:], ALU.pow).then_inc(s_rstd, 1)
            prep(0, 0)
            prep(1, 1)

            def body(b, par, known, it):
                if known is None or known + 2 <= LAST:
                    prep(b + 2, par)
            over_batches(pool, body)

            if stop >= 2:
                small_pool(pool, NEST, s_x1)
            if stop >= 3:
                small_pool(pool, REL, NEST.s_x)
            if stop >= 4:
                experts_pool(pool)

        @block.scalar
        def _(act):
            act.wait_ge(s_ld, 32)
            nc.scalar.activation(gates[:], graw[:], ACT.Tanh).then_inc(s_xb, 1)
            act.wait_ge(s_row, 1)
            nc.scalar.activation(valM[64:128], valM[64:128], ACT.Ln)
            nc.scalar.activation(valN[64:128], valN[64:128], ACT.Ln).then_inc(s_lnw, 1)
            with act.Fori(0, B) as b:
                act.wait_ge(s_abs, b + 1)
                Eb = E[0:64, bass.ds(b, 1), :, :]
                nc.scalar.activation(Eb, Eb, ACT.Ln).then_inc(s_ln, 1)
            with act.Fori(0, B) as b:
                act.wait_ge(s_red, b + 1)
                Eb = E[:, bass.ds(b, 1), :, :]
                nc.scalar.activation(Eb, Eb, ACT.Sin, bias=phase[:, 1:2]).then_inc(s_sin, 1)

            def evict_qk(b1, par, g):
                act.wait_ge(s_qk, b1 * 4 + (g + 1))
                for i in range(2):
                    t = 2 * g + i
                    last = nc.scalar.activation(qS[par][:, t, :], bA[:, 128 * i:128 * i + 128], ACT.Identity,
                                                bias=bq[:, t:t + 1], scale=DK ** -0.5)
                last.then_inc(s_qke, 1)

            def evict_g(b1, g):
                hg, half = g // 2, g % 2
                act.wait_ge(s_G, b1 * 4 + (g + 1))
                if not isinstance(b1, int) or b1 > 0:
                    wait(act, s_gd[hg], b1 * GD)
                nc.scalar.activation(Gc[hg][:, 4 * half:4 * half + 4, :].rearrange("p c m -> p (c m)"), bG[:, :],
                                     ACT.Identity, bias=bgp[:, hg:hg + 1]).then_inc(s_Ge, 1)

            act.wait_ge(s_wb, 1)
            for g in range(4):
                evict_g(0, g)
                evict_qk(0, 0, g)

            def body(b, par, known, it):
                for g in range(4):
                    u = b * 4 + g
                    act.wait_ge(s_mx, u + 1)
                    wait(act, s_T, u - 1)
                    for j in range(4):
                        last = nc.scalar.activation(Pe[g % 2][:, j, :], bS[g % 2][:, 128 * j:128 * j + 128], ACT.Exp,
                                                    bias=nmx[:, g % 2, j:j + 1])
                    last.then_inc(s_exp, 1)
                    if known != 0 or g > 0:
                        act.wait_ge(s_T, u)
                        wait(act, s_Of, pv_done(b, g - 3))
                        nc.scalar.copy(PT[(g - 1) % 2][:].rearrange("p j q -> p (j q)"),
                                       bT[(g - 1) % 2][:, :]).then_inc(s_Te, 1)
                    if known is None or known < LAST:
                        evict_g(b + 1, g)
                        evict_qk(b + 1, 1 - par, g)
            over_batches(act, body)
            act.wait_ge(s_T, 4 * B)
            nc.scalar.copy(PT[1][:].rearrange("p j q -> p (j q)"), bT[1][:, :]).then_inc(s_Te, 1)

            if stop >= 2:
                small_act(act, NEST, s_x1)
            if stop >= 3:
                small_act(act, REL, NEST.s_x)
            if stop >= 4:
                experts_act(act)

        @block.vector
        def _(dve):
            chain = [0]

            def link(ins):
                chain[0] += 1
                ins.then_inc(s_c, 1)
                dve.wait_ge(s_c, chain[0])

            V_ = nc.vector
            V_.memset(mhalf[:], -0.5)
            V_.memset(epst[:], EPS)
            for par in range(2):
                V_.memset(kZ[par][0:64, :, 1, :], 0.0)
                V_.memset(kZ[par][64:128, :, 0, :], 0.0)
            dve.wait_ge(s_ldb, 64)
            link(V_.tensor_tensor(scl[:], pn[:, 1], pn[:, 0], ALU.subtract))
            link(V_.tensor_scalar(scl[:], scl[:], 1.0, None, ALU.add))
            link(V_.tensor_copy(valN[64:128], scl[64:128]))
            link(V_.tensor_tensor(valN[0:64], pn[0:64, 0], pn[0:64, 1], ALU.add))
            link(V_.tensor_scalar(valN[0:64], valN[0:64], 0.5, None, ALU.mult))
            link(V_.reciprocal(scl[0:64], scl[0:64]))
            link(V_.memset(scl[64:128], -1.0))
            link(V_.tensor_tensor(valM[64:128], rowM[64:128], valM[64:128], ALU.subtract))
            link(V_.tensor_scalar(valM[64:128], valM[64:128], 1.0, None, ALU.add))
            link(V_.tensor_tensor(valM[0:64], rowM[0:64], valM[0:64], ALU.add))
            V_.tensor_scalar(valM[0:64], valM[0:64], 0.5, None, ALU.mult).then_inc(s_row, 1)
            dve.wait_ge(s_row, 1)
            dve.wait_ge(s_lnw, 1)
            with dve.Fori(0, B) as b:
                Eb = E[:, bass.ds(b, 1), :, :].rearrange("p a c m -> p (a c) m")
                V_.tensor_tensor(Eb, valM[:, bass.ds(b, 1), :].to_broadcast([128, NC, S]),
                                 valN[:, bass.ds(b, 1), :].rearrange("p a c -> p (a c)").unsqueeze(2)
                                 .to_broadcast([128, NC, S]), ALU.subtract).then_inc(s_sub, 1)
            with dve.Fori(0, B) as b:
                dve.wait_ge(s_scl, b + 1)
                Eb = E[0:64, bass.ds(b, 1), :, :].rearrange("p a c m -> p (a c m)")
                Eu = Eb.bitcast(U32)
                V_.tensor_scalar(Eu, Eu, 0x7FFFFFFF, None, ALU.bitwise_and).then_inc(s_absb, 1)
                dve.wait_ge(s_absb, b + 1)
                V_.tensor_scalar(Eb, Eb, 1e-3, None, ALU.max).then_inc(s_abs, 1)
            with dve.Fori(0, B) as b:
                dve.wait_ge(s_ln, b + 1)
                Eb = E[:, bass.ds(b, 1), :, :].rearrange("p a c m -> p (a c m)")
                Kb = KR[:, 0, :]
                V_.tensor_scalar(Kb, Eb, 100.0 / TWO_PI, phase[:, 0:1], ALU.mult, ALU.add).then_inc(s_redc, 1)
                dve.wait_ge(s_redc, b * 5 + 1)
                V_.tensor_scalar(Kb, Kb, ROUND, -ROUND, ALU.add, ALU.add).then_inc(s_redc, 1)
                V_.tensor_scalar(Eb, Eb, 100.0, None, ALU.mult).then_inc(s_redc, 1)
                dve.wait_ge(s_redc, b * 5 + 3)
                V_.scalar_tensor_tensor(Eb, Kb, -PI_HI, Eb, ALU.mult, ALU.add).then_inc(s_redc, 1)
                dve.wait_ge(s_redc, b * 5 + 4)
                V_.scalar_tensor_tensor(Eb, Kb, -PI_LO, Eb, ALU.mult, ALU.add).then_inc(s_redc, 1)
                dve.wait_ge(s_redc, b * 5 + 5)
                V_.tensor_scalar(Eb, Eb, phase[:, 2:3], phase[:, 3:4], ALU.max, ALU.min).then_inc(s_red, 1)

            dve.wait_ge(s_ldw, 16 * 11)
            for hg in range(2):
                last = V_.tensor_tensor(Wblk[:, hg], wrep[:, 8 * hg:8 * hg + 8].unsqueeze(2).to_broadcast([128, 8, NPF]),
                                        delta[:].unsqueeze(1).to_broadcast([128, 8, NPF]), ALU.mult)
            link(last)
            link(V_.tensor_scalar(bq[:], bq[:], DK ** -0.5, None, ALU.mult))
            dve.wait_ge(s_xb, 1)
            link(V_.tensor_scalar(bob[:], bob[:], gates[:, 0:1], None, ALU.mult))
            dve.wait_ge(s_ldx, 16)
            V_.memset(sums[:], 0.0).then_inc(s_wb, 1)

            def prep(n, par):
                xb = X[:, bass.ds(n, 1), :].rearrange("p a d -> p (a d)")
                V_.bn_stats(st6[:, par, :], xb).then_inc(s_st, 1)
                dve.wait_ge(s_st, n + 1)
                V_.memset(spare[:, par:par + 1], 0.0)
                V_.bn_aggr(mv[:, par, :], st6[:, par, :]).then_inc(s_mv, 1)

            def norm(n, par):
                xb = X[:, bass.ds(n, 1), :].rearrange("p a d -> p (a d)")
                dve.wait_ge(s_rstd, n + 1)
                wait(dve, s_mv, n + 1)
                V_.tensor_scalar(hS[par][:], xb, mv[:, par, 0:1], rstd[:, par:par + 1], ALU.subtract,
                                 ALU.mult).then_inc(s_h, 1)

            def evict_h(par, job):
                dve.wait_ge(s_V, job + 1)
                V_.tensor_copy(hTs[par][:], bV[:, 0:128]).then_inc(s_Ve, 1)

            def evict_v(par, g, job):
                dve.wait_ge(s_V, job + 1)
                V_.tensor_tensor(Vs[par][:, 256 * g:256 * g + 256], bV[:, 0:256], bvb[:, 256 * g:256 * g + 256],
                                 ALU.add).then_inc(s_Ve, 1)

            def evict_k(b1, par, g):
                dve.wait_ge(s_qke, b1 * 4 + (g + 1))
                for r in range(2):
                    rows = slice(64 * r, 64 * r + 64)
                    last = V_.tensor_tensor(kZ[par][rows, 2 * g:2 * g + 2, r, :],
                                            bA[rows, 256:512].rearrange("p (i k) -> p i k", i=2),
                                            bk[rows, 2 * g:2 * g + 2].unsqueeze(2).to_broadcast([64, 2, 128]), ALU.add)
                last.then_inc(s_ke, 1)

            def evict_o(b, g):
                while g < 0:
                    g += 4
                    b = b - 1
                dve.wait_ge(s_Of, pv_done(b, g))
                dve.wait_ge(s_rs, b * 4 + (g + 1))
                V_.tensor_tensor(Os[:, 4 * g:4 * g + 4, :], bO[:, 0:256].rearrange("p (j d) -> p j d", j=4),
                                 rs[:, g, :].unsqueeze(2).to_broadcast([128, 4, DK]), ALU.mult).then_inc(s_Oe, 1)

            def evict_ot(b, half):
                dve.wait_ge(s_Of, b * OJ + (3 + half))
                V_.tensor_copy(OTs[:, 4 * half:4 * half + 4, :].rearrange("p t q -> p (t q)"), bO[:, :]).then_inc(s_Oe, 1)

            def evict_y(b):
                dve.wait_ge(s_Of, b * OJ + 5)
                xb = X[:, bass.ds(b - 1, 1), :].rearrange("p a d -> p (a d)")
                V_.scalar_tensor_tensor(xb, bO[:, 0:128], gates[:, 0:1], xb, ALU.mult, ALU.add).then_inc(s_Oe, 1)
                dve.wait_ge(s_Oe, b * OJ + 5)
                V_.tensor_tensor(xb, xb, bob[:], ALU.add).then_inc(s_x1, 1)

            V_.memset(rs[:], 1.0).then_inc(s_Oe, 5)
            prep(0, 0)
            prep(1, 1)
            norm(0, 0)
            norm(1, 1)
            evict_h(0, 0)
            evict_h(1, 1)
            for g in range(4):
                evict_k(0, 0, g)
                evict_v(0, g, vjob(-1, g))

            def body(b, par, known, it):
                for g in range(4):
                    u = b * 4 + g
                    first = known == 0
                    more = known is None or known < LAST
                    dve.wait_ge(s_S, u + 1)
                    wait(dve, s_exp, u - 1)
                    V_.tensor_reduce(nmx[:, g % 2, :], bS[g % 2][:, :].rearrange("p (j k) -> p j k", j=4), AX.X,
                                     ALU.max, negate=True).then_inc(s_mx, 1)
                    if not (first and g == 0):
                        dve.wait_ge(s_P, u)
                        V_.reciprocal(rs[:, (g - 1) % 4, :], sums[:, (g - 1) % 4, :]).then_inc(s_rs, 1)
                    if not (first and g < 3):
                        evict_o(b, g - 3)
                    if g == 2 and not first:
                        evict_ot(b, 0)
                    if g == 0 and (known is None or known + 2 <= LAST):
                        prep(b + 2, par)
                    if g == 1 and (known is None or known + 2 <= LAST):
                        norm(b + 2, par)
                    if g == 2 and not first:
                        evict_ot(b, 1)
                    dve.wait_ge(s_exp, u + 1)
                    if g % 2 == 0:
                        dve.wait_ge(s_gd[g // 2], (b + 1) * GD)
                    for j in range(4):
                        last = V_.scalar_tensor_tensor(Pe[g % 2][:, j, :], G[par][:, 4 * g + j, :], GMIN,
                                                       Pe[g % 2][:, j, :], ALU.max, ALU.mult,
                                                       accum_out=sums[:, g, j:j + 1])
                    last.then_inc(s_P, 1)
                    if g == 2 and not first:
                        evict_y(b)
                    if more:
                        evict_k(b + 1, 1 - par, g)
                        evict_v(1 - par, g, vjob(b, g))
                if known is None or known + 2 <= LAST:
                    evict_h(par, vjob(b, 4))
            over_batches(dve, body)
            dve.wait_ge(s_P, 4 * B)
            V_.reciprocal(rs[:, 3, :], sums[:, 3, :]).then_inc(s_rs, 1)
            evict_o(B, -3)
            evict_o(B, -2)
            evict_o(B, -1)
            evict_ot(B, 0)
            evict_ot(B, 1)
            evict_y(B)

            if stop >= 2:
                small_dve(dve, NEST, s_x1, link)
            if stop >= 3:
                small_dve(dve, REL, NEST.s_x, link)
            if stop >= 4:
                experts_dve(dve, link)

        @block.tensor
        def _(pe):
            M = nc.tensor.matmul

            def mm(o, l, r, start=True, stop=True):
                return M(o, l, r, start=start, stop=stop)

            def job_h(n, par, job):
                pe.wait_ge(s_h, n + 1)
                wait(pe, s_Ve, job)
                nc.tensor.transpose(bV[:, 0:128], hS[par][:], ident[:]).then_inc(s_V, 1)

            def job_v(n, par, g, job, half):
                if g == 0:
                    pe.wait_ge(s_ctx[par], (half + 1) * 16)
                wait(pe, s_Ve, job)
                mm(bV[:, 0:256], ctxS[par][:], WvT[:, 256 * g:256 * g + 256]).then_inc(s_V, 1)

            def job_qk(n, par, g, hjob, half):
                if g == 0:
                    pe.wait_ge(s_Ve, hjob + 1)
                    pe.wait_ge(s_ctx[par], (half + 1) * 16)
                wait(pe, s_ke, n * 4 + g)
                for i in range(2):
                    t = 2 * g + i
                    mm(bA[:, 128 * i:128 * i + 128], WqT[:, 128 * t:128 * t + 128], hTs[par][:])
                for i in range(2):
                    t = 2 * g + i
                    last = mm(bA[:, 256 + 128 * i:384 + 128 * i], WkT[:, 128 * t:128 * t + 128], ctxS[par][:])
                last.then_inc(s_qk, 1)

            def job_g(n, g):
                if g == 0:
                    pe.wait_ge(s_sin, n + 1)
                wait(pe, s_Ge, n * 4 + g)
                hg, half = g // 2, g % 2
                mm(bG[:, :], Wblk[:, hg].rearrange("p h n -> p (h n)"),
                   E[:, bass.ds(n, 1), 4 * half:4 * half + 4, :].rearrange("p a c m -> p (a c m)")).then_inc(s_G, 1)

            def job_t(b, g):
                while g < 0:
                    g += 4
                    b = b - 1
                u = b * 4 + g
                pe.wait_ge(s_P, u + 1)
                wait(pe, s_Te, u - 1)
                for j in range(4):
                    last = nc.tensor.transpose(bT[g % 2][:, 128 * j:128 * j + 128], Pe[g % 2][:, j, :], ident[:])
                last.then_inc(s_T, 1)

            def job_pv(b, g, par):
                while g < 0:
                    g += 4
                    b = b - 1
                    par = 1 - par
                pe.wait_ge(s_Te, b * 4 + (g + 1))
                pe.wait_ge(s_Oe, pv_done(b, g) - 1)
                if g == 0:
                    wait(pe, s_Ve, vjob(b - 1, 3) + 1)
                for j in range(4):
                    h = 4 * g + j
                    last = mm(bO[:, 64 * j:64 * j + 64], PT[g % 2][:, j, :], Vs[par][:, 64 * h:64 * h + 64])
                last.then_inc(s_Of, 1)

            def job_ot(b, half):
                pe.wait_ge(s_Oe, b * OJ + (2 + half))
                for i in range(4):
                    t = 4 * half + i
                    last = nc.tensor.transpose(bO[:, 128 * i:128 * i + 128],
                                               Os[:, 2 * t:2 * t + 2, :].rearrange("p h d -> p (h d)"), ident[:])
                last.then_inc(s_Of, 1)

            def job_y(b):
                pe.wait_ge(s_Oe, b * OJ + 4)
                for t in range(PAIRS):
                    last = mm(bO[:, 0:128], OTs[:, t, :], WoT[:, t, :], start=t == 0, stop=t == PAIRS - 1)
                last.then_inc(s_Of, 1)

            def job_s(b, g, par):
                u = b * 4 + g
                pe.wait_ge(s_ke, u + 1)
                wait(pe, s_exp, u - 1)
                for i in range(2):
                    t = 2 * g + i
                    last = mm(bS[g % 2][:, 256 * i:256 * i + 256], qS[par][:, t, :],
                              kZ[par][:, t, :, :].rearrange("p r k -> p (r k)"))
                last.then_inc(s_S, 1)

            pe.wait_ge(s_ld, 32)
            pe.wait_ge(s_wb, 1)
            pe.wait_ge(s_Oe, 5)
            job_h(0, 0, 0)
            job_h(1, 1, 1)
            for g in range(4):
                job_g(0, g)
                job_qk(0, 0, g, 0, 0)
                job_v(0, 0, g, vjob(-1, g), 0)

            def body(b, par, known, it):
                first = known == 0
                more = known is None or known < LAST
                for g in range(4):
                    job_s(b, g, par)
                    if g == 2 and not first:
                        job_ot(b, 0)
                    if more:
                        job_g(b + 1, g)
                    if g == 2 and not first:
                        job_ot(b, 1)
                    if not (first and g == 0):
                        job_t(b, g - 1)
                    if more:
                        job_qk(b + 1, 1 - par, g, 1 if first else vjob(b - 1, 4), it + par)
                    if g == 2 and not first:
                        job_y(b)
                    if more:
                        job_v(b + 1, 1 - par, g, vjob(b, g), it + par)
                    if not (first and g < 2):
                        job_pv(b, g - 2, par)
                if known is None or known + 2 <= LAST:
                    job_h(b + 2, par, vjob(b, 4))
            nc.tensor.transpose(bO[:, 0:128], ident[:], ident[:]).then_inc(s_Of, 5)
            over_batches(pe, body)
            job_t(B, -1)
            job_pv(B, -2, 0)
            job_pv(B, -1, 0)
            job_ot(B, 0)
            job_ot(B, 1)
            job_y(B)
            if stop >= 2:
                small_pe(pe, NEST, s_x1)
            if stop >= 3:
                small_pe(pe, REL, NEST.s_x)
            if stop >= 4:
                experts_pe(pe)


NAMES = ["x", "ctxT", "ident", "gates", "box_pn", "box_row", "phase", "wg", "delta", "bg", "WqT", "WkT", "WvT",
         "WoT", "bq", "bk", "bv", "bo", "rel_bias", "mask", "norm_w", "norm_b", "wide"]
NAMES += ["W_e", "V_e", "W_out", "rwT", "ustrict", "rb", "iota8"]
NAMES += [f"{x}_{n}" for n in ("nest", "rel") for x in ("Wq", "Wk", "Wv", "Wo", "bq", "bk", "hm", "bv", "bo")]


def layouts(I):
    a = {k: np.asarray(v) for k, v in I.items()}
    f32 = np.float32
    L = {}
    L["x"] = a["x"]
    L["ctxT"] = a["ctx_1024"].transpose(2, 0, 1)
    L["ident"] = np.eye(128, dtype=f32)
    L["gates"] = np.array([a["g_xattn"][0], a["g_ffn"][0], a["g_xattn"][1], a["g_ffn"][1]], f32)
    box = a["fside_BxSx4_0"]
    axis = [0, 1, 0, 1, 0, 1, 0, 1]
    lo, hi = box[:, :, axis], box[:, :, [2 + i for i in axis]]
    both = np.stack([lo, hi])
    L["box_pn"] = both.reshape(2, B, NPF, NC, NF).transpose(4, 2, 0, 1, 3).reshape(128, 2, B, NC)
    L["box_row"] = np.repeat(both.transpose(0, 3, 1, 2), NPF, axis=1)
    order = [0, 1, 4, 5, 2, 3, 6, 7]
    L["wg"] = np.repeat(a["L0_xattn_Wg"][:, order].T, NPF, axis=0)
    L["delta"] = np.tile(np.eye(NPF, dtype=f32), (NF, 1))
    cos = np.repeat(np.array([0, 0, 1, 1, 0, 0, 1, 1], f32), NPF)
    bias = (cos * f32(math.pi / 2)).astype(f32)
    L["phase"] = np.stack([cos * f32(0.25), bias, -f32(PI_SAFE) - bias, f32(PI_SAFE) - bias], 1).astype(f32)
    L["bg"] = np.repeat(a["L0_xattn_bg"].reshape(2, 8).T, NPF, axis=0)
    for n in "qkv":
        L[f"W{n}T"] = a[f"L0_xattn_W{n}"].T
    L["WoT"] = a["L0_xattn_Wo"].T.reshape(PAIRS, 128, 128).transpose(1, 0, 2)
    L["bq"] = a["L0_xattn_bq"].reshape(PAIRS, 128).T
    L["bk"] = a["L0_xattn_bk"].reshape(PAIRS, 128).T
    L["bv"] = a["L0_xattn_bv"]
    L["bo"] = a["L0_xattn_bo"]
    for n, w, src in (("nest", 16, "L0_ffn_{}_{}"), ("rel", 8, "L1_xattn_{}{}")):
        for x in "qkvo":
            name, bname = (src.format(x, "w"), src.format(x, "b")) if n == "nest" else (src.format("W", x), src.format("b", x))
            L[f"W{x}_{n}"] = a[name].T
            L[f"b{x}_{n}"] = a[bname].reshape(128, 1) if x in "qk" else a[bname]
        L[f"hm_{n}"] = np.repeat(np.eye(128 // w, dtype=f32), w, axis=0)
    L["norm_w"], L["norm_b"] = a["L0_ffn_norm_w"], a["L0_ffn_norm_b"]
    experts = a["L0_ffn_router_prob"].shape[2]
    reach = D // 2 ** (np.arange(S) // (S // experts))
    L["wide"] = (np.arange(D)[None, :] < reach[:, None]).astype(f32)
    L["mask"] = a["mask_Bx1x1xS2_ik0"].reshape(B, S)
    rel = a["L1_xattn_rel_emb"]
    most = (rel.shape[0] - 1) // 2
    at = np.clip(np.arange(S)[None, :] - np.arange(S)[:, None], -most, most) + most
    L["rel_bias"] = rel[at].transpose(0, 2, 1)
    L["W_e"] = a["L1_ffn_W"].transpose(1, 0, 2).reshape(D, 2 * NE, 128)
    L["V_e"] = a["L1_ffn_V"].transpose(1, 0, 2).reshape(D, 2 * NE, 128)
    L["W_out"] = a["L1_ffn_W_out"].reshape(NE, 2, 128, D).transpose(2, 0, 1, 3)
    L["rwT"] = a["L1_ffn_router_w"].T
    L["rb"] = a["L1_ffn_router_b"]
    L["iota8"] = np.arange(NE, dtype=f32)
    L["ustrict"] = np.triu(np.ones((128, 128), f32), 1)
    return {k: np.ascontiguousarray(v) for k, v in L.items()}


def kernel(**inputs):
    import concourse.bacc as bacc
    from concourse.bass_utils import run_bass_kernel_spmd

    L = layouts(inputs)
    nc = bacc.Bacc("TRN2", target_bir_lowering=False, num_devices=1)
    A = {n: nc.dram_tensor(n + "_dram", L[n].shape, mybir.dt.from_np(L[n].dtype), kind="ExternalInput").ap()
         for n in NAMES}
    out = nc.dram_tensor("out_dram", (B, S, D), F32, kind="ExternalOutput").ap()
    build_program(nc, A, out)
    r = run_bass_kernel_spmd(nc, [{n + "_dram": L[n] for n in NAMES}], core_ids=[0])
    return r.results[0]["out_dram"]
```

```python
import math
from contextlib import ExitStack

import numpy as np
import concourse.bass as bass
from concourse import mybir

F32 = mybir.dt.float32
I32 = mybir.dt.int32
U32 = mybir.dt.uint32
ALU = mybir.AluOpType
ACT = mybir.ActivationFunctionType
AX = mybir.AxisListType

B, S, D = 16, 128, 128
NH, DK = 16, 64
PAIRS = NH * DK // 128
NF, NPF = 8, 16
NC = S // NPF
EPS = 1e-5
GMIN = 1e-6
NEG = -1e30
TWO_PI = 2.0 * math.pi
PI_HI = 6.28125
PI_LO = TWO_PI - PI_HI
ROUND = 1.5 * 2.0 ** 23
PI_SAFE = 3.1415925
NE, HID, CAP = 8, 256, 256
SLOTS = NE * CAP
ROW = D + 4
LAST = B - 1


def wait(eng, sem, value):
    if isinstance(value, int) and value <= 0:
        return
    eng.wait_ge(sem, value)


def over_batches(eng, body, tail=1):
    body(0, 0, 0, 0)
    body(1, 1, 1, 0)
    with eng.Fori(1, B // 2 - tail) as it:
        body(it * 2, 0, None, it)
        body(it * 2 + 1, 1, None, it)
    for b in range(B - 2 * tail, B):
        body(b, b % 2, b, b // 2)


class Stage:

    def __init__(self, sem, name, slots, width, nested):
        self.name = name
        self.NS = slots
        self.dh = width
        self.nested = nested
        self.s_S = sem(f"s_S_{name}")
        self.s_mx = sem(f"s_mx_{name}")
        self.s_exp = sem(f"s_exp_{name}")
        self.s_T = sem(f"s_T_{name}")
        self.s_Te = sem(f"s_Te_{name}")
        self.s_Of = sem(f"s_Of_{name}")
        self.s_Oe = sem(f"s_Oe_{name}")
        self.s_ot = sem(f"s_ot_{name}")
        self.s_ote = sem(f"s_ote_{name}")
        self.s_y = sem(f"s_y_{name}")
        self.s_ye = sem(f"s_ye_{name}")
        self.s_qk = sem(f"s_qk_{name}")
        self.s_qke = sem(f"s_qke_{name}")
        self.s_kz = sem(f"s_kz_{name}")
        self.s_add = sem(f"s_add_{name}")
        self.s_V = sem(f"s_V_{name}")
        self.s_Ve = sem(f"s_Ve_{name}")
        self.s_st = sem(f"s_st_{name}")
        self.s_mv = sem(f"s_mv_{name}")
        self.s_var = sem(f"s_var_{name}")
        self.s_rstd = sem(f"s_rstd_{name}")
        self.s_h = sem(f"s_h_{name}")
        self.s_rs = sem(f"s_rs_{name}")
        self.s_rsr = sem(f"s_rsr_{name}")
        self.s_x = sem(f"s_x_{name}")
        self.s_w = sem(f"s_w_{name}")
        self.s_cst = sem(f"s_cst_{name}")
        if nested:
            self.s_h1 = sem(f"s_h1_{name}")
            self.s_st2 = sem(f"s_st2_{name}")
            self.s_mv2 = sem(f"s_mv2_{name}")
            self.s_var2 = sem(f"s_var2_{name}")
            self.s_rstd2 = sem(f"s_rstd2_{name}")
            self.s_tx = sem(f"s_tx_{name}")
            self.s_hb = sem(f"s_hb_{name}")
            self.s_res = sem(f"s_res_{name}")
        else:
            self.s_bm = sem(f"s_bm_{name}")
            self.s_ctx = [sem(f"s_ctx{i}_{name}") for i in range(2)]

    def at(self, g, par):
        return g if self.NS == 4 else 2 * par + g

    def job_of_v(self, n):
        if isinstance(n, int) and n == 0:
            return 2
        if isinstance(n, int) and n == LAST:
            return LAST * 2 + 1
        return n * 2 + (2 if self.nested else 1)

    def job_of_h(self, n):
        return n if isinstance(n, int) and n < 2 else n * 2 + (-1 if self.nested else 0)


def build_program(nc, A, out, stop=99):
    ctx = ExitStack()
    with ctx:
        def sb(name, shape, dt=F32):
            return ctx.enter_context(nc.sbuf_tensor(name, shape, dt))

        def sem(name):
            return ctx.enter_context(nc.semaphore(name))

        banks = {n: ctx.enter_context(nc.psum_tensor(n, [128, 512], F32))
                 for n in ("S0", "S1", "T0", "T1", "A0", "D0", "D1", "O0")}
        bS = [banks["S0"], banks["S1"]]
        bT = [banks["T0"], banks["T1"]]
        bP, bY1 = bT
        bA, bG, bV, bO = banks["A0"], banks["D0"], banks["D1"], banks["O0"]
        bP2 = [bP, bG]

        X = sb("X", [128, B, D])
        ident = sb("ident", [128, 128])
        gates = sb("gates", [128, 4])
        graw = sb("graw", [128, 4])
        mhalf = sb("mhalf", [128, 1])
        epst = sb("epst", [128, 1])
        spare = sb("spare", [128, 2])
        E = sb("E", [128, B, NC, S])
        KR = sb("KR", [128, 2, NC * S])
        Wblk = sb("Wblk", [128, 2, 8, NPF])
        wrep = sb("wrep", [128, NH])
        delta = sb("delta", [128, NPF])
        bgp = sb("bgp", [128, 2])
        phase = sb("phase", [128, 4])
        valM = sb("valM", [128, B, S])
        rowM = sb("rowM", [128, B, S])
        pn = sb("pn", [128, 2, B, NC])
        valN = sb("valN", [128, B, NC])
        scl = sb("scl", [128, B, NC])
        G = [sb(f"G{i}", [128, NH, S]) for i in range(2)]
        Gc = [sb(f"Gc{i}", [128, NC, S]) for i in range(2)]
        WqT = sb("WqT", [128, NH * DK])
        WkT = sb("WkT", [128, NH * DK])
        WvT = sb("WvT", [128, NH * DK])
        WoT = sb("WoT", [128, PAIRS, 128])
        bq = sb("bq", [128, PAIRS])
        bk = sb("bk", [128, PAIRS])
        bvb = sb("bvb", [128, NH * DK])
        bob = sb("bob", [128, 128])
        ctxS = [sb(f"ctxS{i}", [128, 128]) for i in range(2)]
        qS = [sb(f"qS{i}", [128, PAIRS, 128]) for i in range(2)]
        kZ = [sb(f"kZ{i}", [128, PAIRS, 2, 128]) for i in range(2)]
        Vs = [sb(f"Vs{i}", [128, NH * DK]) for i in range(2)]
        st6 = sb("st6", [128, 2, 6])
        mv = sb("mv", [128, 2, 2])
        rstd = sb("rstd", [128, 2])
        hS = [sb(f"hS{i}", [128, 128]) for i in range(2)]
        hTs = [sb(f"hTs{i}", [128, 128]) for i in range(2)]
        Pe = [sb(f"Pe{i}", [128, 4, 128]) for i in range(2)]
        PT = [sb(f"PT{i}", [128, 4, 128]) for i in range(2)]
        nmx = sb("nmx", [128, 2, 4])
        sums = sb("sums", [128, 4, 4])
        rs = sb("rs", [128, 4, 4])
        Os = sb("Os", [128, NH, DK])
        OTs = sb("OTs", [128, PAIRS, 128])

        s_ld = sem("s_ld"); s_ldx = sem("s_ldx"); s_ldb = sem("s_ldb"); s_ldw = sem("s_ldw")
        s_c = sem("s_c")
        s_a = sem("s_a")
        s_const = sem("s_const")
        s_row = sem("s_row"); s_lnw = sem("s_lnw")
        s_sub = sem("s_sub"); s_scl = sem("s_scl"); s_abs = sem("s_abs"); s_absb = sem("s_absb"); s_ln = sem("s_ln")
        s_red = sem("s_red"); s_redc = sem("s_redc"); s_sin = sem("s_sin")
        s_xb = sem("s_xb"); s_wb = sem("s_wb")
        s_S = sem("s_S"); s_mx = sem("s_mx"); s_exp = sem("s_exp"); s_P = sem("s_P")
        s_T = sem("s_T"); s_Te = sem("s_Te"); s_Of = sem("s_Of"); s_Oe = sem("s_Oe"); s_ot = sem("s_ot"); s_ote = sem("s_ote"); s_y = sem("s_y"); s_ye = sem("s_ye")
        s_qk = sem("s_qk"); s_qke = sem("s_qke"); s_ke = sem("s_ke"); s_G = sem("s_G"); s_Ge = sem("s_Ge")
        s_V = sem("s_V"); s_Ve = sem("s_Ve"); s_st = sem("s_st"); s_mv = sem("s_mv"); s_var = sem("s_var")
        s_rstd = sem("s_rstd"); s_h = sem("s_h"); s_ctx = [sem("s_ctx0"), sem("s_ctx1")]
        s_rs = sem("s_rs")
        s_gd = [sem("s_gd0"), sem("s_gd1")]
        s_x1 = sem("s_x1")
        s_out = sem("s_out")

        NEST, REL = Stage(sem, "nest", 2, 16, True), Stage(sem, "rel", 4, 8, False)
        Eflat = E[:].rearrange("p b c m -> p (b c m)")

        def unit(i, shape):
            v = Eflat[:, 2048 * i:2048 * i + shape[0] * shape[1]]
            return v.rearrange("p (a m) -> p a m", a=shape[0])

        for st in (NEST, REL):
            n = st.name
            heads = 4 * st.NS
            st.KZ = [unit(i, [heads, 128]) for i in range(2)]
            st.W = [sb(f"W{x}_{n}", [128, 128]) for x in "qkvo"]
            st.bq, st.bk = sb(f"bq_{n}", [128, 1]), sb(f"bk_{n}", [128, 1])
            st.bv, st.bo = sb(f"bv_{n}", [128, 128]), sb(f"bo_{n}", [128, 128])
            st.hm = sb(f"hm_{n}", [128, heads])
        BM = [unit(2 + i, [NH, 128]) for i in range(2)]
        bias1 = unit(4, [NH, 128])
        mneg = unit(5, [B, 128])
        mrow = unit(6, [B, 128])
        valid = sb("valid", [128, B])
        P4 = [kZ[1][:, 2 * i:2 * i + 2, :, :].rearrange("p a b k -> p (a b) k") for i in range(4)]
        mv2 = sb("mv2", [128, 2, 2])
        st62 = sb("st62", [128, 2, 6])
        rstd2 = sb("rstd2", [128, 2])
        q2, k2, V2, h1 = ([valM[:, 2 * i + j, :] for j in range(2)] for i in range(4))
        O2, OT2, tmpx, tmpy = (valM[:, 8 + i, :] for i in range(4))
        gob = valM[:, 12, :]
        gwide = valM[:, 13, :]
        nwT = sb("nwT", [128, 128]); nbT = sb("nbT", [128, 128])
        nwb = sb("nwb", [128, 2])
        wideT = sb("wideT", [128, 128])
        wide = sb("wide", [128, 128])

        xg = nc.dram_tensor("slot_rows", (SLOTS, ROW), F32).ap()
        blank = sb("blank", [128, ROW])
        Rows = Eflat[:, 6 * 2048:6 * 2048 + B * ROW].rearrange("p (n r) -> p n r", n=B)
        We, Ve, Wout = G[0], G[1], kZ[0]

        def tile(i):
            return KR[:, i // 8, 128 * (i % 8):128 * (i % 8) + 128]

        def by_expert(i):
            return tile(i).rearrange("p (n e) -> p n e", e=NE)
        logits, top8, cnt, pos, base, one0, one1, picked = (by_expert(i) for i in range(8))
        idx8 = by_expert(8).bitcast(U32)
        small = tile(9)
        eid = small[:, 0:32].rearrange("p (k n) -> p k n", k=2)
        place = small[:, 32:64].rearrange("p (k n) -> p k n", k=2)
        full = small[:, 64:96].rearrange("p (k n) -> p k n", k=2)
        slot = small[:, 96:128].rearrange("p (k n) -> p k n", k=2)
        small2 = tile(10)
        w_slot = small2[:, 0:16]
        first = small2[:, 16:32]
        slot_u = small2[:, 32:64].rearrange("p (k n) -> p k n", k=2).bitcast(U32)
        gap = small2[:, 64:80]
        rstd_all = small2[:, 80:96]
        gap1 = tile(12)[:, 32:48]
        iota8 = small2[:, 96:104]
        rb = small2[:, 104:112]
        rwT = small2[:, 112:120]
        token = tile(12)[:, 0:B]
        owner = tile(12)[:, B:2 * B]
        st_all = tile(11)[:, 0:96].rearrange("p (n s) -> p n s", s=6)
        mv_all = tile(11)[:, 96:128].rearrange("p (n s) -> p n s", s=2)
        ustrict, ones = valM[:, 14, :], valM[:, 15, :]
        xTs = [Eflat[:, 4096 + 256 * i:4352 + 256 * i] for i in range(2)]
        sil = [Eflat[:, 5120 + 512 * i:5632 + 512 * i] for i in range(2)]
        hid = [Eflat[:, 6144 + 512 * i:6656 + 512 * i] for i in range(2)]
        Ys = [Eflat[:, 7168 + 256 * i:7424 + 256 * i] for i in range(2)]
        Xs = Eflat[:, 8192:8192 + B * ROW].rearrange("p (t r) -> p t r", t=SLOTS // 128)
        m_w = sem("m_w"); m_st = sem("m_st"); m_mv = sem("m_mv"); m_rstd = sem("m_rstd"); m_h = sem("m_h")
        m_T = sem("m_T"); m_Te = sem("m_Te"); m_L = sem("m_L"); m_Le = sem("m_Le"); m_all = sem("m_all")
        m_cnt = sem("m_cnt"); m_pre = sem("m_pre"); m_gap = sem("m_gap"); m_exp = sem("m_exp")
        m_slot = sem("m_slot"); m_fill = sem("m_fill"); m_put = sem("m_put")
        m_xs = [sem(f"m_xs{i}") for i in range(NE)]
        m_xT = sem("m_xT"); m_xTe = sem("m_xTe"); m_ab = sem("m_ab"); m_sil = sem("m_sil"); m_hid = sem("m_hid")
        m_y = sem("m_y"); m_ye = sem("m_ye"); m_add = sem("m_add"); m_ws = sem("m_ws")
        bAB = [(bS[0], bS[1]), (bT[0], bT[1])]
        bXT = [bA, bO]
        bY = [bG, bV]

        GD = 16 * 8

        block = ctx.enter_context(nc.Block())

        def vjob(b, i):
            return 2 + i if isinstance(b, int) and b < 0 else b * 5 + (6 + i)

        def xrow(n):
            return X[:, bass.ds(n, 1), :].rearrange("p a d -> p (a d)")

        def after(st, b, g, par, it):
            return (b, g + 1, par, it) if g < st.NS - 1 else (b + 1, 0, 1 - par, it + par)

        def small_pool(pool, st, before):
            def std(n, par, s_mv, s_var, s_rstd, mvt, r):
                pool.wait_ge(s_mv, n + 1)
                nc.gpsimd.tensor_tensor(r[:, par:par + 1], mvt[:, par, 1:2], epst[:], ALU.add).then_inc(s_var, 1)
                pool.wait_ge(s_var, n + 1)
                nc.gpsimd.tensor_tensor(r[:, par:par + 1], r[:, par:par + 1], mhalf[:], ALU.pow).then_inc(s_rstd, 1)

            def residual(n, par):
                pool.wait_ge(st.s_tx, n + 1)
                nc.gpsimd.tensor_tensor(tmpx, tmpx, gob, ALU.add).then_inc(st.s_res, 1)
                pool.wait_ge(st.s_res, n * 2 + 1)
                nc.gpsimd.tensor_tensor(xrow(n), xrow(n), tmpx, ALU.add).then_inc(st.s_res, 1)

            def norm_bias(n, par):
                pool.wait_ge(st.s_Ve, st.job_of_h(n) + 1)
                nc.gpsimd.tensor_tensor(hTs[par][:], hTs[par][:], nbT[:], ALU.add).then_inc(st.s_hb, 1)

            def keys(n, par):
                pool.wait_ge(st.s_qke, n + 1)
                wait(pool, st.s_S, (n - 1) * st.NS)
                heads = 4 * st.NS
                nc.gpsimd.tensor_tensor(st.KZ[par], k2[par].unsqueeze(1).to_broadcast([128, heads, 128]),
                                        st.hm[:].unsqueeze(2).to_broadcast([128, heads, 128]), ALU.mult).then_inc(st.s_kz, 1)

            def bias(n, par):
                wait(pool, st.s_S, (n - 1) * st.NS)
                nc.gpsimd.tensor_tensor(BM[par], bias1, mneg[:, bass.ds(n, 1), :].to_broadcast([128, NH, 128]),
                                        ALU.add).then_inc(st.s_bm, 1)

            pool.wait_ge(before, B)
            pool.wait_ge(st.s_cst, 1)
            std1 = (st.s_mv, st.s_var, st.s_rstd, mv, rstd)
            if st.nested:
                std2 = (st.s_mv2, st.s_var2, st.s_rstd2, mv2, rstd2)
                for n in range(3):
                    std(n, n % 2, *std1)
                    std(n, n % 2, *std2)
                    residual(n, n % 2)
                    if n < 2:
                        norm_bias(n, n)
                std(3, 1, *std1)
                std(3, 1, *std2)
                keys(0, 0)
            else:
                for n in range(3):
                    std(n, n % 2, *std1)
                bias(0, 0)
                keys(0, 0)

            def body(b, par, known, it):
                one, two, three, four = (known is None or known + n <= LAST for n in (1, 2, 3, 4))
                if st.nested:
                    if one:
                        keys(b + 1, 1 - par)
                    if three:
                        residual(b + 3, 1 - par)
                    if four:
                        std(b + 4, par, *std1)
                    if two:
                        norm_bias(b + 2, par)
                    if four:
                        std(b + 4, par, *std2)
                else:
                    if one:
                        keys(b + 1, 1 - par)
                        bias(b + 1, 1 - par)
                    if three:
                        std(b + 3, 1 - par, *std1)
            over_batches(pool, body, 2)

        def small_act(act, st, before):
            def evict_qk(n, par):
                act.wait_ge(st.s_qk, n + 1)
                scale = D ** -0.5 if st.nested else st.dh ** -0.5
                nc.scalar.activation(q2[par], bA[:, 0:128], ACT.Identity, bias=st.bq[:], scale=scale)
                if not isinstance(n, int) or n >= 2:
                    act.wait_ge(st.s_kz, n - 1)
                nc.scalar.activation(k2[par], bA[:, 128:256], ACT.Identity, bias=st.bk[:]).then_inc(st.s_qke, 1)

            act.wait_ge(before, B)
            act.wait_ge(st.s_cst, 1)
            def evict_t(b, g):
                while g < 0:
                    g += st.NS
                    b = b - 1
                u = b * st.NS + g
                act.wait_ge(st.s_T, u + 1)
                wait(act, st.s_Of, u - 1)
                nc.scalar.copy(PT[g % 2][:].rearrange("p j q -> p (j q)"), bP2[g % 2][:, :]).then_inc(st.s_Te, 1)

            def gated(n, par):
                act.wait_ge(st.s_h1, n + 1)
                wait(act, st.s_res, n * 2)
                nc.scalar.activation(tmpx, h1[par], ACT.Identity, scale=gates[:, 1:2]).then_inc(st.s_tx, 1)

            if st.nested:
                for n in range(3):
                    gated(n, n % 2)
            evict_qk(0, 0)
            if st.nested:
                evict_qk(1, 1)

            def body(b, par, known, it):
                for g in range(st.NS):
                    u = b * st.NS + g
                    at = st.at(g, par)
                    act.wait_ge(st.s_mx, u + 1)
                    if st.nested:
                        wait(act, st.s_T, u - 3)
                    wait(act, st.s_rs, u - 3)
                    for j in range(4):
                        src = bS[g % 2][:, 128 * j:128 * j + 128] if st.nested else P4[at][:, j, :]
                        last = nc.scalar.activation(P4[at][:, j, :], src, ACT.Exp, bias=nmx[:, g % 2, j:j + 1],
                                                    accum_out=sums[:, st.at(g, par), j:j + 1])
                    last.then_inc(st.s_exp, 1)
                    if not (known == 0 and g == 0):
                        evict_t(b, g - 1)
                    if not st.nested and g == 0 and (known is None or known < LAST):
                        evict_qk(b + 1, 1 - par)
                    if st.nested and g == 0 and (known is None or known + 3 <= LAST):
                        gated(b + 3, 1 - par)
                    if st.nested and g == 1 and (known is None or known + 2 <= LAST):
                        evict_qk(b + 2, par)
            over_batches(act, body, 2)
            evict_t(B, -1)

        def small_dve(dve, st, before, link):
            V_ = nc.vector
            NS = st.NS
            dve.wait_ge(before, B)
            dve.wait_ge(st.s_w, 16 * (12 if st.nested else 11))
            link(V_.tensor_scalar(st.bq[:], st.bq[:], D ** -0.5 if st.nested else st.dh ** -0.5, None, ALU.mult))
            if st.nested:
                link(V_.tensor_scalar(nwT[:], wideT[:], nwb[:, 0:1], None, ALU.mult))
                link(V_.tensor_scalar(nbT[:], wideT[:], nwb[:, 1:2], None, ALU.mult))
                link(V_.tensor_scalar(gwide, wide[:], gates[:, 1:2], None, ALU.mult))
                V_.tensor_tensor(gob, gwide, st.bo[:], ALU.mult).then_inc(st.s_cst, 1)
            else:
                link(V_.tensor_scalar(st.bo[:], st.bo[:], gates[:, 2:3], None, ALU.mult))
                link(V_.tensor_scalar(mneg, mrow.bitcast(I32), 0, NEG, ALU.is_equal, ALU.mult))
                link(V_.tensor_reduce(valid[:], mneg, AX.X, ALU.max))
                V_.tensor_scalar(valid[:], valid[:], 0.5 * NEG, None, ALU.is_gt).then_inc(st.s_cst, 1)

            def stats(n, par, src, six, out2, s_st, s_mv):
                V_.bn_stats(six[:, par, :], src).then_inc(s_st, 1)
                dve.wait_ge(s_st, n + 1)
                V_.memset(spare[:, par:par + 1], 0.0)
                V_.bn_aggr(out2[:, par, :], six[:, par, :]).then_inc(s_mv, 1)

            def stats1(n, par):
                stats(n, par, xrow(n), st6, mv, st.s_st, st.s_mv)

            def norm1(n, par, dst, s_done):
                dve.wait_ge(st.s_rstd, n + 1)
                V_.tensor_scalar(dst, xrow(n), mv[:, par, 0:1], rstd[:, par:par + 1], ALU.subtract,
                                 ALU.mult).then_inc(s_done, 1)

            def inner_stats(n, par):
                if not isinstance(n, int) or n >= 2:
                    dve.wait_ge(st.s_tx, n - 1)
                norm1(n, par, h1[par], st.s_h1)
                dve.wait_ge(st.s_h1, n + 1)
                stats(n, par, h1[par], st62, mv2, st.s_st2, st.s_mv2)

            def inner_norm(n, par):
                dve.wait_ge(st.s_rstd2, n + 1)
                if not isinstance(n, int) or n >= 2:
                    dve.wait_ge(st.s_V, st.job_of_h(n - 2) + 1)
                V_.tensor_scalar(hS[par][:], h1[par], mv2[:, par, 0:1], rstd2[:, par:par + 1], ALU.subtract,
                                 ALU.mult).then_inc(st.s_h, 1)

            def evict_h(n, par, job):
                dve.wait_ge(st.s_V, job + 1)
                if not st.nested:
                    V_.tensor_copy(hTs[par][:], bV[:, 0:128]).then_inc(st.s_Ve, 1)
                    return
                V_.tensor_tensor(hTs[par][:], bV[:, 0:128], nwT[:], ALU.mult).then_inc(st.s_Ve, 1)

            def evict_v(par, job):
                dve.wait_ge(st.s_V, job + 1)
                V_.tensor_tensor(V2[par], bV[:, 0:128], st.bv[:], ALU.add).then_inc(st.s_Ve, 1)

            def evict_o(b, g, par):
                while g < 0:
                    g += NS
                    b = b - 1
                    par = 1 - par
                at = st.at(g, par)
                dve.wait_ge(st.s_Of, b * NS + (g + 1))
                dve.wait_ge(st.s_rs, b * NS + (g + 1))
                w = 4 * st.dh
                V_.tensor_tensor(O2[:, w * g:w * g + w].rearrange("p (j d) -> p j d", j=4),
                                 bO[:, 0:w].rearrange("p (j d) -> p j d", j=4),
                                 rs[:, at, :].unsqueeze(2).to_broadcast([128, 4, st.dh]), ALU.mult).then_inc(st.s_Oe, 1)

            def evict_ot(n):
                dve.wait_ge(st.s_ot, n + 1)
                V_.tensor_copy(OT2, bY1[:, 0:128]).then_inc(st.s_ote, 1)

            def evict_y(n):
                dve.wait_ge(st.s_y, n + 1)
                if st.nested:
                    if not isinstance(n, int) or n >= 1:
                        dve.wait_ge(st.s_x, n)
                    V_.tensor_tensor(tmpy, bY1[:, 0:128], gwide, ALU.mult).then_inc(st.s_ye, 1)
                    dve.wait_ge(st.s_res, n * 2 + 2)
                    dve.wait_ge(st.s_ye, n + 1)
                    V_.tensor_tensor(xrow(n), xrow(n), tmpy, ALU.add).then_inc(st.s_x, 1)
                else:
                    V_.scalar_tensor_tensor(xrow(n), bY1[:, 0:128], gates[:, 2:3], xrow(n), ALU.mult,
                                            ALU.add).then_inc(st.s_ye, 1)
                    dve.wait_ge(st.s_ye, n + 1)
                    V_.tensor_tensor(xrow(n), xrow(n), st.bo[:], ALU.add).then_inc(st.s_x, 1)

            def invert(b, g, par):
                while g < 0:
                    g += NS
                    b = b - 1
                    par = 1 - par
                at = st.at(g, par)
                dve.wait_ge(st.s_exp, b * NS + (g + 1))
                V_.reciprocal(rs[:, at, :], sums[:, at, :]).then_inc(st.s_rsr, 1)
                dve.wait_ge(st.s_rsr, b * NS + (g + 1))
                if st.nested:
                    reach = wide[:].rearrange("p (h d) -> p h d", d=st.dh)[:, 4 * g:4 * g + 4, 0]
                    V_.tensor_tensor(rs[:, at, :], rs[:, at, :], reach, ALU.mult).then_inc(st.s_rs, 1)
                else:
                    V_.tensor_tensor(rs[:, at, :], rs[:, at, :], valid[:, bass.ds(b, 1)].to_broadcast([128, 4]),
                                     ALU.mult).then_inc(st.s_rs, 1)

            if st.nested:
                for n in range(3):
                    stats1(n, n % 2)
                    inner_stats(n, n % 2)
                    inner_norm(n, n % 2)
                    if n < 2:
                        evict_h(n, n, n)
                stats1(3, 1)
                inner_stats(3, 1)
            else:
                for n in range(3):
                    stats1(n, n % 2)
                    if n < 2:
                        norm1(n, n % 2, hS[n % 2][:], st.s_h)
                evict_h(0, 0, 0)
                evict_h(1, 1, 1)
            evict_v(0, 2)

            def top(b, g, par):
                u = b * NS + g
                dve.wait_ge(st.s_S, u + 1)
                src = bS[g % 2][:, :].rearrange("p (j k) -> p j k", j=4)
                if not st.nested:
                    if g == 0:
                        dve.wait_ge(st.s_bm, b + 1)
                    wait(dve, st.s_T, u - 3)
                    V_.tensor_tensor(P4[g][:], src, BM[par][:, 4 * g:4 * g + 4, :], ALU.add).then_inc(st.s_add, 1)
                    dve.wait_ge(st.s_add, u + 1)
                    src = P4[g][:]
                wait(dve, st.s_exp, u - 1)
                V_.tensor_reduce(nmx[:, g % 2, :], src, AX.X, ALU.max, negate=True).then_inc(st.s_mx, 1)

            top(0, 0, 0)

            def body(b, par, known, it):
                first = known == 0
                one, two, three, four = (known is None or known + n <= LAST for n in (1, 2, 3, 4))
                if st.nested:
                    if known not in (0, 1):
                        evict_o(b, -3, par)
                    top(b, 1, par)
                    if not first:
                        invert(b, -1, par)
                    if known not in (0, 1):
                        evict_ot(b - 2)
                    if three:
                        inner_norm(b + 3, 1 - par)
                    if four:
                        stats1(b + 4, par)
                    if not first:
                        evict_o(b, -2, par)
                    if two:
                        evict_h(b + 2, par, st.job_of_h(b + 2))
                    if one:
                        top(b + 1, 0, 1 - par)
                    invert(b, 0, par)
                    if known not in (0, 1):
                        evict_y(b - 2)
                    if four:
                        inner_stats(b + 4, par)
                    if one:
                        evict_v(1 - par, st.job_of_v(b + 1))
                    return
                for g in range(NS):
                    if g == 3 and not first:
                        evict_ot(b - 1)
                    if not (first and g < 3):
                        evict_o(b, g - 3, par)
                    if one or g < 3:
                        top(*after(st, b, g, par, it)[:3])
                    if g == 2 and one:
                        evict_v(1 - par, st.job_of_v(b + 1))
                    if g == 3 and two:
                        evict_h(b + 2, par, st.job_of_h(b + 2))
                    if not (first and g == 0):
                        invert(b, g - 1, par)
                    if g == 0 and two:
                        norm1(b + 2, par, hS[par][:], st.s_h)
                    if g == 1 and three:
                        stats1(b + 3, 1 - par)
                    if g == 3 and not first:
                        evict_y(b - 1)

            over_batches(dve, body, 2)
            invert(B, -1, 0)
            if NS == 4:
                evict_o(B, -3, 0)
                evict_o(B, -2, 0)
                evict_o(B, -1, 0)
                evict_ot(LAST)
                evict_y(LAST)
            else:
                evict_o(B, -3, 0)
                evict_ot(B - 2)
                evict_o(B, -2, 0)
                evict_o(B, -1, 0)
                evict_y(B - 2)
                evict_ot(LAST)
                evict_y(LAST)

        def small_pe(pe, st, before):
            NS = st.NS

            def mm(o, l, r, start=True, stop=True):
                return nc.tensor.matmul(o, l, r, start=start, stop=stop)

            def job_h(n, par, job):
                pe.wait_ge(st.s_h, n + 1)
                wait(pe, st.s_Ve, job)
                nc.tensor.transpose(bV[:, 0:128], hS[par][:], ident[:]).then_inc(st.s_V, 1)

            def source(par):
                return hTs[par] if st.nested else ctxS[par]

            def job_v(n, par, job):
                wait(pe, st.s_Ve, job)
                mm(bV[:, 0:128], source(par)[:], st.W[2][:]).then_inc(st.s_V, 1)

            def job_qk(n, par, hjob, half):
                if st.nested:
                    pe.wait_ge(st.s_hb, n + 1)
                else:
                    pe.wait_ge(st.s_Ve, hjob + 1)
                if not st.nested:
                    pe.wait_ge(st.s_ctx[par], (half + 1) * 16)
                wait(pe, st.s_qke, n)
                mm(bA[:, 0:128], st.W[0][:], hTs[par][:])
                mm(bA[:, 128:256], st.W[1][:], source(par)[:]).then_inc(st.s_qk, 1)

            def job_s(b, g, par):
                u = b * NS + g
                if g == 0:
                    pe.wait_ge(st.s_kz, b + 1)
                wait(pe, st.s_exp if st.nested else st.s_add, u - 1)
                mm(bS[g % 2][:, :], q2[par], st.KZ[par][:, 4 * g:4 * g + 4, :].rearrange("p h k -> p (h k)")
                   ).then_inc(st.s_S, 1)

            def job_t(b, g, par):
                while g < 0:
                    g += NS
                    b = b - 1
                    par = 1 - par
                u = b * NS + g
                pe.wait_ge(st.s_exp, u + 1)
                wait(pe, st.s_Te, u - 1)
                for j in range(4):
                    last = nc.tensor.transpose(bP2[g % 2][:, 128 * j:128 * j + 128], P4[st.at(g, par)][:, j, :], ident[:])
                last.then_inc(st.s_T, 1)

            def job_pv(b, g, par):
                while g < 0:
                    g += NS
                    b = b - 1
                    par = 1 - par
                pe.wait_ge(st.s_Te, b * NS + (g + 1))
                wait(pe, st.s_Oe, b * NS + g)
                if g == 0:
                    pe.wait_ge(st.s_Ve, st.job_of_v(b) + 1)
                for j in range(4):
                    h = 4 * g + j
                    last = mm(bO[:, st.dh * j:st.dh * j + st.dh], PT[g % 2][:, j, :], V2[par][:, st.dh * h:st.dh * h + st.dh])
                last.then_inc(st.s_Of, 1)

            def job_ot(n):
                pe.wait_ge(st.s_Oe, n * NS + NS)
                wait(pe, st.s_ye, n)
                nc.tensor.transpose(bY1[:, 0:128], O2, ident[:]).then_inc(st.s_ot, 1)

            def job_y(n):
                pe.wait_ge(st.s_ote, n + 1)
                mm(bY1[:, 0:128], OT2, st.W[3][:]).then_inc(st.s_y, 1)

            pe.wait_ge(before, B)
            pe.wait_ge(st.s_cst, 1)
            job_h(0, 0, 0)
            job_h(1, 1, 1)
            job_qk(0, 0, 0, 0)
            if st.nested:
                job_qk(1, 1, 1, 0)
            job_v(0, 0, 2)
            job_s(0, 0, 0)

            def body(b, par, known, it):
                first = known == 0
                one, two = (known is None or known + n <= LAST for n in (1, 2))
                if st.nested:
                    job_s(b, 1, par)
                    if not first:
                        job_t(b, -1, par)
                    if known not in (0, 1):
                        job_ot(b - 2)
                    if not first:
                        job_pv(b, -2, par)
                    if two:
                        job_h(b + 2, par, st.job_of_h(b + 2))
                    if one:
                        job_s(b + 1, 0, 1 - par)
                    job_t(b, 0, par)
                    if known not in (0, 1):
                        job_y(b - 2)
                    if not first:
                        job_pv(b, -1, par)
                    if one:
                        job_v(b + 1, 1 - par, st.job_of_v(b + 1))
                    if two:
                        job_qk(b + 2, par, st.job_of_h(b + 2), 0)
                    return
                for g in range(NS):
                    if one or g < 3:
                        job_s(*after(st, b, g, par, it)[:3])
                    if not (first and g == 0):
                        job_t(b, g - 1, par)
                    if g == 0 and one:
                        job_qk(b + 1, 1 - par, 1 if first else st.job_of_h(b + 1), it + par)
                    if g == 3 and not first:
                        job_y(b - 1)
                    if not (first and g < 2):
                        job_pv(b, g - 2, par)
                    if g == 2 and not first:
                        job_ot(b - 1)
                    if g == 1 and one:
                        job_v(b + 1, 1 - par, st.job_of_v(b + 1))
                    if g == 2 and two:
                        job_h(b + 2, par, st.job_of_h(b + 2))
            over_batches(pe, body, 2)
            job_t(B, -1, 0)
            if NS == 2:
                job_ot(B - 2)
            job_pv(B, -2, 0)
            job_pv(B, -1, 0)
            if NS == 2:
                job_y(B - 2)
            job_ot(LAST)
            job_y(LAST)

        def experts_sp(sp):
            sp.wait_ge(REL.s_x, B)
            sp.dma_start(out.rearrange("b t d -> t b d"), X[:]).then_inc(s_out, 16)
            sp.wait_ge(m_put, 2 * B * 16)
            for e in range(NE):
                sp.dma_start(Xs[:, 2 * e:2 * e + 2, :],
                             xg[CAP * e:CAP * e + CAP, :].rearrange("(t p) d -> p t d", p=128)).then_inc(m_xs[e], 16)

        def experts_pool(pool):
            pool.wait_ge(m_mv, 1)
            nc.gpsimd.tensor_scalar(rstd_all, mv_all[:, :, 1], EPS, None, ALU.add).then_inc(m_all, 1)
            pool.wait_ge(m_all, 1)
            nc.gpsimd.tensor_tensor(rstd_all, rstd_all, mhalf[:].to_broadcast([128, B]), ALU.pow).then_inc(m_rstd, 1)
            pool.wait_ge(m_slot, 1)
            pool.wait_ge(m_fill, 16)
            for k in range(2):
                for n in range(B):
                    nc.gpsimd.indirect_dma_start(
                        out=xg, out_offset=bass.IndirectOffsetOnAxis(ap=slot_u[:, k, n:n + 1], axis=0),
                        in_=Rows[:, n, :], in_offset=None, bounds_check=SLOTS - 1, oob_is_err=False).then_inc(m_put, 16)
            pool.wait_ge(s_out, 16)
            rows = out.rearrange("b t d -> (b t) d")
            for e in range(NE):
                pool.wait_ge(m_ye, e + 1)
                wait(pool, m_add, 32 * e)
                for t in range(2):
                    nc.gpsimd.indirect_dma_start(
                        out=rows, out_offset=bass.IndirectOffsetOnAxis(ap=Xs[:, 2 * e + t, D + 3:D + 4].bitcast(U32), axis=0),
                        in_=Ys[e % 2][:, 128 * t:128 * t + 128], in_offset=None, bounds_check=B * S - 1, oob_is_err=False,
                        compute_op=ALU.add).then_inc(m_add, 16)
            pool.wait_ge(m_add, 32 * NE)

        def experts_act(act):
            act.wait_ge(REL.s_x, B)
            act.wait_ge(m_gap, 1)
            nc.scalar.activation(gap, gap, ACT.Exp).then_inc(m_exp, 1)
            for e in range(NE):
                act.wait_ge(m_ab, e + 1)
                wait(act, m_hid, e - 1)
                nc.scalar.activation(sil[e % 2], bAB[e % 2][1][:, :], ACT.Silu).then_inc(m_sil, 1)
                if e >= 1:
                    evict_result(act, e - 1)
            evict_result(act, NE - 1)

        def evict_result(act, e):
            act.wait_ge(m_y, e + 1)
            wait(act, m_add, 32 * (e - 1))
            if e == 0:
                act.wait_ge(m_ws, 1)
            for t in range(2):
                last = nc.scalar.activation(Ys[e % 2][:, 128 * t:128 * t + 128], bY[e % 2][:, 128 * t:128 * t + 128],
                                            ACT.Identity, scale=w_slot[:, 2 * e + t:2 * e + t + 1])
            last.then_inc(m_ye, 1)

        def experts_dve(dve, link):
            V_ = nc.vector
            dve.wait_ge(REL.s_x, B)
            for n in range(B):
                last = V_.bn_stats(st_all[:, n, :], X[:, n, :])
            last.then_inc(m_st, 1)
            dve.wait_ge(m_st, 1)
            for n in range(B):
                last = V_.bn_aggr(mv_all[:, n, :], st_all[:, n, :])
            last.then_inc(m_mv, 1)
            V_.memset(ones, 1.0)
            dve.wait_ge(m_w, 16 * 10)
            dve.wait_ge(m_rstd, 1)
            for n in range(B + 2):
                if n < B:
                    V_.tensor_scalar(Rows[:, n, 0:D], X[:, n, :], mv_all[:, n, 0:1], rstd_all[:, n:n + 1], ALU.subtract,
                                     ALU.mult).then_inc(m_h, 1)
                if 1 <= n <= B:
                    dve.wait_ge(m_T, n)
                    V_.tensor_copy(hTs[(n - 1) % 2][:], bXT[(n - 1) % 2][:, 0:128]).then_inc(m_Te, 1)
                if n >= 2:
                    dve.wait_ge(m_L, n - 1)
                    V_.tensor_tensor(logits[:, n - 2, :], bY[n % 2][:, 0:NE], rb, ALU.add).then_inc(m_Le, 1)
            dve.wait_ge(m_Le, B)
            for n in range(B):
                last = V_.max(top8[:, n, :], logits[:, n, :])
            link(last)
            for n in range(B):
                last = V_.max_index(idx8[:, n, :], top8[:, n, :], logits[:, n, :])
            V_.tensor_tensor(gap, top8[:, :, 1], top8[:, :, 0], ALU.subtract).then_inc(m_gap, 1)
            link(last)
            link(V_.tensor_copy(eid, idx8[:, :, 0:2].rearrange("p n k -> p k n")))
            for k, one in enumerate((one0, one1)):
                link(V_.tensor_tensor(one, eid[:, k, :].unsqueeze(2).to_broadcast([128, B, NE]),
                                      iota8.unsqueeze(1).to_broadcast([128, B, NE]), ALU.is_equal))
            V_.tensor_tensor(cnt, one0, one1, ALU.add).then_inc(m_cnt, 1)
            V_.memset(base[:, 0, :], 0.0)
            dve.wait_ge(m_exp, 1)
            w0, w1 = Rows[:, :, D], Rows[:, :, D + 1]
            link(V_.tensor_scalar(gap1, gap, 1.0, None, ALU.add))
            link(V_.reciprocal(gap1, gap1))
            link(V_.tensor_scalar(w0, gap1, gates[:, 3:4], None, ALU.mult))
            link(V_.tensor_tensor(w1, w0, gap, ALU.mult))
            V_.tensor_copy(Rows[:, :, D + 2], eid[:, 0, :])
            V_.tensor_copy(Rows[:, :, D + 3].bitcast(U32), token.bitcast(U32))
            dve.wait_ge(m_pre, 2)
            for n in range(1, B):
                link(V_.tensor_tensor(base[:, n, :], bS[1][:, NE * (n - 1):NE * n], base[:, n - 1, :], ALU.add))
            link(V_.tensor_tensor(pos, bS[0][:, 0:128].rearrange("p (n e) -> p n e", e=NE), base, ALU.add))
            for k, one in enumerate((one0, one1)):
                link(V_.tensor_tensor(picked, one, pos, ALU.mult))
                link(V_.tensor_reduce(place[:, k, :], picked, AX.X, ALU.add))
            link(V_.tensor_scalar(full, place, float(CAP), None, ALU.is_ge))
            link(V_.scalar_tensor_tensor(slot, eid, float(CAP), place, ALU.mult, ALU.add))
            link(V_.scalar_tensor_tensor(slot, full, float(16 * SLOTS), slot, ALU.mult, ALU.add))
            V_.tensor_copy(slot_u, slot).then_inc(m_slot, 1)
            for e in range(NE):
                dve.wait_ge(m_xs[e], 16)
            link(V_.tensor_tensor(first, Xs[:, :, D + 2], owner, ALU.is_equal))
            link(V_.tensor_tensor(w_slot, Xs[:, :, D], Xs[:, :, D + 1], ALU.subtract))
            link(V_.tensor_tensor(w_slot, w_slot, first, ALU.mult))
            V_.tensor_tensor(w_slot, w_slot, Xs[:, :, D + 1], ALU.add).then_inc(m_ws, 1)
            for e in range(NE + 1):
                if e < NE:
                    dve.wait_ge(m_xT, e + 1)
                    V_.tensor_copy(xTs[e % 2], bXT[e % 2][:, 0:256]).then_inc(m_xTe, 1)
                if e >= 1:
                    dve.wait_ge(m_sil, e)
                    wait(dve, m_y, e - 2)
                    V_.tensor_tensor(hid[(e - 1) % 2], bAB[(e - 1) % 2][0][:, :], sil[(e - 1) % 2],
                                     ALU.mult).then_inc(m_hid, 1)

        def experts_pe(pe):
            def mm(o, l, r, start=True, stop=True):
                return nc.tensor.matmul(o, l, r, start=start, stop=stop)
            pe.wait_ge(REL.s_x, B)
            pe.wait_ge(m_w, 16 * 10)
            for n in range(B + 1):
                if n < B:
                    pe.wait_ge(m_h, n + 1)
                    wait(pe, m_Te, n - 1)
                    nc.tensor.transpose(bXT[n % 2][:, 0:128], Rows[:, n, 0:D], ident[:]).then_inc(m_T, 1)
                if n >= 1:
                    pe.wait_ge(m_Te, n)
                    wait(pe, m_Le, n - 2)
                    mm(bY[(n - 1) % 2][:, 0:NE], hTs[(n - 1) % 2][:], rwT).then_inc(m_L, 1)
            pe.wait_ge(m_cnt, 1)
            both = cnt.rearrange("p n e -> p (n e)")
            mm(bS[0][:, 0:128], ustrict, both).then_inc(m_pre, 1)
            mm(bS[1][:, 0:128], ones, both).then_inc(m_pre, 1)
            pe.wait_ge(m_slot, 1)

            def result(e):
                pe.wait_ge(m_hid, e + 1)
                wait(pe, m_ye, e - 1)
                for t in range(2):
                    for c in range(2):
                        last = mm(bY[e % 2][:, 128 * t:128 * t + 128], hid[e % 2][:, 256 * c + 128 * t:256 * c + 128 * t + 128],
                                  Wout[:, e, c, :], start=c == 0, stop=c == 1)
                last.then_inc(m_y, 1)

            for e in range(NE):
                pe.wait_ge(m_xs[e], 16)
                wait(pe, m_xTe, e - 1)
                for t in range(2):
                    last = nc.tensor.transpose(bXT[e % 2][:, 128 * t:128 * t + 128], Xs[:, 2 * e + t, 0:D], ident[:])
                last.then_inc(m_xT, 1)
                pe.wait_ge(m_xTe, e + 1)
                wait(pe, m_hid, e - 1)
                for bank, w in zip(bAB[e % 2], (We, Ve)):
                    for c in range(2):
                        last = mm(bank[:, 256 * c:256 * c + 256], w[:, 2 * e + c, :], xTs[e % 2])
                last.then_inc(m_ab, 1)
                if e >= 1:
                    result(e - 1)
            result(NE - 1)

        @block.sync
        def _(sp):
            sp.dma_start(ident[:], A["ident"]).then_inc(s_ld, 16)
            sp.dma_start(graw[:], A["gates"].partition_broadcast(128)).then_inc(s_ld, 16)
            sp.dma_start(pn[:], A["box_pn"]).then_inc(s_ldb, 16)
            sp.dma_start(valM[:], A["box_row"][0]).then_inc(s_ldb, 16)
            sp.dma_start(rowM[:], A["box_row"][1]).then_inc(s_ldb, 16)
            sp.dma_start(phase[:], A["phase"]).then_inc(s_ldb, 16)
            sp.dma_start(X[:], A["x"].rearrange("b t d -> t b d")).then_inc(s_ldx, 16)
            for dst, name in ((wrep, "wg"), (delta, "delta"), (bgp, "bg"), (WqT, "WqT"), (WkT, "WkT"), (WvT, "WvT"),
                              (WoT, "WoT"), (bq, "bq"), (bk, "bk")):
                sp.dma_start(dst[:], A[name]).then_inc(s_ldw, 16)
            sp.dma_start(bvb[:], A["bv"].partition_broadcast(128)).then_inc(s_ldw, 16)
            sp.dma_start(bob[:], A["bo"].partition_broadcast(128)).then_inc(s_ldw, 16)

            for st in (NEST, REL):
                n = st.name
                for dst, name in zip(st.W + [st.bq, st.bk, st.hm], ("Wq", "Wk", "Wv", "Wo", "bq", "bk", "hm")):
                    sp.dma_start(dst[:], A[f"{name}_{n}"]).then_inc(st.s_w, 16)
                for dst, name in ((st.bv, "bv"), (st.bo, "bo")):
                    sp.dma_start(dst[:], A[f"{name}_{n}"].partition_broadcast(128)).then_inc(st.s_w, 16)
            sp.dma_start(nwb[:], A["norm_wb"]).then_inc(NEST.s_w, 16)
            sp.dma_start(wideT[:], A["wideT"]).then_inc(NEST.s_w, 16)
            sp.dma_start(wide[:], A["wide"]).then_inc(NEST.s_w, 16)

            def load_ctx(n, par, known):
                if known is None or known >= 2:
                    wait(sp, s_V, vjob(n - 3, 3) + 1)
                sp.dma_start(ctxS[par][:], A["ctxT"][:, bass.ds(n, 1) if not isinstance(n, int) else slice(n, n + 1), :]
                             .rearrange("d a t -> d (a t)")).then_inc(s_ctx[par], 16)

            def spread(b1, par, known):
                for hg in range(2):
                    wait(sp, s_Ge, b1 * 4 + (2 * hg + 2))
                    wait(sp, s_P, (b1 - 1) * 4)
                    for h in range(8):
                        sp.dma_start(G[par][:, 8 * hg + h, :],
                                     Gc[hg][NPF * h:NPF * h + NPF, :, :].rearrange("n c m -> n (c m)")).then_inc(s_gd[hg], 16)

            load_ctx(0, 0, 0)
            load_ctx(1, 1, 1)

            def body(b, par, known, it):
                spread(b, par, known)
                if known is None or known + 2 <= LAST:
                    load_ctx(b + 2, par, None if known is None else known + 2)
            over_batches(sp, body)

            sp.wait_ge(s_x1, B)
            sp.wait_ge(s_G, 4 * B)
            sp.dma_start(bias1, A["rel_bias"]).then_inc(REL.s_w, 16)
            sp.dma_start(mrow.bitcast(I32), A["mask"].partition_broadcast(128)).then_inc(REL.s_w, 16)

            if stop >= 4:
                for dst, name in ((We, "W_e"), (Ve, "V_e"), (Wout, "W_out"), (rwT, "rwT"), (ustrict, "ustrict")):
                    sp.dma_start(dst[:] if dst in (We, Ve, Wout) else dst, A[name]).then_inc(m_w, 16)
                sp.dma_start(token.bitcast(I32), A["token"]).then_inc(m_w, 16)
                sp.dma_start(owner, A["owner"].partition_broadcast(128)).then_inc(m_w, 16)
                sp.dma_start(blank[:].bitcast(I32), A["blank"].partition_broadcast(128)).then_inc(m_w, 16)
                for dst, name in ((rb, "rb"), (iota8, "iota8")):
                    sp.dma_start(dst, A[name].partition_broadcast(128)).then_inc(m_w, 16)

            def rel_ctx(n, par, known):
                if known is None or known >= 2:
                    wait(sp, REL.s_V, REL.job_of_v(n - 2) + 1)
                else:
                    sp.wait_ge(s_x1, B)
                sp.dma_start(ctxS[par][:], A["ctxT"][:, bass.ds(n, 1) if not isinstance(n, int) else slice(n, n + 1), :]
                             .rearrange("d a t -> d (a t)")).then_inc(REL.s_ctx[par], 16)
            if stop >= 3:
                rel_ctx(0, 0, 0)
                rel_ctx(1, 1, 1)

                def body(b, par, known, it):
                    if known is None or known + 2 <= LAST:
                        rel_ctx(b + 2, par, None if known is None else known + 2)
                over_batches(sp, body)

            if stop < 4:
                sp.wait_ge([None, s_x1, NEST.s_x, REL.s_x][stop], B)
                sp.dma_start(out.rearrange("b t d -> t b d"), X[:]).then_inc(s_out, 16)
                sp.wait_ge(s_out, 16)
            else:
                sp.wait_ge(m_w, 16 * 10)
                sp.dma_start(xg.rearrange("(a p) r -> p a r", p=128),
                             blank[:].unsqueeze(1).to_broadcast([128, SLOTS // 128, ROW])).then_inc(m_fill, 16)
                experts_sp(sp)

        @block.gpsimd
        def _(pool):
            pool.wait_ge(s_ldb, 64)
            with pool.Fori(0, B) as b:
                pool.wait_ge(s_sub, b + 1)
                Eb = E[:, bass.ds(b, 1), :, :].rearrange("p a c m -> p (a c) m")
                nc.gpsimd.tensor_tensor(Eb, Eb, scl[:, bass.ds(b, 1), :].rearrange("p a c -> p (a c)").unsqueeze(2)
                                        .to_broadcast([128, NC, S]), ALU.mult).then_inc(s_scl, 1)

            def prep(n, par):
                pool.wait_ge(s_mv, n + 1)
                nc.gpsimd.tensor_tensor(rstd[:, par:par + 1], mv[:, par, 1:2], epst[:], ALU.add).then_inc(s_var, 1)
                pool.wait_ge(s_var, n + 1)
                nc.gpsimd.tensor_tensor(rstd[:, par:par + 1], rstd[:, par:par + 1], mhalf[:], ALU.pow).then_inc(s_rstd, 1)
            prep(0, 0)
            prep(1, 1)

            def body(b, par, known, it):
                if known is None or known + 2 <= LAST:
                    prep(b + 2, par)
            over_batches(pool, body)

            if stop >= 2:
                small_pool(pool, NEST, s_x1)
            if stop >= 3:
                small_pool(pool, REL, NEST.s_x)
            if stop >= 4:
                experts_pool(pool)

        @block.scalar
        def _(act):
            act.wait_ge(s_ld, 32)
            nc.scalar.activation(gates[:], graw[:], ACT.Tanh).then_inc(s_xb, 1)
            act.wait_ge(s_row, 1)
            nc.scalar.activation(valM[64:128], valM[64:128], ACT.Ln)
            nc.scalar.activation(valN[64:128], valN[64:128], ACT.Ln).then_inc(s_lnw, 1)
            with act.Fori(0, B) as b:
                act.wait_ge(s_abs, b + 1)
                Eb = E[0:64, bass.ds(b, 1), :, :]
                nc.scalar.activation(Eb, Eb, ACT.Ln).then_inc(s_ln, 1)
            with act.Fori(0, B) as b:
                act.wait_ge(s_red, b + 1)
                Eb = E[:, bass.ds(b, 1), :, :]
                nc.scalar.activation(Eb, Eb, ACT.Sin, bias=phase[:, 1:2]).then_inc(s_sin, 1)

            def evict_qk(b1, par, g):
                act.wait_ge(s_qk, b1 * 4 + (g + 1))
                for i in range(2):
                    t = 2 * g + i
                    last = nc.scalar.activation(qS[par][:, t, :], bA[:, 128 * i:128 * i + 128], ACT.Identity,
                                                bias=bq[:, t:t + 1], scale=DK ** -0.5)
                last.then_inc(s_qke, 1)

            def evict_g(b1, g):
                hg, half = g // 2, g % 2
                act.wait_ge(s_G, b1 * 4 + (g + 1))
                if not isinstance(b1, int) or b1 > 0:
                    wait(act, s_gd[hg], b1 * GD)
                nc.scalar.activation(Gc[hg][:, 4 * half:4 * half + 4, :].rearrange("p c m -> p (c m)"), bG[:, :],
                                     ACT.Identity, bias=bgp[:, hg:hg + 1]).then_inc(s_Ge, 1)

            act.wait_ge(s_wb, 1)
            for g in range(4):
                evict_g(0, g)
                evict_qk(0, 0, g)

            def body(b, par, known, it):
                for g in range(4):
                    u = b * 4 + g
                    act.wait_ge(s_mx, u + 1)
                    wait(act, s_T, u - 1)
                    for j in range(4):
                        last = nc.scalar.activation(Pe[g % 2][:, j, :], bS[g % 2][:, 128 * j:128 * j + 128], ACT.Exp,
                                                    bias=nmx[:, g % 2, j:j + 1])
                    last.then_inc(s_exp, 1)
                    if known != 0 or g > 0:
                        act.wait_ge(s_T, u)
                        wait(act, s_Of, u - 2)
                        nc.scalar.copy(PT[(g - 1) % 2][:].rearrange("p j q -> p (j q)"),
                                       bP[:, :]).then_inc(s_Te, 1)
                    if known is None or known < LAST:
                        evict_g(b + 1, g)
                        evict_qk(b + 1, 1 - par, g)
            over_batches(act, body)
            act.wait_ge(s_T, 4 * B)
            nc.scalar.copy(PT[1][:].rearrange("p j q -> p (j q)"), bP[:, :]).then_inc(s_Te, 1)

            if stop >= 2:
                small_act(act, NEST, s_x1)
            if stop >= 3:
                small_act(act, REL, NEST.s_x)
            if stop >= 4:
                experts_act(act)

        @block.vector
        def _(dve):
            chain = [0]

            def link(ins):
                chain[0] += 1
                ins.then_inc(s_c, 1)
                dve.wait_ge(s_c, chain[0])

            V_ = nc.vector
            V_.memset(mhalf[:], -0.5)
            V_.memset(epst[:], EPS)
            for par in range(2):
                V_.memset(kZ[par][0:64, :, 1, :], 0.0)
                V_.memset(kZ[par][64:128, :, 0, :], 0.0)
            dve.wait_ge(s_ldb, 64)
            link(V_.tensor_tensor(scl[:], pn[:, 1], pn[:, 0], ALU.subtract))
            link(V_.tensor_scalar(scl[:], scl[:], 1.0, None, ALU.add))
            link(V_.tensor_copy(valN[64:128], scl[64:128]))
            link(V_.tensor_tensor(valN[0:64], pn[0:64, 0], pn[0:64, 1], ALU.add))
            link(V_.tensor_scalar(valN[0:64], valN[0:64], 0.5, None, ALU.mult))
            link(V_.reciprocal(scl[0:64], scl[0:64]))
            link(V_.memset(scl[64:128], -1.0))
            link(V_.tensor_tensor(valM[64:128], rowM[64:128], valM[64:128], ALU.subtract))
            link(V_.tensor_scalar(valM[64:128], valM[64:128], 1.0, None, ALU.add))
            link(V_.tensor_tensor(valM[0:64], rowM[0:64], valM[0:64], ALU.add))
            V_.tensor_scalar(valM[0:64], valM[0:64], 0.5, None, ALU.mult).then_inc(s_row, 1)
            dve.wait_ge(s_row, 1)
            dve.wait_ge(s_lnw, 1)
            with dve.Fori(0, B) as b:
                Eb = E[:, bass.ds(b, 1), :, :].rearrange("p a c m -> p (a c) m")
                V_.tensor_tensor(Eb, valM[:, bass.ds(b, 1), :].to_broadcast([128, NC, S]),
                                 valN[:, bass.ds(b, 1), :].rearrange("p a c -> p (a c)").unsqueeze(2)
                                 .to_broadcast([128, NC, S]), ALU.subtract).then_inc(s_sub, 1)
            with dve.Fori(0, B) as b:
                dve.wait_ge(s_scl, b + 1)
                Eb = E[0:64, bass.ds(b, 1), :, :].rearrange("p a c m -> p (a c m)")
                Eu = Eb.bitcast(U32)
                V_.tensor_scalar(Eu, Eu, 0x7FFFFFFF, None, ALU.bitwise_and).then_inc(s_absb, 1)
                dve.wait_ge(s_absb, b + 1)
                V_.tensor_scalar(Eb, Eb, 1e-3, None, ALU.max).then_inc(s_abs, 1)
            with dve.Fori(0, B) as b:
                dve.wait_ge(s_ln, b + 1)
                Eb = E[:, bass.ds(b, 1), :, :].rearrange("p a c m -> p (a c m)")
                Kb = KR[:, 0, :]
                V_.tensor_scalar(Kb, Eb, 100.0 / TWO_PI, phase[:, 0:1], ALU.mult, ALU.add).then_inc(s_redc, 1)
                dve.wait_ge(s_redc, b * 5 + 1)
                V_.tensor_scalar(Kb, Kb, ROUND, -ROUND, ALU.add, ALU.add).then_inc(s_redc, 1)
                V_.tensor_scalar(Eb, Eb, 100.0, None, ALU.mult).then_inc(s_redc, 1)
                dve.wait_ge(s_redc, b * 5 + 3)
                V_.scalar_tensor_tensor(Eb, Kb, -PI_HI, Eb, ALU.mult, ALU.add).then_inc(s_redc, 1)
                dve.wait_ge(s_redc, b * 5 + 4)
                V_.scalar_tensor_tensor(Eb, Kb, -PI_LO, Eb, ALU.mult, ALU.add).then_inc(s_redc, 1)
                dve.wait_ge(s_redc, b * 5 + 5)
                V_.tensor_scalar(Eb, Eb, phase[:, 2:3], phase[:, 3:4], ALU.max, ALU.min).then_inc(s_red, 1)

            dve.wait_ge(s_ldw, 16 * 11)
            for hg in range(2):
                last = V_.tensor_tensor(Wblk[:, hg], wrep[:, 8 * hg:8 * hg + 8].unsqueeze(2).to_broadcast([128, 8, NPF]),
                                        delta[:].unsqueeze(1).to_broadcast([128, 8, NPF]), ALU.mult)
            link(last)
            link(V_.tensor_scalar(bq[:], bq[:], DK ** -0.5, None, ALU.mult))
            dve.wait_ge(s_xb, 1)
            link(V_.tensor_scalar(bob[:], bob[:], gates[:, 0:1], None, ALU.mult))
            dve.wait_ge(s_ldx, 16)
            V_.memset(sums[:], 0.0).then_inc(s_wb, 1)

            def prep(n, par):
                xb = X[:, bass.ds(n, 1), :].rearrange("p a d -> p (a d)")
                V_.bn_stats(st6[:, par, :], xb).then_inc(s_st, 1)
                dve.wait_ge(s_st, n + 1)
                V_.memset(spare[:, par:par + 1], 0.0)
                V_.bn_aggr(mv[:, par, :], st6[:, par, :]).then_inc(s_mv, 1)

            def norm(n, par):
                xb = X[:, bass.ds(n, 1), :].rearrange("p a d -> p (a d)")
                dve.wait_ge(s_rstd, n + 1)
                wait(dve, s_mv, n + 1)
                V_.tensor_scalar(hS[par][:], xb, mv[:, par, 0:1], rstd[:, par:par + 1], ALU.subtract,
                                 ALU.mult).then_inc(s_h, 1)

            def evict_h(par, job):
                dve.wait_ge(s_V, job + 1)
                V_.tensor_copy(hTs[par][:], bV[:, 0:128]).then_inc(s_Ve, 1)

            def evict_v(par, g, job):
                dve.wait_ge(s_V, job + 1)
                V_.tensor_tensor(Vs[par][:, 256 * g:256 * g + 256], bV[:, 0:256], bvb[:, 256 * g:256 * g + 256],
                                 ALU.add).then_inc(s_Ve, 1)

            def evict_k(b1, par, g):
                dve.wait_ge(s_qke, b1 * 4 + (g + 1))
                for r in range(2):
                    rows = slice(64 * r, 64 * r + 64)
                    last = V_.tensor_tensor(kZ[par][rows, 2 * g:2 * g + 2, r, :],
                                            bA[rows, 256:512].rearrange("p (i k) -> p i k", i=2),
                                            bk[rows, 2 * g:2 * g + 2].unsqueeze(2).to_broadcast([64, 2, 128]), ALU.add)
                last.then_inc(s_ke, 1)

            def evict_o(b, g):
                while g < 0:
                    g += 4
                    b = b - 1
                dve.wait_ge(s_Of, b * 4 + (g + 1))
                dve.wait_ge(s_rs, b * 4 + (g + 1))
                V_.tensor_tensor(Os[:, 4 * g:4 * g + 4, :], bO[:, 0:256].rearrange("p (j d) -> p j d", j=4),
                                 rs[:, g, :].unsqueeze(2).to_broadcast([128, 4, DK]), ALU.mult).then_inc(s_Oe, 1)

            def evict_ot(n, half):
                dve.wait_ge(s_ot, n * 2 + (half + 1))
                V_.tensor_copy(OTs[:, 4 * half:4 * half + 4, :].rearrange("p t q -> p (t q)"), bY1[:, :]).then_inc(s_ote, 1)

            def evict_y(n):
                dve.wait_ge(s_y, n + 1)
                V_.scalar_tensor_tensor(xrow(n), bY1[:, 0:128], gates[:, 0:1], xrow(n), ALU.mult, ALU.add).then_inc(s_ye, 1)
                dve.wait_ge(s_ye, n + 1)
                V_.tensor_tensor(xrow(n), xrow(n), bob[:], ALU.add).then_inc(s_x1, 1)

            prep(0, 0)
            prep(1, 1)
            norm(0, 0)
            norm(1, 1)
            evict_h(0, 0)
            evict_h(1, 1)
            for g in range(4):
                evict_k(0, 0, g)
                evict_v(0, g, vjob(-1, g))

            def top(b, g):
                u = b * 4 + g
                dve.wait_ge(s_S, u + 1)
                wait(dve, s_exp, u - 1)
                V_.tensor_reduce(nmx[:, g % 2, :], bS[g % 2][:, :].rearrange("p (j k) -> p j k", j=4), AX.X,
                                 ALU.max, negate=True).then_inc(s_mx, 1)

            top(0, 0)

            def body(b, par, known, it):
                for g in range(4):
                    u = b * 4 + g
                    first = known == 0
                    more = known is None or known < LAST
                    if g == 3 and not first:
                        evict_ot(b - 1, 0)
                    if more or g < 3:
                        top(b + (g + 1) // 4, (g + 1) % 4)
                    if not (first and g == 0):
                        dve.wait_ge(s_P, u)
                        V_.reciprocal(rs[:, (g - 1) % 4, :], sums[:, (g - 1) % 4, :]).then_inc(s_rs, 1)
                    if not (first and g < 3):
                        evict_o(b, g - 3)
                    if g == 0 and (known is None or known + 2 <= LAST):
                        prep(b + 2, par)
                    if g == 1 and (known is None or known + 2 <= LAST):
                        norm(b + 2, par)
                    dve.wait_ge(s_exp, u + 1)
                    if g % 2 == 0:
                        dve.wait_ge(s_gd[g // 2], (b + 1) * GD)
                    for j in range(4):
                        last = V_.scalar_tensor_tensor(Pe[g % 2][:, j, :], G[par][:, 4 * g + j, :], GMIN,
                                                       Pe[g % 2][:, j, :], ALU.max, ALU.mult,
                                                       accum_out=sums[:, g, j:j + 1])
                    last.then_inc(s_P, 1)
                    if g == 3 and not first:
                        evict_ot(b - 1, 1)
                    if g == 0 and known not in (0, 1):
                        evict_y(b - 2)
                    if more:
                        evict_k(b + 1, 1 - par, g)
                        evict_v(1 - par, g, vjob(b, g))
                if known is None or known + 2 <= LAST:
                    evict_h(par, vjob(b, 4))
            over_batches(dve, body)
            dve.wait_ge(s_P, 4 * B)
            V_.reciprocal(rs[:, 3, :], sums[:, 3, :]).then_inc(s_rs, 1)
            evict_y(B - 2)
            evict_o(B, -3)
            evict_o(B, -2)
            evict_o(B, -1)
            evict_ot(LAST, 0)
            evict_ot(LAST, 1)
            evict_y(LAST)

            if stop >= 2:
                small_dve(dve, NEST, s_x1, link)
            if stop >= 3:
                small_dve(dve, REL, NEST.s_x, link)
            if stop >= 4:
                experts_dve(dve, link)

        @block.tensor
        def _(pe):
            M = nc.tensor.matmul

            def mm(o, l, r, start=True, stop=True):
                return M(o, l, r, start=start, stop=stop)

            def job_h(n, par, job):
                pe.wait_ge(s_h, n + 1)
                wait(pe, s_Ve, job)
                nc.tensor.transpose(bV[:, 0:128], hS[par][:], ident[:]).then_inc(s_V, 1)

            def job_v(n, par, g, job, half):
                if g == 0:
                    pe.wait_ge(s_ctx[par], (half + 1) * 16)
                wait(pe, s_Ve, job)
                mm(bV[:, 0:256], ctxS[par][:], WvT[:, 256 * g:256 * g + 256]).then_inc(s_V, 1)

            def job_qk(n, par, g, hjob, half):
                if g == 0:
                    pe.wait_ge(s_Ve, hjob + 1)
                    pe.wait_ge(s_ctx[par], (half + 1) * 16)
                wait(pe, s_ke, n * 4 + g)
                for i in range(2):
                    t = 2 * g + i
                    mm(bA[:, 128 * i:128 * i + 128], WqT[:, 128 * t:128 * t + 128], hTs[par][:])
                for i in range(2):
                    t = 2 * g + i
                    last = mm(bA[:, 256 + 128 * i:384 + 128 * i], WkT[:, 128 * t:128 * t + 128], ctxS[par][:])
                last.then_inc(s_qk, 1)

            def job_g(n, g):
                if g == 0:
                    pe.wait_ge(s_sin, n + 1)
                wait(pe, s_Ge, n * 4 + g)
                hg, half = g // 2, g % 2
                mm(bG[:, :], Wblk[:, hg].rearrange("p h n -> p (h n)"),
                   E[:, bass.ds(n, 1), 4 * half:4 * half + 4, :].rearrange("p a c m -> p (a c m)")).then_inc(s_G, 1)

            def job_t(b, g):
                while g < 0:
                    g += 4
                    b = b - 1
                u = b * 4 + g
                pe.wait_ge(s_P, u + 1)
                wait(pe, s_Te, u)
                for j in range(4):
                    last = nc.tensor.transpose(bP[:, 128 * j:128 * j + 128], Pe[g % 2][:, j, :], ident[:])
                last.then_inc(s_T, 1)

            def job_pv(b, g, par):
                while g < 0:
                    g += 4
                    b = b - 1
                    par = 1 - par
                pe.wait_ge(s_Te, b * 4 + (g + 1))
                wait(pe, s_Oe, b * 4 + g)
                if g == 0:
                    wait(pe, s_Ve, vjob(b - 1, 3) + 1)
                for j in range(4):
                    h = 4 * g + j
                    last = mm(bO[:, 64 * j:64 * j + 64], PT[g % 2][:, j, :], Vs[par][:, 64 * h:64 * h + 64])
                last.then_inc(s_Of, 1)

            def job_ot(n, half):
                pe.wait_ge(s_Oe, n * 4 + 4)
                if half == 0:
                    wait(pe, s_ye, n)
                else:
                    pe.wait_ge(s_ote, n * 2 + 1)
                for i in range(4):
                    t = 4 * half + i
                    last = nc.tensor.transpose(bY1[:, 128 * i:128 * i + 128],
                                               Os[:, 2 * t:2 * t + 2, :].rearrange("p h d -> p (h d)"), ident[:])
                last.then_inc(s_ot, 1)

            def job_y(n):
                pe.wait_ge(s_ote, n * 2 + 2)
                for t in range(PAIRS):
                    last = mm(bY1[:, 0:128], OTs[:, t, :], WoT[:, t, :], start=t == 0, stop=t == PAIRS - 1)
                last.then_inc(s_y, 1)

            def job_s(b, g, par):
                u = b * 4 + g
                pe.wait_ge(s_ke, u + 1)
                wait(pe, s_exp, u - 1)
                for i in range(2):
                    t = 2 * g + i
                    last = mm(bS[g % 2][:, 256 * i:256 * i + 256], qS[par][:, t, :],
                              kZ[par][:, t, :, :].rearrange("p r k -> p (r k)"))
                last.then_inc(s_S, 1)

            pe.wait_ge(s_ld, 32)
            pe.wait_ge(s_wb, 1)
            job_h(0, 0, 0)
            job_h(1, 1, 1)
            for g in range(4):
                job_g(0, g)
                job_qk(0, 0, g, 0, 0)
                job_v(0, 0, g, vjob(-1, g), 0)
            job_s(0, 0, 0)

            def body(b, par, known, it):
                first = known == 0
                more = known is None or known < LAST
                for g in range(4):
                    if g < 3:
                        job_s(b, g + 1, par)
                    elif more:
                        job_s(b + 1, 0, 1 - par)
                    if more:
                        job_g(b + 1, g)
                    if g == 3 and not first:
                        job_ot(b - 1, 1)
                    if not (first and g == 0):
                        job_t(b, g - 1)
                    if more:
                        job_qk(b + 1, 1 - par, g, 1 if first else vjob(b - 1, 4), it + par)
                    if g == 0 and known not in (0, 1):
                        job_y(b - 2)
                    if more:
                        job_v(b + 1, 1 - par, g, vjob(b, g), it + par)
                    if not (first and g < 2):
                        job_pv(b, g - 2, par)
                    if g == 2 and not first:
                        job_ot(b - 1, 0)
                if known is None or known + 2 <= LAST:
                    job_h(b + 2, par, vjob(b, 4))
            over_batches(pe, body)
            job_t(B, -1)
            job_y(B - 2)
            job_pv(B, -2, 0)
            job_pv(B, -1, 0)
            job_ot(LAST, 0)
            job_ot(LAST, 1)
            job_y(LAST)
            if stop >= 2:
                small_pe(pe, NEST, s_x1)
            if stop >= 3:
                small_pe(pe, REL, NEST.s_x)
            if stop >= 4:
                experts_pe(pe)


NAMES = ["x", "ctxT", "ident", "gates", "box_pn", "box_row", "phase", "wg", "delta", "bg", "WqT", "WkT", "WvT",
         "WoT", "bq", "bk", "bv", "bo", "rel_bias", "mask", "norm_wb", "wide", "wideT"]
NAMES += ["W_e", "V_e", "W_out", "rwT", "ustrict", "rb", "iota8", "token", "owner", "blank"]
NAMES += [f"{x}_{n}" for n in ("nest", "rel") for x in ("Wq", "Wk", "Wv", "Wo", "bq", "bk", "hm", "bv", "bo")]


def layouts(I):
    a = {k: np.asarray(v) for k, v in I.items()}
    f32 = np.float32
    L = {}
    L["x"] = a["x"]
    L["ctxT"] = a["ctx_1024"].transpose(2, 0, 1)
    L["ident"] = np.eye(128, dtype=f32)
    L["gates"] = np.array([a["g_xattn"][0], a["g_ffn"][0], a["g_xattn"][1], a["g_ffn"][1]], f32)
    box = a["fside_BxSx4_0"]
    axis = [0, 1, 0, 1, 0, 1, 0, 1]
    lo, hi = box[:, :, axis], box[:, :, [2 + i for i in axis]]
    both = np.stack([lo, hi])
    L["box_pn"] = both.reshape(2, B, NPF, NC, NF).transpose(4, 2, 0, 1, 3).reshape(128, 2, B, NC)
    L["box_row"] = np.repeat(both.transpose(0, 3, 1, 2), NPF, axis=1)
    order = [0, 1, 4, 5, 2, 3, 6, 7]
    L["wg"] = np.repeat(a["L0_xattn_Wg"][:, order].T, NPF, axis=0)
    L["delta"] = np.tile(np.eye(NPF, dtype=f32), (NF, 1))
    cos = np.repeat(np.array([0, 0, 1, 1, 0, 0, 1, 1], f32), NPF)
    bias = (cos * f32(math.pi / 2)).astype(f32)
    L["phase"] = np.stack([cos * f32(0.25), bias, -f32(PI_SAFE) - bias, f32(PI_SAFE) - bias], 1).astype(f32)
    L["bg"] = np.repeat(a["L0_xattn_bg"].reshape(2, 8).T, NPF, axis=0)
    for n in "qkv":
        L[f"W{n}T"] = a[f"L0_xattn_W{n}"].T
    L["WoT"] = a["L0_xattn_Wo"].T.reshape(PAIRS, 128, 128).transpose(1, 0, 2)
    L["bq"] = a["L0_xattn_bq"].reshape(PAIRS, 128).T
    L["bk"] = a["L0_xattn_bk"].reshape(PAIRS, 128).T
    L["bv"] = a["L0_xattn_bv"]
    L["bo"] = a["L0_xattn_bo"]
    for n, w, src in (("nest", 16, "L0_ffn_{}_{}"), ("rel", 8, "L1_xattn_{}{}")):
        for x in "qkvo":
            name, bname = (src.format(x, "w"), src.format(x, "b")) if n == "nest" else (src.format("W", x), src.format("b", x))
            L[f"W{x}_{n}"] = a[name].T
            L[f"b{x}_{n}"] = a[bname].reshape(128, 1) if x in "qk" else a[bname]
        L[f"hm_{n}"] = np.repeat(np.eye(128 // w, dtype=f32), w, axis=0)
    L["norm_wb"] = np.stack([a["L0_ffn_norm_w"], a["L0_ffn_norm_b"]], 1)
    experts = a["L0_ffn_router_prob"].shape[2]
    reach = D // 2 ** (np.arange(S) // (S // experts))
    L["wide"] = (np.arange(D)[None, :] < reach[:, None]).astype(f32)
    L["wideT"] = L["wide"].T
    L["mask"] = a["mask_Bx1x1xS2_ik0"].reshape(B, S)
    rel = a["L1_xattn_rel_emb"]
    most = (rel.shape[0] - 1) // 2
    at = np.clip(np.arange(S)[None, :] - np.arange(S)[:, None], -most, most) + most
    L["rel_bias"] = rel[at].transpose(0, 2, 1)
    L["W_e"] = a["L1_ffn_W"].transpose(1, 0, 2).reshape(D, 2 * NE, 128)
    L["V_e"] = a["L1_ffn_V"].transpose(1, 0, 2).reshape(D, 2 * NE, 128)
    L["W_out"] = a["L1_ffn_W_out"].reshape(NE, 2, 128, D).transpose(2, 0, 1, 3)
    L["rwT"] = a["L1_ffn_router_w"].T
    L["rb"] = a["L1_ffn_router_b"]
    L["iota8"] = np.arange(NE, dtype=f32)
    L["token"] = (np.arange(B)[None, :] * S + np.arange(S)[:, None]).astype(np.int32)
    L["owner"] = (np.arange(SLOTS // 128) * 128 // CAP).astype(f32)
    L["blank"] = np.array([0] * (ROW - 1) + [1 << 20], np.int32)
    L["ustrict"] = np.triu(np.ones((128, 128), f32), 1)
    return {k: np.ascontiguousarray(v) for k, v in L.items()}


def kernel(**inputs):
    import concourse.bacc as bacc
    from concourse.bass_utils import run_bass_kernel_spmd

    L = layouts(inputs)
    nc = bacc.Bacc("TRN2", target_bir_lowering=False, num_devices=1)
    A = {n: nc.dram_tensor(n + "_dram", L[n].shape, mybir.dt.from_np(L[n].dtype), kind="ExternalInput").ap()
         for n in NAMES}
    out = nc.dram_tensor("out_dram", (B, S, D), F32, kind="ExternalOutput").ap()
    build_program(nc, A, out)
    r = run_bass_kernel_spmd(nc, [{n + "_dram": L[n] for n in NAMES}], core_ids=[0])
    return r.results[0]["out_dram"]
```

```python
import math
from contextlib import ExitStack

import numpy as np
import concourse.bass as bass
from concourse import mybir

F32 = mybir.dt.float32
I32 = mybir.dt.int32
U32 = mybir.dt.uint32
ALU = mybir.AluOpType
ACT = mybir.ActivationFunctionType
AX = mybir.AxisListType

B, S, D = 16, 128, 128
NH, DK = 16, 64
PAIRS = NH * DK // 128
NF, NPF = 8, 16
NC = S // NPF
EPS = 1e-5
GMIN = 1e-6
NEG = -1e30
TWO_PI = 2.0 * math.pi
PI_HI = 6.28125
PI_LO = TWO_PI - PI_HI
ROUND = 1.5 * 2.0 ** 23
PI_SAFE = 3.1415925
NE, HID, CAP = 8, 256, 256
SLOTS = NE * CAP
ROW = D + 3
LAST = B - 1
EARLY = 4


def wait(eng, sem, value):
    if isinstance(value, int) and value <= 0:
        return
    eng.wait_ge(sem, value)


def over_batches(eng, body, tail=1, head=1):
    for b in range(2 * head):
        body(b, b % 2, b, b // 2)
    with eng.Fori(head, B // 2 - tail) as it:
        body(it * 2, 0, None, it)
        body(it * 2 + 1, 1, None, it)
    for b in range(B - 2 * tail, B):
        body(b, b % 2, b, b // 2)


class Stage:

    def __init__(self, sem, name, slots, width, nested):
        self.name = name
        self.NS = slots
        self.dh = width
        self.nested = nested
        self.s_S = sem(f"s_S_{name}")
        self.s_mx = sem(f"s_mx_{name}")
        self.s_exp = sem(f"s_exp_{name}")
        self.s_T = sem(f"s_T_{name}")
        self.s_Te = sem(f"s_Te_{name}")
        self.s_Of = sem(f"s_Of_{name}")
        self.s_Oe = sem(f"s_Oe_{name}")
        self.s_ot = sem(f"s_ot_{name}")
        self.s_ote = sem(f"s_ote_{name}")
        self.s_y = sem(f"s_y_{name}")
        self.s_ye = sem(f"s_ye_{name}")
        self.s_qk = sem(f"s_qk_{name}")
        self.s_qke = sem(f"s_qke_{name}")
        self.s_kz = sem(f"s_kz_{name}")
        self.s_add = sem(f"s_add_{name}")
        self.s_V = sem(f"s_V_{name}")
        self.s_Ve = sem(f"s_Ve_{name}")
        self.s_st = sem(f"s_st_{name}")
        self.s_mv = sem(f"s_mv_{name}")
        self.s_var = sem(f"s_var_{name}")
        self.s_rstd = sem(f"s_rstd_{name}")
        self.s_h = sem(f"s_h_{name}")
        self.s_rs = sem(f"s_rs_{name}")
        self.s_rsr = sem(f"s_rsr_{name}")
        self.s_x = sem(f"s_x_{name}")
        self.s_w = sem(f"s_w_{name}")
        self.s_cst = sem(f"s_cst_{name}")
        if nested:
            self.s_h1 = sem(f"s_h1_{name}")
            self.s_st2 = sem(f"s_st2_{name}")
            self.s_mv2 = sem(f"s_mv2_{name}")
            self.s_var2 = sem(f"s_var2_{name}")
            self.s_rstd2 = sem(f"s_rstd2_{name}")
            self.s_tx = sem(f"s_tx_{name}")
            self.s_hb = sem(f"s_hb_{name}")
            self.s_res = sem(f"s_res_{name}")
        else:
            self.s_bm = sem(f"s_bm_{name}")
            self.s_ctx = [sem(f"s_ctx{i}_{name}") for i in range(2)]

    def at(self, g, par):
        return g if self.NS == 4 else 2 * par + g

    def job_of_v(self, n):
        if isinstance(n, int) and n == 0:
            return 2
        if isinstance(n, int) and n == LAST:
            return LAST * 2 + 1
        return n * 2 + (2 if self.nested else 1)

    def job_of_h(self, n):
        return n if isinstance(n, int) and n < 2 else n * 2 + (-1 if self.nested else 0)


def build_program(nc, A, out, stop=99):
    ctx = ExitStack()
    with ctx:
        def sb(name, shape, dt=F32):
            return ctx.enter_context(nc.sbuf_tensor(name, shape, dt))

        def sem(name):
            return ctx.enter_context(nc.semaphore(name))

        banks = {n: ctx.enter_context(nc.psum_tensor(n, [128, 512], F32))
                 for n in ("S0", "S1", "T0", "T1", "A0", "D0", "D1", "O0")}
        bS = [banks["S0"], banks["S1"]]
        bT = [banks["T0"], banks["T1"]]
        bP, bY1 = bT
        bA, bG, bV, bO = banks["A0"], banks["D0"], banks["D1"], banks["O0"]
        bP2 = [bP, bG]

        X = sb("X", [128, B, D])
        ident = sb("ident", [128, 128])
        gates = sb("gates", [128, 4])
        graw = sb("graw", [128, 4])
        mhalf = sb("mhalf", [128, 1])
        epst = sb("epst", [128, 1])
        one = sb("one", [128, 1])
        spare = sb("spare", [128, 2])
        pad = sb("pad", [128, B * NC * S])
        KR = sb("KR", [128, 2, NC * S])
        factor = sb("factor", [128, 4])
        Wblk = sb("Wblk", [128, 2, 8, NPF])
        wrep = sb("wrep", [128, NH])
        delta = sb("delta", [128, NPF])
        bgp = sb("bgp", [128, 2])
        phase = sb("phase", [128, 4])
        valM = sb("valM", [128, B, S])
        rowM = sb("rowM", [128, B, S])
        pn = sb("pn", [128, 2, B, NC])
        valN = sb("valN", [128, B, NC])
        scl = sb("scl", [128, B, NC])
        G = [sb(f"G{i}", [128, NH, S]) for i in range(2)]
        Gc = [sb(f"Gc{i}", [128, NC, S]) for i in range(2)]
        WqT = sb("WqT", [128, NH * DK])
        WkT = sb("WkT", [128, NH * DK])
        WvT = sb("WvT", [128, NH * DK])
        WoT = sb("WoT", [128, PAIRS, 128])
        bq = sb("bq", [128, PAIRS])
        bk = sb("bk", [128, PAIRS])
        bvb = sb("bvb", [128, NH * DK])
        bob = sb("bob", [128, 128])
        ctxS = [sb(f"ctxS{i}", [128, 128]) for i in range(2)]
        qS = [sb(f"qS{i}", [128, PAIRS, 128]) for i in range(2)]
        kZ = [sb(f"kZ{i}", [128, PAIRS, 2, 128]) for i in range(2)]
        Vs = [sb(f"Vs{i}", [128, NH * DK]) for i in range(2)]
        st6 = sb("st6", [128, 2, 6])
        mv = sb("mv", [128, 2, 2])
        rstd = sb("rstd", [128, 2])
        hS = [sb(f"hS{i}", [128, 128]) for i in range(2)]
        hTs = [sb(f"hTs{i}", [128, 128]) for i in range(2)]
        Pe = [sb(f"Pe{i}", [128, 4, 128]) for i in range(2)]
        PT = [sb(f"PT{i}", [128, 4, 128]) for i in range(2)]
        nmx = sb("nmx", [128, 2, 4])
        sums = sb("sums", [128, 4, 4])
        rs = sb("rs", [128, 4, 4])
        Os = sb("Os", [128, NH, DK])
        OTs = sb("OTs", [128, PAIRS, 128])

        s_ld = sem("s_ld"); s_ldx = sem("s_ldx"); s_ldb = sem("s_ldb"); s_ldr = sem("s_ldr"); s_ldw = sem("s_ldw")
        s_c = sem("s_c")
        s_a = sem("s_a")
        s_const = sem("s_const")
        s_row = sem("s_row"); s_lnw = sem("s_lnw")
        s_sub = sem("s_sub"); s_turn = sem("s_turn"); s_early = sem("s_early"); s_scl = sem("s_scl"); s_abs = sem("s_abs"); s_absb = sem("s_absb"); s_ln = sem("s_ln")
        s_red = sem("s_red"); s_redc = sem("s_redc"); s_sin = sem("s_sin")
        s_xb = sem("s_xb"); s_wb = sem("s_wb")
        s_S = sem("s_S"); s_mx = sem("s_mx"); s_exp = sem("s_exp"); s_P = sem("s_P")
        s_T = sem("s_T"); s_Te = sem("s_Te"); s_Of = sem("s_Of"); s_Oe = sem("s_Oe"); s_ot = sem("s_ot"); s_ote = sem("s_ote"); s_y = sem("s_y"); s_ye = sem("s_ye")
        s_qk = sem("s_qk"); s_qke = sem("s_qke"); s_ke = sem("s_ke"); s_G = sem("s_G"); s_Ge = sem("s_Ge")
        s_V = sem("s_V"); s_Ve = sem("s_Ve"); s_st = sem("s_st"); s_mv = sem("s_mv"); s_var = sem("s_var")
        s_rstd = sem("s_rstd"); s_h = sem("s_h"); s_ctx = [sem("s_ctx0"), sem("s_ctx1")]
        s_rs = sem("s_rs")
        s_gd = [sem("s_gd0"), sem("s_gd1")]
        s_x1 = sem("s_x1")
        s_out = sem("s_out")

        NEST, REL = Stage(sem, "nest", 2, 16, True), Stage(sem, "rel", 4, 8, False)
        Eflat = pad[:]
        F, R, E = ([Eflat[:, 1024 * (2 * j + i):1024 * (2 * j + i) + 1024].rearrange("p (c m) -> p c m", c=NC)
                    for i in range(2)] for j in range(3))
        Kb = KR[:, 0, :].rearrange("p (c m) -> p c m", c=NC)

        def unit(i, shape):
            v = Eflat[:, 2048 * i:2048 * i + shape[0] * shape[1]]
            return v.rearrange("p (a m) -> p a m", a=shape[0])

        for st in (NEST, REL):
            n = st.name
            heads = 4 * st.NS
            st.KZ = ([Gc[i][:] for i in range(2)] if st.nested else [unit(i, [heads, 128]) for i in range(2)])
            st.W = [sb(f"W{x}_{n}", [128, 128]) for x in "qkvo"]
            st.bq, st.bk = sb(f"bq_{n}", [128, 1]), sb(f"bk_{n}", [128, 1])
            st.bv, st.bo = sb(f"bv_{n}", [128, 128]), sb(f"bo_{n}", [128, 128])
            st.hm = sb(f"hm_{n}", [128, heads])
        BM = [unit(2 + i, [NH, 128]) for i in range(2)]
        bias1 = unit(4, [NH, 128])
        mneg = unit(5, [B, 128])
        mrow = unit(6, [B, 128])
        valid = sb("valid", [128, B])
        P4 = [kZ[1][:, 2 * i:2 * i + 2, :, :].rearrange("p a b k -> p (a b) k") for i in range(4)]
        mv2 = sb("mv2", [128, 2, 2])
        st62 = sb("st62", [128, 2, 6])
        rstd2 = sb("rstd2", [128, 2])
        q2, k2, V2, h1 = ([valM[:, 2 * i + j, :] for j in range(2)] for i in range(4))
        O2, OT2, tmpx, tmpy = (valM[:, 8 + i, :] for i in range(4))
        gob = valM[:, 12, :]
        gwide = valM[:, 13, :]
        nwT = sb("nwT", [128, 128]); nbT = sb("nbT", [128, 128])
        nwb = sb("nwb", [128, 2])
        wideT = sb("wideT", [128, 128])
        wide = sb("wide", [128, 128])

        xg = nc.dram_tensor("slot_rows", (SLOTS, ROW), F32).ap()
        blank = sb("blank", [128, ROW])
        Rows = Eflat[:, 6 * 2048:6 * 2048 + B * ROW].rearrange("p (n r) -> p n r", n=B)
        We, Ve, Wout = G[0], G[1], kZ[0]

        def tile(i):
            return KR[:, i // 8, 128 * (i % 8):128 * (i % 8) + 128]

        scores = tile(0)[:, 0:16].rearrange("p (n e) -> p n e", n=2)
        top8 = tile(0)[:, 16:32].rearrange("p (n e) -> p n e", n=2)
        idx8 = tile(0)[:, 32:48].rearrange("p (n e) -> p n e", n=2).bitcast(U32)
        chosen = tile(0)[:, 64:96].rearrange("p (n k e) -> p n k e", n=2, k=2)
        picked = tile(0)[:, 96:128].rearrange("p (n k e) -> p n k e", n=2, k=2)
        cnt = tile(1)[:, 0:16].rearrange("p (n e) -> p n e", n=2)
        pos = tile(1)[:, 16:32].rearrange("p (n e) -> p n e", n=2)
        base = tile(1)[:, 32:40]
        eid, place, full, slot = (tile(2)[:, 4 * i:4 * i + 4].rearrange("p (n k) -> p n k", n=2) for i in range(4))
        st_r = tile(3)[:, 0:12].rearrange("p (n s) -> p n s", n=2)
        mv_r = tile(3)[:, 12:16].rearrange("p (n s) -> p n s", n=2)
        rstd_r = tile(3)[:, 16:18]
        spare_r = tile(3)[:, 18:22]
        slot_u = tile(4)[:, 0:32].rearrange("p (n k) -> p n k", k=2).bitcast(U32)
        hN = KR[:, 1, 0:256].rearrange("p (n d) -> p n d", n=2)
        hR = KR[:, 1, 256:512].rearrange("p (n d) -> p n d", n=2)
        first, behind, w0, w1, w_slot = (tile(5)[:, 16 * i:16 * i + 16] for i in range(5))
        iota8, rb, rwT = (tile(6)[:, 8 * i:8 * i + 8] for i in range(3))
        token = tile(7)[:, 0:B]
        owner = tile(7)[:, B:2 * B]
        ustrict, ones = valM[:, 14, :], valM[:, 15, :]
        xTs = [Eflat[:, 4096 + 256 * i:4352 + 256 * i] for i in range(2)]
        sil = [Eflat[:, 5120 + 512 * i:5632 + 512 * i] for i in range(2)]
        hid = [Eflat[:, 6144 + 512 * i:6656 + 512 * i] for i in range(2)]
        Ys = [Eflat[:, 7168 + 256 * i:7424 + 256 * i] for i in range(2)]
        Xs = Eflat[:, 8192:8192 + B * ROW].rearrange("p (t r) -> p t r", t=SLOTS // 128)
        m_ce = sem("m_ce"); m_co = sem("m_co"); m_pos = sem("m_pos"); m_row = sem("m_row"); m_var = sem("m_var")
        m_w = sem("m_w"); m_st = sem("m_st"); m_mv = sem("m_mv"); m_rstd = sem("m_rstd"); m_h = sem("m_h")
        m_T = sem("m_T"); m_Te = sem("m_Te"); m_L = sem("m_L"); m_Le = sem("m_Le")
        m_cnt = sem("m_cnt"); m_pre = sem("m_pre"); m_exp = sem("m_exp")
        m_slot = sem("m_slot"); m_fill = sem("m_fill"); m_put = sem("m_put")
        m_xs = [sem(f"m_xs{i}") for i in range(NE)]
        m_xT = sem("m_xT"); m_xTe = sem("m_xTe"); m_ab = sem("m_ab"); m_sil = sem("m_sil"); m_hid = sem("m_hid")
        m_y = sem("m_y"); m_ye = sem("m_ye"); m_add = sem("m_add"); m_ws = sem("m_ws")
        bAB = [(bS[0], bS[1]), (bT[0], bT[1])]
        bXT = [bA, bO]
        bY = [bG, bV]

        GD = 16 * 8

        block = ctx.enter_context(nc.Block())

        def vjob(b, i):
            return 2 + i if isinstance(b, int) and b < 0 else b * 5 + (6 + i)

        def xrow(n):
            return X[:, bass.ds(n, 1), :].rearrange("p a d -> p (a d)")

        def after(st, b, g, par, it):
            return (b, g + 1, par, it) if g < st.NS - 1 else (b + 1, 0, 1 - par, it + par)

        def small_pool(pool, st):
            def std(n, par, s_mv, s_var, s_rstd, mvt, r):
                pool.wait_ge(s_mv, n + 1)
                nc.gpsimd.tensor_tensor(r[:, par:par + 1], mvt[:, par, 1:2], epst[:], ALU.add).then_inc(s_var, 1)
                pool.wait_ge(s_var, n + 1)
                nc.gpsimd.tensor_tensor(r[:, par:par + 1], r[:, par:par + 1], mhalf[:], ALU.pow).then_inc(s_rstd, 1)

            def residual(n, par):
                pool.wait_ge(st.s_tx, n + 1)
                nc.gpsimd.tensor_tensor(tmpx, tmpx, gob, ALU.add).then_inc(st.s_res, 1)
                pool.wait_ge(st.s_res, n * 2 + 1)
                nc.gpsimd.tensor_tensor(xrow(n), xrow(n), tmpx, ALU.add).then_inc(st.s_res, 1)

            def norm_bias(n, par):
                pool.wait_ge(st.s_Ve, st.job_of_h(n) + 1)
                nc.gpsimd.tensor_tensor(hTs[par][:], hTs[par][:], nbT[:], ALU.add).then_inc(st.s_hb, 1)

            def keys(n, par):
                pool.wait_ge(st.s_qke, n + 1)
                if st.nested and isinstance(n, int) and n < 2:
                    pool.wait_ge(s_gd[n], B * GD)
                wait(pool, st.s_S, (n - 1) * st.NS)
                heads = 4 * st.NS
                nc.gpsimd.tensor_tensor(st.KZ[par], k2[par].unsqueeze(1).to_broadcast([128, heads, 128]),
                                        st.hm[:].unsqueeze(2).to_broadcast([128, heads, 128]), ALU.mult).then_inc(st.s_kz, 1)

            def bias(n, par):
                wait(pool, st.s_add, (n - 1) * st.NS)
                nc.gpsimd.tensor_tensor(BM[par], bias1, mneg[:, bass.ds(n, 1), :].to_broadcast([128, NH, 128]),
                                        ALU.add).then_inc(st.s_bm, 1)

            pool.wait_ge(st.s_cst, 1)
            std1 = (st.s_mv, st.s_var, st.s_rstd, mv, rstd)
            if st.nested:
                std2 = (st.s_mv2, st.s_var2, st.s_rstd2, mv2, rstd2)
                for n in range(2):
                    std(n, n, *std1)
                    std(n, n, *std2)
                    residual(n, n)
                std(2, 0, *std1)
                norm_bias(0, 0)
                std(2, 0, *std2)
                norm_bias(1, 1)
                residual(2, 0)
                std(3, 1, *std1)
                std(3, 1, *std2)
                keys(0, 0)
            else:
                for n in range(3):
                    std(n, n % 2, *std1)
                bias(0, 0)
                keys(0, 0)

            def body(b, par, known, it):
                one, two, three, four = (known is None or known + n <= LAST for n in (1, 2, 3, 4))
                if st.nested:
                    if one:
                        keys(b + 1, 1 - par)
                    if three:
                        residual(b + 3, 1 - par)
                    if four:
                        std(b + 4, par, *std1)
                    if two:
                        norm_bias(b + 2, par)
                    if four:
                        std(b + 4, par, *std2)
                else:
                    if one:
                        bias(b + 1, 1 - par)
                        keys(b + 1, 1 - par)
                    if three:
                        std(b + 3, 1 - par, *std1)
                    m_stats, _, _, m_place = route_steps(par, known, it)
                    if m_stats is not None:
                        route_std(pool, m_stats)
                    if m_place is not None:
                        route_scatter(pool, m_place)
            if st.nested:
                over_batches(pool, body, 2)
            else:
                for b in range(B):
                    body(b, b % 2, b, b // 2)

        def small_act(act, st):
            def evict_qk(n, par):
                act.wait_ge(st.s_qk, n + 1)
                scale = D ** -0.5 if st.nested else st.dh ** -0.5
                nc.scalar.activation(q2[par], bA[:, 0:128], ACT.Identity, bias=st.bq[:], scale=scale)
                if not isinstance(n, int) or n >= 2:
                    act.wait_ge(st.s_kz, n - 1)
                nc.scalar.activation(k2[par], bA[:, 128:256], ACT.Identity, bias=st.bk[:]).then_inc(st.s_qke, 1)

            def evict_t(b, g):
                while g < 0:
                    g += st.NS
                    b = b - 1
                u = b * st.NS + g
                act.wait_ge(st.s_T, u + 1)
                wait(act, st.s_Of, u - 1)
                nc.scalar.copy(PT[g % 2][:].rearrange("p j q -> p (j q)"), bP2[g % 2][:, :]).then_inc(st.s_Te, 1)

            def gated(n, par):
                act.wait_ge(st.s_h1, n + 1)
                wait(act, st.s_res, n * 2)
                nc.scalar.activation(tmpx, h1[par], ACT.Identity, scale=gates[:, 1:2]).then_inc(st.s_tx, 1)

            def start(step):
                if st.nested and step == 3:
                    act.wait_ge(st.s_cst, 1)
                    gated(0, 0)
                elif st.nested and step == 4:
                    gated(1, 1)
                elif st.nested and step == 6:
                    gated(2, 0)
                elif st.nested and step == 7:
                    evict_qk(0, 0)

            def body(b, par, known, it):
                for g in range(st.NS):
                    u = b * st.NS + g
                    at = st.at(g, par)
                    act.wait_ge(st.s_mx, u + 1)
                    if st.nested:
                        wait(act, st.s_T, u - 3)
                    wait(act, st.s_rs, u - 3)
                    for j in range(4):
                        src = bS[g % 2][:, 128 * j:128 * j + 128] if st.nested else P4[at][:, j, :]
                        last = nc.scalar.activation(P4[at][:, j, :], src, ACT.Exp, bias=nmx[:, g % 2, j:j + 1],
                                                    accum_out=sums[:, st.at(g, par), j:j + 1])
                    last.then_inc(st.s_exp, 1)
                    if not (known == 0 and g == 0):
                        evict_t(b, g - 1)
                    if not st.nested and g == 0 and (known is None or known < LAST):
                        evict_qk(b + 1, 1 - par)
                    m_score = None if st.nested else route_steps(par, known, it)[1]
                    if m_score is not None and g == 1:
                        route_row(act, m_score)
                    if st.nested and g == 0 and (known is None or known + 3 <= LAST):
                        gated(b + 3, 1 - par)
                    if st.nested and g == 1 and (known is None or known + 2 <= LAST):
                        evict_qk(b + 2, par)
            def run(follow=None):
                if st.nested:
                    evict_qk(1, 1)
                else:
                    act.wait_ge(st.s_cst, 1)
                    evict_qk(0, 0)
                over_batches(act, body, 2, 1 if st.nested else 3)
                evict_t(B, -1)
            return start, run

        def small_dve(dve, st, link, follow=None):
            V_ = nc.vector
            NS = st.NS
            def constants():
                dve.wait_ge(st.s_w, 16 * (12 if st.nested else 11))
                link(V_.tensor_scalar(st.bq[:], st.bq[:], D ** -0.5 if st.nested else st.dh ** -0.5, None, ALU.mult))
                if st.nested:
                    link(V_.tensor_scalar(nwT[:], wideT[:], nwb[:, 0:1], None, ALU.mult))
                    link(V_.tensor_scalar(nbT[:], wideT[:], nwb[:, 1:2], None, ALU.mult))
                    link(V_.tensor_scalar(gwide, wide[:], gates[:, 1:2], None, ALU.mult))
                    V_.tensor_tensor(gob, gwide, st.bo[:], ALU.mult).then_inc(st.s_cst, 1)
                else:
                    link(V_.tensor_scalar(st.bo[:], st.bo[:], gates[:, 2:3], None, ALU.mult))
                    link(V_.tensor_scalar(mneg, mrow.bitcast(I32), 0, NEG, ALU.is_equal, ALU.mult))
                    link(V_.tensor_reduce(valid[:], mneg, AX.X, ALU.max))
                    V_.tensor_scalar(valid[:], valid[:], 0.5 * NEG, None, ALU.is_gt).then_inc(st.s_cst, 1)
                    if stop >= 4:
                        dve.wait_ge(m_w, 16 * 10)
                        V_.tensor_copy(Rows[:, :, D + 2].bitcast(U32), token.bitcast(U32))
                        V_.memset(base, 0.0)
                        link(V_.memset(ones, 1.0))

            def stats(n, par, src, six, out2, s_st, s_mv):
                V_.bn_stats(six[:, par, :], src).then_inc(s_st, 1)
                dve.wait_ge(s_st, n + 1)
                V_.memset(spare[:, par:par + 1], 0.0)
                V_.bn_aggr(out2[:, par, :], six[:, par, :]).then_inc(s_mv, 1)

            def stats1(n, par):
                stats(n, par, xrow(n), st6, mv, st.s_st, st.s_mv)

            def norm1(n, par, dst, s_done):
                dve.wait_ge(st.s_rstd, n + 1)
                V_.tensor_scalar(dst, xrow(n), mv[:, par, 0:1], rstd[:, par:par + 1], ALU.subtract,
                                 ALU.mult).then_inc(s_done, 1)

            def inner_stats(n, par):
                if not isinstance(n, int) or n >= 2:
                    dve.wait_ge(st.s_tx, n - 1)
                norm1(n, par, h1[par], st.s_h1)
                dve.wait_ge(st.s_h1, n + 1)
                stats(n, par, h1[par], st62, mv2, st.s_st2, st.s_mv2)

            def inner_norm(n, par):
                dve.wait_ge(st.s_rstd2, n + 1)
                if not isinstance(n, int) or n >= 2:
                    dve.wait_ge(st.s_V, st.job_of_h(n - 2) + 1)
                V_.tensor_scalar(hS[par][:], h1[par], mv2[:, par, 0:1], rstd2[:, par:par + 1], ALU.subtract,
                                 ALU.mult).then_inc(st.s_h, 1)

            def evict_h(n, par, job):
                dve.wait_ge(st.s_V, job + 1)
                if not st.nested:
                    V_.tensor_copy(hTs[par][:], bV[:, 0:128]).then_inc(st.s_Ve, 1)
                    return
                V_.tensor_tensor(hTs[par][:], bV[:, 0:128], nwT[:], ALU.mult).then_inc(st.s_Ve, 1)

            def evict_v(par, job):
                dve.wait_ge(st.s_V, job + 1)
                V_.tensor_tensor(V2[par], bV[:, 0:128], st.bv[:], ALU.add).then_inc(st.s_Ve, 1)

            def evict_o(b, g, par):
                while g < 0:
                    g += NS
                    b = b - 1
                    par = 1 - par
                at = st.at(g, par)
                dve.wait_ge(st.s_Of, b * NS + (g + 1))
                dve.wait_ge(st.s_rs, b * NS + (g + 1))
                w = 4 * st.dh
                V_.tensor_tensor(O2[:, w * g:w * g + w].rearrange("p (j d) -> p j d", j=4),
                                 bO[:, 0:w].rearrange("p (j d) -> p j d", j=4),
                                 rs[:, at, :].unsqueeze(2).to_broadcast([128, 4, st.dh]), ALU.mult).then_inc(st.s_Oe, 1)

            def evict_ot(n):
                dve.wait_ge(st.s_ot, n + 1)
                V_.tensor_copy(OT2, bY1[:, 0:128]).then_inc(st.s_ote, 1)

            def evict_y(n):
                dve.wait_ge(st.s_y, n + 1)
                if st.nested:
                    if not isinstance(n, int) or n >= 1:
                        dve.wait_ge(st.s_x, n)
                    V_.tensor_tensor(tmpy, bY1[:, 0:128], gwide, ALU.mult).then_inc(st.s_ye, 1)
                    dve.wait_ge(st.s_res, n * 2 + 2)
                    dve.wait_ge(st.s_ye, n + 1)
                    V_.tensor_tensor(xrow(n), xrow(n), tmpy, ALU.add).then_inc(st.s_x, 1)
                else:
                    V_.scalar_tensor_tensor(xrow(n), bY1[:, 0:128], gates[:, 2:3], xrow(n), ALU.mult,
                                            ALU.add).then_inc(st.s_ye, 1)
                    dve.wait_ge(st.s_ye, n + 1)
                    V_.tensor_tensor(xrow(n), xrow(n), st.bo[:], ALU.add).then_inc(st.s_x, 1)

            def invert(b, g, par):
                while g < 0:
                    g += NS
                    b = b - 1
                    par = 1 - par
                at = st.at(g, par)
                dve.wait_ge(st.s_exp, b * NS + (g + 1))
                V_.reciprocal(rs[:, at, :], sums[:, at, :]).then_inc(st.s_rsr, 1)
                dve.wait_ge(st.s_rsr, b * NS + (g + 1))
                if st.nested:
                    reach = wide[:].rearrange("p (h d) -> p h d", d=st.dh)[:, 4 * g:4 * g + 4, 0]
                    V_.tensor_tensor(rs[:, at, :], rs[:, at, :], reach, ALU.mult).then_inc(st.s_rs, 1)
                else:
                    V_.tensor_tensor(rs[:, at, :], rs[:, at, :], valid[:, bass.ds(b, 1)].to_broadcast([128, 4]),
                                     ALU.mult).then_inc(st.s_rs, 1)

            def start(step):
                if st.nested:
                    if step == 0:
                        constants()
                    elif step == 1:
                        stats1(0, 0)
                    elif step == 2:
                        inner_stats(0, 0)
                        stats1(1, 1)
                    elif step == 3:
                        inner_norm(0, 0)
                        inner_stats(1, 1)
                    elif step == 4:
                        inner_norm(1, 1)
                        stats1(2, 0)
                    elif step == 5:
                        evict_h(0, 0, 0)
                        inner_stats(2, 0)
                    elif step == 6:
                        evict_h(1, 1, 1)
                        inner_norm(2, 0)
                        stats1(3, 1)
                    elif step == 7:
                        inner_stats(3, 1)
                elif step == 2:
                    constants()
                elif step == 4:
                    stats1(0, 0)
                    stats1(1, 1)
                elif step == 6:
                    norm1(0, 0, hS[0][:], st.s_h)
                    norm1(1, 1, hS[1][:], st.s_h)
                elif step == 7:
                    stats1(2, 0)
                elif step == 8:
                    evict_h(0, 0, 0)
                elif step == 9:
                    evict_h(1, 1, 1)

            def top(b, g, par):
                u = b * NS + g
                dve.wait_ge(st.s_S, u + 1)
                src = bS[g % 2][:, :].rearrange("p (j k) -> p j k", j=4)
                if not st.nested:
                    if g == 0:
                        dve.wait_ge(st.s_bm, b + 1)
                    wait(dve, st.s_T, u - 3)
                    V_.tensor_tensor(P4[g][:], src, BM[par][:, 4 * g:4 * g + 4, :], ALU.add).then_inc(st.s_add, 1)
                    dve.wait_ge(st.s_add, u + 1)
                    src = P4[g][:]
                wait(dve, st.s_exp, u - 1)
                V_.tensor_reduce(nmx[:, g % 2, :], src, AX.X, ALU.max, negate=True).then_inc(st.s_mx, 1)

            def body(b, par, known, it):
                first = known == 0
                one, two, three, four = (known is None or known + n <= LAST for n in (1, 2, 3, 4))
                if st.nested:
                    if known not in (0, 1):
                        evict_o(b, -3, par)
                    top(b, 1, par)
                    if not first:
                        invert(b, -1, par)
                    if known not in (0, 1):
                        evict_ot(b - 2)
                    if three:
                        inner_norm(b + 3, 1 - par)
                    if four:
                        stats1(b + 4, par)
                    if known is not None and known >= B - 4 and follow is not None:
                        follow(2 * (known - (B - 4)))
                    if not first:
                        evict_o(b, -2, par)
                    if two:
                        evict_h(b + 2, par, st.job_of_h(b + 2))
                    if one:
                        top(b + 1, 0, 1 - par)
                    invert(b, 0, par)
                    if known not in (0, 1):
                        evict_y(b - 2)
                    if four:
                        inner_stats(b + 4, par)
                    if one:
                        evict_v(1 - par, st.job_of_v(b + 1))
                    if known is not None and known >= B - 4 and follow is not None:
                        follow(2 * (known - (B - 4)) + 1)
                    return
                m_stats, m_score, m_choose, m_place = route_steps(par, known, it)
                for g in range(NS):
                    if g == 3 and not first:
                        evict_ot(b - 1)
                    if not (first and g < 3):
                        evict_o(b, g - 3, par)
                    if one or g < 3:
                        top(*after(st, b, g, par, it)[:3])
                    if g == 2 and one:
                        evict_v(1 - par, st.job_of_v(b + 1))
                    if g == 3 and two:
                        evict_h(b + 2, par, st.job_of_h(b + 2))
                    if not (first and g == 0):
                        invert(b, g - 1, par)
                    if g == 0 and two:
                        norm1(b + 2, par, hS[par][:], st.s_h)
                    if g == 1 and three:
                        stats1(b + 3, 1 - par)
                    if m_stats is not None and g in (1, 2):
                        route_stats(dve, m_stats, g - 1)
                    if m_score is not None and g == 0:
                        route_norm(dve, m_score)
                    if m_score is not None and g == 2:
                        route_evict(dve, m_score)
                    if m_choose is not None and g == 0:
                        route_choose(dve, m_choose)
                    if m_place is not None and g == 0:
                        route_count(dve, m_place)
                    if m_place is not None and g == 1:
                        route_slots(dve, m_place)
                    if g == 3 and not first:
                        evict_y(b - 1)
                    if m_score is not None and g == 3:
                        route_scores(dve, m_score)

            def run():
                evict_v(0, 2)
                top(0, 0, 0)
                over_batches(dve, body, 2, 1 if st.nested else 3)
                invert(B, -1, 0)
                if NS == 4:
                    evict_o(B, -3, 0)
                    if stop >= 4:
                        route_norm(dve, 6)
                        route_count(dve, 5)
                        route_slots(dve, 5)
                    evict_o(B, -2, 0)
                    if stop >= 4:
                        route_evict(dve, 6)
                    evict_o(B, -1, 0)
                    evict_ot(LAST)
                    if stop >= 4:
                        route_scores(dve, 6)
                        route_choose(dve, 6)
                    evict_y(LAST)
                else:
                    evict_o(B, -3, 0)
                    if follow is not None:
                        follow(8)
                    evict_ot(B - 2)
                    evict_o(B, -2, 0)
                    if follow is not None:
                        follow(9)
                    evict_o(B, -1, 0)
                    evict_y(B - 2)
                    evict_ot(LAST)
                    evict_y(LAST)
            return start, run

        def small_pe(pe, st, before, follow=None):
            NS = st.NS

            def mm(o, l, r, start=True, stop=True):
                return nc.tensor.matmul(o, l, r, start=start, stop=stop)

            def job_h(n, par, job):
                pe.wait_ge(st.s_h, n + 1)
                wait(pe, st.s_Ve, job)
                nc.tensor.transpose(bV[:, 0:128], hS[par][:], ident[:]).then_inc(st.s_V, 1)

            def source(par):
                return hTs[par] if st.nested else ctxS[par]

            def job_v(n, par, job):
                wait(pe, st.s_Ve, job)
                mm(bV[:, 0:128], source(par)[:], st.W[2][:]).then_inc(st.s_V, 1)

            def job_qk(n, par, hjob, half):
                if st.nested:
                    pe.wait_ge(st.s_hb, n + 1)
                else:
                    pe.wait_ge(st.s_Ve, hjob + 1)
                if not st.nested:
                    pe.wait_ge(st.s_ctx[par], (half + 1) * 16)
                wait(pe, st.s_qke, n)
                mm(bA[:, 0:128], st.W[0][:], hTs[par][:])
                mm(bA[:, 128:256], st.W[1][:], source(par)[:]).then_inc(st.s_qk, 1)

            def job_s(b, g, par):
                u = b * NS + g
                if g == 0:
                    pe.wait_ge(st.s_kz, b + 1)
                wait(pe, st.s_exp if st.nested else st.s_add, u - 1)
                mm(bS[g % 2][:, :], q2[par], st.KZ[par][:, 4 * g:4 * g + 4, :].rearrange("p h k -> p (h k)")
                   ).then_inc(st.s_S, 1)

            def job_t(b, g, par):
                while g < 0:
                    g += NS
                    b = b - 1
                    par = 1 - par
                u = b * NS + g
                pe.wait_ge(st.s_exp, u + 1)
                wait(pe, st.s_Te, u - 1)
                for j in range(4):
                    last = nc.tensor.transpose(bP2[g % 2][:, 128 * j:128 * j + 128], P4[st.at(g, par)][:, j, :], ident[:])
                last.then_inc(st.s_T, 1)

            def job_pv(b, g, par):
                while g < 0:
                    g += NS
                    b = b - 1
                    par = 1 - par
                pe.wait_ge(st.s_Te, b * NS + (g + 1))
                wait(pe, st.s_Oe, b * NS + g)
                if g == 0:
                    pe.wait_ge(st.s_Ve, st.job_of_v(b) + 1)
                for j in range(4):
                    h = 4 * g + j
                    last = mm(bO[:, st.dh * j:st.dh * j + st.dh], PT[g % 2][:, j, :], V2[par][:, st.dh * h:st.dh * h + st.dh])
                last.then_inc(st.s_Of, 1)

            def job_ot(n):
                pe.wait_ge(st.s_Oe, n * NS + NS)
                wait(pe, st.s_ye, n)
                nc.tensor.transpose(bY1[:, 0:128], O2, ident[:]).then_inc(st.s_ot, 1)

            def job_y(n):
                pe.wait_ge(st.s_ote, n + 1)
                mm(bY1[:, 0:128], OT2, st.W[3][:]).then_inc(st.s_y, 1)

            def start(step):
                if st.nested:
                    if step == 4:
                        pe.wait_ge(s_Ve, vjob(B - 3, 4) + 5)
                        pe.wait_ge(s_Ge, 4 * B)
                        job_h(0, 0, 0)
                    elif step == 5:
                        job_h(1, 1, 1)
                    elif step == 6:
                        pe.wait_ge(s_ke, 4 * B)
                        job_qk(0, 0, 0, 0)
                    elif step == 7:
                        job_v(0, 0, 2)
                        job_qk(1, 1, 1, 0)
                elif step == 7:
                    pe.wait_ge(NEST.s_Ve, 2 * B)
                    pe.wait_ge(NEST.s_qke, B)
                    job_h(0, 0, 0)
                elif step == 8:
                    job_h(1, 1, 1)
                elif step == 9:
                    job_qk(0, 0, 0, 0)
                    job_v(0, 0, 2)

            def body(b, par, known, it):
                first = known == 0
                one, two = (known is None or known + n <= LAST for n in (1, 2))
                if st.nested:
                    job_s(b, 1, par)
                    if not first:
                        job_t(b, -1, par)
                    if known not in (0, 1):
                        job_ot(b - 2)
                    if not first:
                        job_pv(b, -2, par)
                    if two:
                        job_h(b + 2, par, st.job_of_h(b + 2))
                    if known is not None and known >= B - 4 and follow is not None:
                        follow(2 * (known - (B - 4)))
                    if one:
                        job_s(b + 1, 0, 1 - par)
                    job_t(b, 0, par)
                    if known not in (0, 1):
                        job_y(b - 2)
                    if not first:
                        job_pv(b, -1, par)
                    if one:
                        job_v(b + 1, 1 - par, st.job_of_v(b + 1))
                    if two:
                        job_qk(b + 2, par, st.job_of_h(b + 2), 0)
                    if known is not None and known >= B - 4 and follow is not None:
                        follow(2 * (known - (B - 4)) + 1)
                    return
                _, m_score, m_choose, m_place = route_steps(par, known, it)
                for g in range(NS):
                    if one or g < 3:
                        job_s(*after(st, b, g, par, it)[:3])
                    if not (first and g == 0):
                        job_t(b, g - 1, par)
                    if g == 0 and m_choose is not None:
                        pe.wait_ge(m_Le, m_choose + 1)
                    if m_score is not None and g == 3:
                        route_logits(pe, m_score)
                    if g == 0 and one:
                        job_qk(b + 1, 1 - par, 1 if first else st.job_of_h(b + 1), it + par)
                    if g == 3 and not first:
                        job_y(b - 1)
                    if not (first and g < 2):
                        job_pv(b, g - 2, par)
                    if m_score is not None and g == 1:
                        route_transpose(pe, m_score, b + 2)
                    if g == 2 and not first:
                        job_ot(b - 1)
                    if m_place is not None and g == 1:
                        pe.wait_ge(m_pos, m_place + 1)
                    if g == 1 and one:
                        job_v(b + 1, 1 - par, st.job_of_v(b + 1))
                    if g == 2 and two:
                        job_h(b + 2, par, st.job_of_h(b + 2))
                    if m_choose is not None and g == 3:
                        route_prefix(pe, m_choose, st.job_of_h(b + 2) + 1 if two else 2 * B)
            def run():
                job_s(0, 0, 0)
                pe.wait_ge(before, B)
                over_batches(pe, body, 2, 1 if st.nested else 3)
                job_t(B, -1, 0)
                if NS == 2:
                    job_ot(B - 2)
                    if follow is not None:
                        follow(8)
                job_pv(B, -2, 0)
                job_pv(B, -1, 0)
                if NS == 2:
                    job_y(B - 2)
                    if follow is not None:
                        follow(9)
                if NS == 4 and stop >= 4:
                    route_transpose(pe, 6, B)
                    route_logits(pe, 6)
                job_ot(LAST)
                job_y(LAST)
            return start, run

        def route_steps(par, known, it):
            def due(since, m):
                return m if stop >= 4 and par == since % 2 and (known is None or known >= since) else None
            return due(3, it - 1), due(4, it - 2), due(5, it - 2), due(6, it - 3)

        def rows(m):
            return bass.ds(m * 2, 2)

        def route_stats(dve, m, j):
            nc.vector.bn_stats(st_r[:, j, :], xrow(m * 2 + j)).then_inc(m_st, 1)
            dve.wait_ge(m_st, m * 2 + (j + 1))
            nc.vector.memset(spare_r[:, j:j + 1], 0.0)
            nc.vector.bn_aggr(mv_r[:, j, :], st_r[:, j, :]).then_inc(m_mv, 1)

        def route_norm(dve, m):
            dve.wait_ge(m_rstd, m + 1)
            wait(dve, m_row, m)
            for j in range(2):
                nc.vector.tensor_scalar(hN[:, j, :], xrow(m * 2 + j), mv_r[:, j, 0:1], rstd_r[:, j:j + 1], ALU.subtract,
                                        ALU.mult).then_inc(m_h, 1)

        def route_evict(dve, m):
            dve.wait_ge(m_T, m + 1)
            nc.vector.tensor_copy(hR.rearrange("p n d -> p (n d)"), bA[:, 0:256]).then_inc(m_Te, 1)

        def route_scores(dve, m):
            dve.wait_ge(m_L, m + 1)
            nc.vector.tensor_tensor(scores, bA[:, 0:16].rearrange("p (n e) -> p n e", n=2),
                                    rb.unsqueeze(1).to_broadcast([128, 2, NE]), ALU.add).then_inc(m_Le, 1)

        def route_choose(dve, m):
            V_ = nc.vector

            def then(ins, i):
                ins.then_inc(m_ce, 1)
                dve.wait_ge(m_ce, m * 4 + (i + 1))
            dve.wait_ge(m_Le, m + 1)
            V_.memset(spare_r[:, 2:3], 0.0)
            V_.max(top8[:, 0, :], scores[:, 0, :])
            then(V_.max(top8[:, 1, :], scores[:, 1, :]), 0)
            V_.memset(spare_r[:, 3:4], 0.0)
            V_.max_index(idx8[:, 0, :], top8[:, 0, :], scores[:, 0, :])
            then(V_.max_index(idx8[:, 1, :], top8[:, 1, :], scores[:, 1, :]), 1)
            then(V_.tensor_copy(eid, idx8[:, :, 0:2]), 2)
            V_.tensor_tensor(Rows[:, rows(m), D], top8[:, :, 1], top8[:, :, 0], ALU.subtract)
            V_.tensor_copy(Rows[:, rows(m), D + 1], eid[:, :, 0])
            then(V_.tensor_tensor(chosen, eid.unsqueeze(3).to_broadcast([128, 2, 2, NE]),
                                  iota8.unsqueeze(1).unsqueeze(1).to_broadcast([128, 2, 2, NE]), ALU.is_equal), 3)
            V_.tensor_tensor(cnt, chosen[:, :, 0, :], chosen[:, :, 1, :], ALU.add).then_inc(m_cnt, 1)

        def route_count(dve, m):
            V_ = nc.vector

            def then(ins, i):
                ins.then_inc(m_co, 1)
                dve.wait_ge(m_co, m * 6 + (i + 1))
            dve.wait_ge(m_pre, m + 1)
            then(V_.tensor_tensor(pos, bV[:, 0:16].rearrange("p (n e) -> p n e", n=2),
                                  base.unsqueeze(1).to_broadcast([128, 2, NE]), ALU.add), 0)
            V_.tensor_tensor(base, base, bV[:, 16:24], ALU.add).then_inc(m_pos, 1)

        def route_slots(dve, m):
            V_ = nc.vector

            def then(ins, i):
                ins.then_inc(m_co, 1)
                dve.wait_ge(m_co, m * 6 + (i + 1))
            then(V_.tensor_tensor(picked, chosen, pos.unsqueeze(2).to_broadcast([128, 2, 2, NE]), ALU.mult), 1)
            then(V_.tensor_reduce(place, picked, AX.X, ALU.add), 2)
            then(V_.tensor_scalar(full, place, float(CAP), None, ALU.is_ge), 3)
            then(V_.scalar_tensor_tensor(slot, eid, float(CAP), place, ALU.mult, ALU.add), 4)
            then(V_.scalar_tensor_tensor(slot, full, float(16 * SLOTS), slot, ALU.mult, ALU.add), 5)
            V_.tensor_copy(slot_u[:, rows(m), :], slot).then_inc(m_slot, 1)

        def route_std(pool, m):
            pool.wait_ge(m_mv, m * 2 + 2)
            nc.gpsimd.tensor_tensor(rstd_r, mv_r[:, :, 1], epst[:].to_broadcast([128, 2]), ALU.add).then_inc(m_var, 1)
            pool.wait_ge(m_var, m + 1)
            nc.gpsimd.tensor_tensor(rstd_r, rstd_r, mhalf[:].to_broadcast([128, 2]), ALU.pow).then_inc(m_rstd, 1)

        def route_scatter(pool, m):
            pool.wait_ge(m_slot, m + 1)
            pool.wait_ge(m_row, m + 1)
            if m == 0:
                pool.wait_ge(m_fill, 16)
            for n in (2 * m, 2 * m + 1):
                for k in range(2):
                    nc.gpsimd.indirect_dma_start(
                        out=xg, out_offset=bass.IndirectOffsetOnAxis(ap=slot_u[:, n, k:k + 1], axis=0),
                        in_=Rows[:, n, :], in_offset=None, bounds_check=SLOTS - 1, oob_is_err=False).then_inc(m_put, 16)

        def route_row(act, m):
            act.wait_ge(m_h, m * 2 + 2)
            nc.scalar.copy(Rows[:, rows(m), 0:D], hN).then_inc(m_row, 1)

        def route_transpose(pe, m, qk):
            pe.wait_ge(m_h, m * 2 + 2)
            pe.wait_ge(REL.s_qke, qk)
            wait(pe, m_Le, m)
            nc.tensor.transpose(bA[:, 0:128], hN[:, 0, :], ident[:])
            nc.tensor.transpose(bA[:, 128:256], hN[:, 1, :], ident[:]).then_inc(m_T, 1)

        def route_logits(pe, m):
            pe.wait_ge(m_Te, m + 1)
            nc.tensor.matmul(bA[:, 0:8], hR[:, 0, :], rwT, start=True, stop=True)
            nc.tensor.matmul(bA[:, 8:16], hR[:, 1, :], rwT, start=True, stop=True).then_inc(m_L, 1)

        def route_prefix(pe, m, jobs):
            pe.wait_ge(m_cnt, m + 1)
            pe.wait_ge(REL.s_Ve, jobs)
            def mm(at, l, j, start=True, stop=True):
                return nc.tensor.matmul(bV[:, 8 * at:8 * at + 8], l, cnt[:, j, :], start=start, stop=stop)
            mm(0, ustrict, 0)
            mm(1, ustrict, 1, stop=False)
            mm(1, ones, 0, start=False)
            mm(2, ones, 0, stop=False)
            mm(2, ones, 1, start=False).then_inc(m_pre, 1)

        def experts_sp(sp):
            sp.wait_ge(REL.s_x, B)
            sp.dma_start(out.rearrange("b t d -> t b d"), X[:]).then_inc(s_out, 16)
            sp.wait_ge(m_put, 2 * B * 16)
            for e in range(NE):
                sp.dma_start(Xs[:, 2 * e:2 * e + 2, :],
                             xg[CAP * e:CAP * e + CAP, :].rearrange("(t p) d -> p t d", p=128)).then_inc(m_xs[e], 16)

        def experts_pool(pool):
            route_scatter(pool, 5)
            route_std(pool, 7)
            route_scatter(pool, 6)
            route_scatter(pool, 7)
            pool.wait_ge(s_out, 16)
            tokens = out.rearrange("b t d -> (b t) d")
            for e in range(NE):
                pool.wait_ge(m_ye, e + 1)
                wait(pool, m_add, 32 * e)
                for t in range(2):
                    nc.gpsimd.indirect_dma_start(
                        out=tokens, out_offset=bass.IndirectOffsetOnAxis(ap=Xs[:, 2 * e + t, D + 2:D + 3].bitcast(U32), axis=0),
                        in_=Ys[e % 2][:, 128 * t:128 * t + 128], in_offset=None, bounds_check=B * S - 1, oob_is_err=False,
                        compute_op=ALU.add).then_inc(m_add, 16)
            pool.wait_ge(m_add, 32 * NE)

        def experts_act(act):
            route_row(act, 6)
            route_row(act, 7)
            for e in range(NE):
                act.wait_ge(m_xs[e], 16)
            nc.scalar.activation(behind, Xs[:, :, D], ACT.Exp).then_inc(m_exp, 1)
            for e in range(NE):
                act.wait_ge(m_ab, e + 1)
                wait(act, m_hid, e - 1)
                nc.scalar.activation(sil[e % 2], bAB[e % 2][1][:, :], ACT.Silu).then_inc(m_sil, 1)
                if e >= 1:
                    evict_result(act, e - 1)
            evict_result(act, NE - 1)

        def evict_result(act, e):
            act.wait_ge(m_y, e + 1)
            wait(act, m_add, 32 * (e - 1))
            if e == 0:
                act.wait_ge(m_ws, 1)
            for t in range(2):
                last = nc.scalar.activation(Ys[e % 2][:, 128 * t:128 * t + 128], bY[e % 2][:, 128 * t:128 * t + 128],
                                            ACT.Identity, scale=w_slot[:, 2 * e + t:2 * e + t + 1])
            last.then_inc(m_ye, 1)

        def experts_dve(dve, link):
            V_ = nc.vector
            dve.wait_ge(REL.s_x, B)
            route_stats(dve, 7, 0)
            route_stats(dve, 7, 1)
            route_count(dve, 6)
            route_slots(dve, 6)
            route_norm(dve, 7)
            route_evict(dve, 7)
            route_scores(dve, 7)
            route_choose(dve, 7)
            route_count(dve, 7)
            route_slots(dve, 7)
            dve.wait_ge(m_exp, 1)
            link(V_.tensor_scalar(w0, behind, 1.0, None, ALU.add))
            link(V_.reciprocal(w0, w0))
            link(V_.tensor_scalar(w0, w0, gates[:, 3:4], None, ALU.mult))
            link(V_.tensor_tensor(w1, w0, behind, ALU.mult))
            link(V_.tensor_tensor(first, Xs[:, :, D + 1], owner, ALU.is_equal))
            link(V_.tensor_tensor(w_slot, w0, w1, ALU.subtract))
            link(V_.tensor_tensor(w_slot, w_slot, first, ALU.mult))
            V_.tensor_tensor(w_slot, w_slot, w1, ALU.add).then_inc(m_ws, 1)
            for e in range(NE + 1):
                if e < NE:
                    dve.wait_ge(m_xT, e + 1)
                    V_.tensor_copy(xTs[e % 2], bXT[e % 2][:, 0:256]).then_inc(m_xTe, 1)
                if e >= 1:
                    dve.wait_ge(m_sil, e)
                    wait(dve, m_y, e - 2)
                    V_.tensor_tensor(hid[(e - 1) % 2], bAB[(e - 1) % 2][0][:, :], sil[(e - 1) % 2],
                                     ALU.mult).then_inc(m_hid, 1)

        def experts_pe(pe):
            def mm(o, l, r, start=True, stop=True):
                return nc.tensor.matmul(o, l, r, start=start, stop=stop)
            pe.wait_ge(m_pos, 6)
            route_prefix(pe, 6, 2 * B)
            route_transpose(pe, 7, B)
            route_logits(pe, 7)
            pe.wait_ge(m_pos, 7)
            route_prefix(pe, 7, 2 * B)

            def result(e):
                pe.wait_ge(m_hid, e + 1)
                wait(pe, m_ye, e - 1)
                for t in range(2):
                    for c in range(2):
                        last = mm(bY[e % 2][:, 128 * t:128 * t + 128], hid[e % 2][:, 256 * c + 128 * t:256 * c + 128 * t + 128],
                                  Wout[:, e, c, :], start=c == 0, stop=c == 1)
                last.then_inc(m_y, 1)

            for e in range(NE):
                pe.wait_ge(m_xs[e], 16)
                wait(pe, m_xTe, e - 1)
                for t in range(2):
                    last = nc.tensor.transpose(bXT[e % 2][:, 128 * t:128 * t + 128], Xs[:, 2 * e + t, 0:D], ident[:])
                last.then_inc(m_xT, 1)
                pe.wait_ge(m_xTe, e + 1)
                wait(pe, m_hid, e - 1)
                for bank, w in zip(bAB[e % 2], (We, Ve)):
                    for c in range(2):
                        last = mm(bank[:, 256 * c:256 * c + 256], w[:, 2 * e + c, :], xTs[e % 2])
                last.then_inc(m_ab, 1)
                if e >= 1:
                    result(e - 1)
            result(NE - 1)

        @block.sync
        def _(sp):
            sp.dma_start(ident[:], A["ident"]).then_inc(s_ld, 16)
            sp.dma_start(graw[:], A["gates"].partition_broadcast(128)).then_inc(s_ld, 16)
            sp.dma_start(pn[:], A["box_pn"]).then_inc(s_ldb, 16)
            sp.dma_start(phase[:], A["phase"]).then_inc(s_ldb, 16)
            for part, s_part in ((slice(0, EARLY), s_ldb), (slice(EARLY, B), s_ldr)):
                sp.dma_start(valM[:, part, :], A["box_row"][0][:, part, :]).then_inc(s_part, 16)
                sp.dma_start(rowM[:, part, :], A["box_row"][1][:, part, :]).then_inc(s_part, 16)
            sp.dma_start(X[:], A["x"].rearrange("b t d -> t b d")).then_inc(s_ldx, 16)
            for dst, name in ((wrep, "wg"), (delta, "delta"), (bgp, "bg"), (WqT, "WqT"), (WkT, "WkT"), (WvT, "WvT"),
                              (WoT, "WoT"), (bq, "bq"), (bk, "bk")):
                sp.dma_start(dst[:], A[name]).then_inc(s_ldw, 16)
            sp.dma_start(bvb[:], A["bv"].partition_broadcast(128)).then_inc(s_ldw, 16)
            sp.dma_start(bob[:], A["bo"].partition_broadcast(128)).then_inc(s_ldw, 16)

            for st in (NEST, REL):
                n = st.name
                for dst, name in zip(st.W + [st.bq, st.bk, st.hm], ("Wq", "Wk", "Wv", "Wo", "bq", "bk", "hm")):
                    sp.dma_start(dst[:], A[f"{name}_{n}"]).then_inc(st.s_w, 16)
                for dst, name in ((st.bv, "bv"), (st.bo, "bo")):
                    sp.dma_start(dst[:], A[f"{name}_{n}"].partition_broadcast(128)).then_inc(st.s_w, 16)
            sp.dma_start(nwb[:], A["norm_wb"]).then_inc(NEST.s_w, 16)
            sp.dma_start(wideT[:], A["wideT"]).then_inc(NEST.s_w, 16)
            sp.dma_start(wide[:], A["wide"]).then_inc(NEST.s_w, 16)

            def load_ctx(n, par, known):
                if known is None or known >= 2:
                    wait(sp, s_V, vjob(n - 3, 3) + 1)
                sp.dma_start(ctxS[par][:], A["ctxT"][:, bass.ds(n, 1) if not isinstance(n, int) else slice(n, n + 1), :]
                             .rearrange("d a t -> d (a t)")).then_inc(s_ctx[par], 16)

            def spread(b1, par, known):
                for hg in range(2):
                    wait(sp, s_Ge, b1 * 4 + (2 * hg + 2))
                    wait(sp, s_P, (b1 - 1) * 4)
                    for h in range(8):
                        sp.dma_start(G[par][:, 8 * hg + h, :],
                                     Gc[hg][NPF * h:NPF * h + NPF, :, :].rearrange("n c m -> n (c m)")).then_inc(s_gd[hg], 16)

            load_ctx(0, 0, 0)
            load_ctx(1, 1, 1)

            def body(b, par, known, it):
                spread(b, par, known)
                if known is None or known + 2 <= LAST:
                    load_ctx(b + 2, par, None if known is None else known + 2)
            over_batches(sp, body)

            sp.wait_ge(s_x1, B)
            sp.wait_ge(s_G, 4 * B)
            sp.dma_start(bias1, A["rel_bias"]).then_inc(REL.s_w, 16)
            sp.dma_start(mrow.bitcast(I32), A["mask"].partition_broadcast(128)).then_inc(REL.s_w, 16)

            if stop >= 4:
                for dst, name in ((We, "W_e"), (Ve, "V_e"), (Wout, "W_out"), (rwT, "rwT"), (ustrict, "ustrict")):
                    sp.dma_start(dst[:] if dst in (We, Ve, Wout) else dst, A[name]).then_inc(m_w, 16)
                sp.dma_start(token.bitcast(I32), A["token"]).then_inc(m_w, 16)
                sp.dma_start(owner, A["owner"].partition_broadcast(128)).then_inc(m_w, 16)
                sp.dma_start(blank[:].bitcast(I32), A["blank"].partition_broadcast(128)).then_inc(m_w, 16)
                for dst, name in ((rb, "rb"), (iota8, "iota8")):
                    sp.dma_start(dst, A[name].partition_broadcast(128)).then_inc(m_w, 16)

                sp.wait_ge(m_w, 16 * 10)
                sp.dma_start(xg.rearrange("(a p) r -> p a r", p=128),
                             blank[:].unsqueeze(1).to_broadcast([128, SLOTS // 128, ROW])).then_inc(m_fill, 16)

            def rel_ctx(n, par, known):
                if known is None or known >= 2:
                    wait(sp, REL.s_V, REL.job_of_v(n - 2) + 1)
                else:
                    sp.wait_ge(s_x1, B)
                sp.dma_start(ctxS[par][:], A["ctxT"][:, bass.ds(n, 1) if not isinstance(n, int) else slice(n, n + 1), :]
                             .rearrange("d a t -> d (a t)")).then_inc(REL.s_ctx[par], 16)
            if stop >= 3:
                rel_ctx(0, 0, 0)
                rel_ctx(1, 1, 1)

                def body(b, par, known, it):
                    if known is None or known + 2 <= LAST:
                        rel_ctx(b + 2, par, None if known is None else known + 2)
                over_batches(sp, body)

            if stop < 4:
                sp.wait_ge([None, s_x1, NEST.s_x, REL.s_x][stop], B)
                sp.dma_start(out.rearrange("b t d -> t b d"), X[:]).then_inc(s_out, 16)
                sp.wait_ge(s_out, 16)
            else:
                experts_sp(sp)

        @block.gpsimd
        def _(pool):
            pool.wait_ge(s_ldb, 64)
            pool.wait_ge(s_lnw, 1)
            pool.wait_ge(s_const, 1)

            def relations(n, par):
                if isinstance(n, int) and n in (2, 3, 4):
                    pool.wait_ge(s_early, n - 1)
                nc.gpsimd.tensor_tensor(F[par], valM[:, bass.ds(n, 1), :].to_broadcast([128, NC, S]),
                                        valN[:, bass.ds(n, 1), :].rearrange("p a c -> p (a c)").unsqueeze(2)
                                        .to_broadcast([128, NC, S]), ALU.subtract).then_inc(s_sub, 1)
                pool.wait_ge(s_sub, n + 1)
                nc.gpsimd.tensor_tensor(F[par], F[par], scl[:, bass.ds(n, 1), :].rearrange("p a c -> p (a c)").unsqueeze(2)
                                        .to_broadcast([128, NC, S]), ALU.mult).then_inc(s_scl, 1)

            def turns(n, par):
                def const(i):
                    return factor[:, i:i + 1].unsqueeze(1).to_broadcast([128, NC, S])
                pool.wait_ge(s_ln, n + 1)
                pool.wait_ge(s_sin, n - 1)
                nc.gpsimd.tensor_tensor(R[par], F[par], const(0), ALU.mult).then_inc(s_turn, 1)
                pool.wait_ge(s_turn, (n - 3) * 5 + 1)
                if isinstance(n, int) and n == 3:
                    pool.wait_ge(s_early, 4)
                else:
                    pool.wait_ge(s_redc, (n - 3) * 2)
                nc.gpsimd.tensor_tensor(Kb, R[par], const(1), ALU.mult).then_inc(s_turn, 1)
                pool.wait_ge(s_turn, (n - 3) * 5 + 2)
                nc.gpsimd.tensor_tensor(Kb, Kb, phase[:, 0:1].unsqueeze(1).to_broadcast([128, NC, S]),
                                        ALU.add).then_inc(s_turn, 1)
                pool.wait_ge(s_turn, (n - 3) * 5 + 3)
                nc.gpsimd.tensor_tensor(Kb, Kb, const(2), ALU.add).then_inc(s_turn, 1)
                pool.wait_ge(s_turn, (n - 3) * 5 + 4)
                nc.gpsimd.tensor_tensor(Kb, Kb, const(2), ALU.subtract).then_inc(s_turn, 1)
            def prep(n, par):
                pool.wait_ge(s_mv, n + 1)
                nc.gpsimd.tensor_tensor(rstd[:, par:par + 1], mv[:, par, 1:2], epst[:], ALU.add).then_inc(s_var, 1)
                pool.wait_ge(s_var, n + 1)
                nc.gpsimd.tensor_tensor(rstd[:, par:par + 1], rstd[:, par:par + 1], mhalf[:], ALU.pow).then_inc(s_rstd, 1)
            for n in range(2):
                relations(n, n)
            for n in range(2):
                prep(n, n)
            for n in range(2, 5):
                if n == EARLY:
                    pool.wait_ge(s_lnw, 2)
                relations(n, n % 2)
                if n == 2:
                    prep(n, 0)

            def body(b, par, known, it):
                if known is None or known + 3 <= LAST:
                    turns(b + 3, 1 - par)
                if known is None or known + 5 <= LAST:
                    relations(b + 5, 1 - par)
                if known is None or known + 3 <= LAST:
                    prep(b + 3, 1 - par)
            over_batches(pool, body, 3)

            if stop >= 2:
                small_pool(pool, NEST)
            if stop >= 3:
                small_pool(pool, REL)
            if stop >= 4:
                experts_pool(pool)

        @block.scalar
        def _(act):
            act.wait_ge(s_ld, 32)
            nc.scalar.activation(gates[:], graw[:], ACT.Tanh).then_inc(s_xb, 1)
            def size_logs(part):
                nc.scalar.activation(valM[64:128, part, :], valM[64:128, part, :], ACT.Ln, bias=one[64:128]).then_inc(s_lnw, 1)
            act.wait_ge(s_row, 1)
            nc.scalar.activation(valN[64:128], valN[64:128], ACT.Ln, bias=one[64:128])
            size_logs(slice(0, EARLY))
            act.wait_ge(s_row, 2)
            size_logs(slice(EARLY, B))

            def logs(n, par):
                act.wait_ge(s_abs, n + 1)
                nc.scalar.activation(F[par][0:64], F[par][0:64], ACT.Ln).then_inc(s_ln, 1)

            def sines(n, par):
                act.wait_ge(s_red, n + 1)
                wait(act, s_G, (n - 1) * 4)
                nc.scalar.activation(E[par], R[par], ACT.Sin, bias=phase[:, 1:2]).then_inc(s_sin, 1)
            def evict_qk(b1, par, g):
                act.wait_ge(s_qk, b1 * 4 + (g + 1))
                for i in range(2):
                    t = 2 * g + i
                    last = nc.scalar.activation(qS[par][:, t, :], bA[:, 128 * i:128 * i + 128], ACT.Identity,
                                                bias=bq[:, t:t + 1], scale=DK ** -0.5)
                last.then_inc(s_qke, 1)

            def evict_g(b1, g):
                hg, half = g // 2, g % 2
                act.wait_ge(s_G, b1 * 4 + (g + 1))
                if not isinstance(b1, int) or b1 > 0:
                    wait(act, s_gd[hg], b1 * GD)
                nc.scalar.activation(Gc[hg][:, 4 * half:4 * half + 4, :].rearrange("p c m -> p (c m)"), bG[:, :],
                                     ACT.Identity, bias=bgp[:, hg:hg + 1]).then_inc(s_Ge, 1)

            logs(0, 0)
            logs(1, 1)
            sines(0, 0)
            act.wait_ge(s_wb, 1)
            for g in range(4):
                evict_g(0, g)
                evict_qk(0, 0, g)
                if g == 1:
                    sines(1, 1)
                    logs(2, 0)
                elif g == 2:
                    logs(3, 1)

            def body(b, par, known, it):
                for g in range(4):
                    u = b * 4 + g
                    act.wait_ge(s_mx, u + 1)
                    wait(act, s_T, u - 1)
                    for j in range(4):
                        last = nc.scalar.activation(Pe[g % 2][:, j, :], bS[g % 2][:, 128 * j:128 * j + 128], ACT.Exp,
                                                    bias=nmx[:, g % 2, j:j + 1])
                    last.then_inc(s_exp, 1)
                    if known != 0 or g > 0:
                        act.wait_ge(s_T, u)
                        wait(act, s_Of, u - 2)
                        nc.scalar.copy(PT[(g - 1) % 2][:].rearrange("p j q -> p (j q)"),
                                       bP[:, :]).then_inc(s_Te, 1)
                    if g == 1 and (known is None or known + 2 <= LAST):
                        sines(b + 2, par)
                    if known is None or known < LAST:
                        evict_g(b + 1, g)
                        evict_qk(b + 1, 1 - par, g)
                    if g == 3 and (known is None or known + 4 <= LAST):
                        logs(b + 4, par)
                    if known is not None and known >= B - 2:
                        start_nest(4 * (known - (B - 2)) + g)
            start_nest, run_nest = small_act(act, NEST)
            over_batches(act, body, 3)
            act.wait_ge(s_T, 4 * B)
            nc.scalar.copy(PT[1][:].rearrange("p j q -> p (j q)"), bP[:, :]).then_inc(s_Te, 1)

            if stop >= 2:
                run_nest()
            if stop >= 3:
                small_act(act, REL)[1]()
            if stop >= 4:
                experts_act(act)

        @block.vector
        def _(dve):
            chain = [0]

            def link(ins):
                chain[0] += 1
                ins.then_inc(s_c, 1)
                dve.wait_ge(s_c, chain[0])

            V_ = nc.vector
            V_.memset(mhalf[:], -0.5)
            V_.memset(epst[:], EPS)
            V_.memset(one[:], 1.0)
            for i, v in enumerate((100.0, 1.0 / TWO_PI, ROUND)):
                V_.memset(factor[:, i:i + 1], v)
            for par in range(2):
                V_.memset(kZ[par][0:64, :, 1, :], 0.0)
                V_.memset(kZ[par][64:128, :, 0, :], 0.0)
            dve.wait_ge(s_ldb, 64)
            def box_rows(part):
                V_.tensor_tensor(valM[64:128, part, :], rowM[64:128, part, :], valM[64:128, part, :], ALU.subtract)
                V_.tensor_tensor(valM[0:64, part, :], rowM[0:64, part, :], valM[0:64, part, :], ALU.add).then_inc(s_row, 1)
            V_.tensor_tensor(valN[64:128], pn[64:128, 1], pn[64:128, 0], ALU.subtract)
            V_.tensor_tensor(valN[0:64], pn[0:64, 0], pn[0:64, 1], ALU.add)
            box_rows(slice(0, EARLY))
            link(V_.tensor_tensor(scl[0:64], pn[0:64, 1], pn[0:64, 0], ALU.subtract))
            link(V_.tensor_scalar(scl[0:64], scl[0:64], 1.0, None, ALU.add))
            link(V_.reciprocal(scl[0:64], scl[0:64]))
            V_.memset(scl[64:128], -1.0)
            V_.tensor_scalar(scl[0:64], scl[0:64], 0.5, None, ALU.mult).then_inc(s_const, 1)
            dve.wait_ge(s_ldr, 32)
            box_rows(slice(EARLY, B))

            def magnitude(n, par):
                dve.wait_ge(s_scl, n + 1)
                Fu = F[par][0:64].bitcast(U32)
                V_.tensor_scalar(Fu, Fu, 0x7FFFFFFF, None, ALU.bitwise_and).then_inc(s_absb, 1)

            def bound(n, par):
                dve.wait_ge(s_absb, n + 1)
                V_.tensor_scalar(F[par][0:64], F[par][0:64], 1e-3, None, ALU.max).then_inc(s_abs, 1)

            def turns_off(n, par, part):
                if part == 0:
                    dve.wait_ge(s_turn, (n - 3) * 5 + 5)
                else:
                    dve.wait_ge(s_redc, (n - 3) * 2 + 1)
                V_.scalar_tensor_tensor(R[par], Kb, -(PI_HI, PI_LO)[part], R[par], ALU.mult, ALU.add).then_inc(s_redc, 1)

            def clamp(n, par):
                if isinstance(n, int) and n < 3:
                    dve.wait_ge(s_early, n + 1)
                else:
                    dve.wait_ge(s_redc, (n - 3) * 2 + 2)
                V_.tensor_scalar(R[par], R[par], phase[:, 2:3], phase[:, 3:4], ALU.max, ALU.min).then_inc(s_red, 1)

            def angles(n, par):
                dve.wait_ge(s_ln, n + 1)
                if n == 2:
                    dve.wait_ge(s_sin, 1)
                link(V_.tensor_scalar(R[par], F[par], 100.0, None, ALU.mult))
                V_.tensor_scalar(Kb, R[par], 1.0 / TWO_PI, phase[:, 0:1], ALU.mult, ALU.add).then_inc(s_early, 1)
                dve.wait_ge(s_early, n + 1)
                link(V_.tensor_scalar(Kb, Kb, ROUND, -ROUND, ALU.add, ALU.add))
                link(V_.scalar_tensor_tensor(R[par], Kb, -PI_HI, R[par], ALU.mult, ALU.add))
                if n < 2:
                    link(V_.scalar_tensor_tensor(R[par], Kb, -PI_LO, R[par], ALU.mult, ALU.add))
                    clamp(n, par)
                else:
                    link(V_.scalar_tensor_tensor(R[par], Kb, -PI_LO, R[par], ALU.mult, ALU.add))
                    V_.memset(spare[:, 1:2], 0.0).then_inc(s_early, 1)

            for n in range(2):
                magnitude(n, n)
                bound(n, n)
            angles(0, 0)

            dve.wait_ge(s_ldw, 16 * 11)
            for hg in range(2):
                last = V_.tensor_tensor(Wblk[:, hg], wrep[:, 8 * hg:8 * hg + 8].unsqueeze(2).to_broadcast([128, 8, NPF]),
                                        delta[:].unsqueeze(1).to_broadcast([128, 8, NPF]), ALU.mult)
            link(last)
            link(V_.tensor_scalar(bq[:], bq[:], DK ** -0.5, None, ALU.mult))
            dve.wait_ge(s_xb, 1)
            link(V_.tensor_scalar(bob[:], bob[:], gates[:, 0:1], None, ALU.mult))
            dve.wait_ge(s_ldx, 16)
            V_.memset(sums[:], 0.0).then_inc(s_wb, 1)

            def prep(n, par):
                xb = X[:, bass.ds(n, 1), :].rearrange("p a d -> p (a d)")
                V_.bn_stats(st6[:, par, :], xb).then_inc(s_st, 1)
                dve.wait_ge(s_st, n + 1)
                V_.memset(spare[:, par:par + 1], 0.0)
                V_.bn_aggr(mv[:, par, :], st6[:, par, :]).then_inc(s_mv, 1)

            def norm(n, par):
                xb = X[:, bass.ds(n, 1), :].rearrange("p a d -> p (a d)")
                dve.wait_ge(s_rstd, n + 1)
                wait(dve, s_mv, n + 1)
                V_.tensor_scalar(hS[par][:], xb, mv[:, par, 0:1], rstd[:, par:par + 1], ALU.subtract,
                                 ALU.mult).then_inc(s_h, 1)

            def evict_h(par, job):
                dve.wait_ge(s_V, job + 1)
                V_.tensor_copy(hTs[par][:], bV[:, 0:128]).then_inc(s_Ve, 1)

            def evict_v(par, g, job):
                dve.wait_ge(s_V, job + 1)
                V_.tensor_tensor(Vs[par][:, 256 * g:256 * g + 256], bV[:, 0:256], bvb[:, 256 * g:256 * g + 256],
                                 ALU.add).then_inc(s_Ve, 1)

            def evict_k(b1, par, g):
                dve.wait_ge(s_qke, b1 * 4 + (g + 1))
                for r in range(2):
                    rows = slice(64 * r, 64 * r + 64)
                    last = V_.tensor_tensor(kZ[par][rows, 2 * g:2 * g + 2, r, :],
                                            bA[rows, 256:512].rearrange("p (i k) -> p i k", i=2),
                                            bk[rows, 2 * g:2 * g + 2].unsqueeze(2).to_broadcast([64, 2, 128]), ALU.add)
                last.then_inc(s_ke, 1)

            def evict_o(b, g):
                while g < 0:
                    g += 4
                    b = b - 1
                dve.wait_ge(s_Of, b * 4 + (g + 1))
                dve.wait_ge(s_rs, b * 4 + (g + 1))
                V_.tensor_tensor(Os[:, 4 * g:4 * g + 4, :], bO[:, 0:256].rearrange("p (j d) -> p j d", j=4),
                                 rs[:, g, :].unsqueeze(2).to_broadcast([128, 4, DK]), ALU.mult).then_inc(s_Oe, 1)

            def evict_ot(n, half):
                dve.wait_ge(s_ot, n * 2 + (half + 1))
                V_.tensor_copy(OTs[:, 4 * half:4 * half + 4, :].rearrange("p t q -> p (t q)"), bY1[:, :]).then_inc(s_ote, 1)

            def evict_y(n):
                dve.wait_ge(s_y, n + 1)
                V_.scalar_tensor_tensor(xrow(n), bY1[:, 0:128], gates[:, 0:1], xrow(n), ALU.mult, ALU.add).then_inc(s_ye, 1)
                dve.wait_ge(s_ye, n + 1)
                V_.tensor_tensor(xrow(n), xrow(n), bob[:], ALU.add).then_inc(s_x1, 1)

            for n in range(3):
                prep(n, n % 2)
                if n < 2:
                    norm(n, n)
            evict_h(0, 0)
            evict_h(1, 1)
            angles(1, 1)
            for g in range(4):
                evict_k(0, 0, g)
                evict_v(0, g, vjob(-1, g))
                if g in (1, 2):
                    magnitude(g + 1, (g + 1) % 2)
                    bound(g + 1, (g + 1) % 2)
            angles(2, 0)

            def top(b, g):
                u = b * 4 + g
                dve.wait_ge(s_S, u + 1)
                wait(dve, s_exp, u - 1)
                V_.tensor_reduce(nmx[:, g % 2, :], bS[g % 2][:, :].rearrange("p (j k) -> p j k", j=4), AX.X,
                                 ALU.max, negate=True).then_inc(s_mx, 1)

            top(0, 0)

            def body(b, par, known, it):
                for g in range(4):
                    u = b * 4 + g
                    first = known == 0
                    more = known is None or known < LAST
                    if g == 3 and not first:
                        evict_ot(b - 1, 0)
                    if more or g < 3:
                        top(b + (g + 1) // 4, (g + 1) % 4)
                    if not (first and g == 0):
                        dve.wait_ge(s_P, u)
                        V_.reciprocal(rs[:, (g - 1) % 4, :], sums[:, (g - 1) % 4, :]).then_inc(s_rs, 1)
                    if not (first and g < 3):
                        evict_o(b, g - 3)
                    if g == 1 and (known is None or known + 3 <= LAST):
                        prep(b + 3, 1 - par)
                    if g == 0 and (known is None or known + 2 <= LAST):
                        norm(b + 2, par)
                    dve.wait_ge(s_exp, u + 1)
                    if g % 2 == 0:
                        dve.wait_ge(s_gd[g // 2], (b + 1) * GD)
                    for j in range(4):
                        last = V_.scalar_tensor_tensor(Pe[g % 2][:, j, :], G[par][:, 4 * g + j, :], GMIN,
                                                       Pe[g % 2][:, j, :], ALU.max, ALU.mult,
                                                       accum_out=sums[:, g, j:j + 1])
                    last.then_inc(s_P, 1)
                    if g == 3 and not first:
                        evict_ot(b - 1, 1)
                    if g == 0 and known not in (0, 1):
                        evict_y(b - 2)
                    if more:
                        evict_k(b + 1, 1 - par, g)
                        evict_v(1 - par, g, vjob(b, g))
                    two, three, four = (known is None or known + n <= LAST for n in (2, 3, 4))
                    if g == 0 and two:
                        clamp(b + 2, par)
                    if g == 0 and four:
                        magnitude(b + 4, par)
                    if g == 1 and four:
                        bound(b + 4, par)
                    if g in (2, 3) and three:
                        turns_off(b + 3, 1 - par, g - 2)
                    if known is not None and known >= B - 2:
                        start_nest(4 * (known - (B - 2)) + g)
                if known is None or known + 2 <= LAST:
                    evict_h(par, vjob(b, 4))
            start_rel, run_rel = small_dve(dve, REL, link)
            start_nest, run_nest = small_dve(dve, NEST, link, start_rel)
            over_batches(dve, body, 3)
            dve.wait_ge(s_P, 4 * B)
            V_.reciprocal(rs[:, 3, :], sums[:, 3, :]).then_inc(s_rs, 1)
            evict_y(B - 2)
            evict_o(B, -3)
            evict_o(B, -2)
            evict_o(B, -1)
            evict_ot(LAST, 0)
            evict_ot(LAST, 1)
            evict_y(LAST)

            if stop >= 2:
                run_nest()
            if stop >= 3:
                run_rel()
            if stop >= 4:
                experts_dve(dve, link)

        @block.tensor
        def _(pe):
            M = nc.tensor.matmul

            def mm(o, l, r, start=True, stop=True):
                return M(o, l, r, start=start, stop=stop)

            def job_h(n, par, job):
                pe.wait_ge(s_h, n + 1)
                wait(pe, s_Ve, job)
                nc.tensor.transpose(bV[:, 0:128], hS[par][:], ident[:]).then_inc(s_V, 1)

            def job_v(n, par, g, job, half):
                if g == 0:
                    pe.wait_ge(s_ctx[par], (half + 1) * 16)
                wait(pe, s_Ve, job)
                mm(bV[:, 0:256], ctxS[par][:], WvT[:, 256 * g:256 * g + 256]).then_inc(s_V, 1)

            def job_qk(n, par, g, hjob, half):
                if g == 0:
                    pe.wait_ge(s_Ve, hjob + 1)
                    pe.wait_ge(s_ctx[par], (half + 1) * 16)
                wait(pe, s_ke, n * 4 + g)
                for i in range(2):
                    t = 2 * g + i
                    mm(bA[:, 128 * i:128 * i + 128], WqT[:, 128 * t:128 * t + 128], hTs[par][:])
                for i in range(2):
                    t = 2 * g + i
                    last = mm(bA[:, 256 + 128 * i:384 + 128 * i], WkT[:, 128 * t:128 * t + 128], ctxS[par][:])
                last.then_inc(s_qk, 1)

            def job_g(n, par, g):
                if g == 0:
                    pe.wait_ge(s_sin, n + 1)
                wait(pe, s_Ge, n * 4 + g)
                hg, half = g // 2, g % 2
                mm(bG[:, :], Wblk[:, hg].rearrange("p h n -> p (h n)"),
                   E[par][:, 4 * half:4 * half + 4, :].rearrange("p c m -> p (c m)")).then_inc(s_G, 1)

            def job_t(b, g):
                while g < 0:
                    g += 4
                    b = b - 1
                u = b * 4 + g
                pe.wait_ge(s_P, u + 1)
                wait(pe, s_Te, u)
                for j in range(4):
                    last = nc.tensor.transpose(bP[:, 128 * j:128 * j + 128], Pe[g % 2][:, j, :], ident[:])
                last.then_inc(s_T, 1)

            def job_pv(b, g, par):
                while g < 0:
                    g += 4
                    b = b - 1
                    par = 1 - par
                pe.wait_ge(s_Te, b * 4 + (g + 1))
                wait(pe, s_Oe, b * 4 + g)
                if g == 0:
                    wait(pe, s_Ve, vjob(b - 1, 3) + 1)
                for j in range(4):
                    h = 4 * g + j
                    last = mm(bO[:, 64 * j:64 * j + 64], PT[g % 2][:, j, :], Vs[par][:, 64 * h:64 * h + 64])
                last.then_inc(s_Of, 1)

            def job_ot(n, half):
                pe.wait_ge(s_Oe, n * 4 + 4)
                if half == 0:
                    wait(pe, s_ye, n)
                else:
                    pe.wait_ge(s_ote, n * 2 + 1)
                for i in range(4):
                    t = 4 * half + i
                    last = nc.tensor.transpose(bY1[:, 128 * i:128 * i + 128],
                                               Os[:, 2 * t:2 * t + 2, :].rearrange("p h d -> p (h d)"), ident[:])
                last.then_inc(s_ot, 1)

            def job_y(n):
                pe.wait_ge(s_ote, n * 2 + 2)
                for t in range(PAIRS):
                    last = mm(bY1[:, 0:128], OTs[:, t, :], WoT[:, t, :], start=t == 0, stop=t == PAIRS - 1)
                last.then_inc(s_y, 1)

            def job_s(b, g, par):
                u = b * 4 + g
                pe.wait_ge(s_ke, u + 1)
                wait(pe, s_exp, u - 1)
                for i in range(2):
                    t = 2 * g + i
                    last = mm(bS[g % 2][:, 256 * i:256 * i + 256], qS[par][:, t, :],
                              kZ[par][:, t, :, :].rearrange("p r k -> p (r k)"))
                last.then_inc(s_S, 1)

            pe.wait_ge(s_ld, 32)
            pe.wait_ge(s_wb, 1)
            job_h(0, 0, 0)
            job_h(1, 1, 1)
            for g in range(4):
                job_g(0, 0, g)
                job_qk(0, 0, g, 0, 0)
                job_v(0, 0, g, vjob(-1, g), 0)
            job_s(0, 0, 0)

            def body(b, par, known, it):
                first = known == 0
                more = known is None or known < LAST
                for g in range(4):
                    if g < 3:
                        job_s(b, g + 1, par)
                    elif more:
                        job_s(b + 1, 0, 1 - par)
                    if more:
                        job_g(b + 1, 1 - par, g)
                    if g == 3 and not first:
                        job_ot(b - 1, 1)
                    if not (first and g == 0):
                        job_t(b, g - 1)
                    if more:
                        job_qk(b + 1, 1 - par, g, 1 if first else vjob(b - 1, 4), it + par)
                    if g == 0 and known not in (0, 1):
                        job_y(b - 2)
                    if more:
                        job_v(b + 1, 1 - par, g, vjob(b, g), it + par)
                    if not (first and g < 2):
                        job_pv(b, g - 2, par)
                    if g == 2 and not first:
                        job_ot(b - 1, 0)
                    if known is not None and known >= B - 2:
                        start_nest(4 * (known - (B - 2)) + g)
                if known is None or known + 2 <= LAST:
                    job_h(b + 2, par, vjob(b, 4))
            start_rel, run_rel = small_pe(pe, REL, NEST.s_x)
            start_nest, run_nest = small_pe(pe, NEST, s_x1, start_rel)
            over_batches(pe, body, 3)
            job_t(B, -1)
            job_y(B - 2)
            job_pv(B, -2, 0)
            job_pv(B, -1, 0)
            job_ot(LAST, 0)
            job_ot(LAST, 1)
            job_y(LAST)
            if stop >= 2:
                run_nest()
            if stop >= 3:
                run_rel()
            if stop >= 4:
                experts_pe(pe)


NAMES = ["x", "ctxT", "ident", "gates", "box_pn", "box_row", "phase", "wg", "delta", "bg", "WqT", "WkT", "WvT",
         "WoT", "bq", "bk", "bv", "bo", "rel_bias", "mask", "norm_wb", "wide", "wideT"]
NAMES += ["W_e", "V_e", "W_out", "rwT", "ustrict", "rb", "iota8", "token", "owner", "blank"]
NAMES += [f"{x}_{n}" for n in ("nest", "rel") for x in ("Wq", "Wk", "Wv", "Wo", "bq", "bk", "hm", "bv", "bo")]


def layouts(I):
    a = {k: np.asarray(v) for k, v in I.items()}
    f32 = np.float32
    L = {}
    L["x"] = a["x"]
    L["ctxT"] = a["ctx_1024"].transpose(2, 0, 1)
    L["ident"] = np.eye(128, dtype=f32)
    L["gates"] = np.array([a["g_xattn"][0], a["g_ffn"][0], a["g_xattn"][1], a["g_ffn"][1]], f32)
    box = a["fside_BxSx4_0"]
    axis = [0, 1, 0, 1, 0, 1, 0, 1]
    lo, hi = box[:, :, axis], box[:, :, [2 + i for i in axis]]
    both = np.stack([lo, hi])
    L["box_pn"] = both.reshape(2, B, NPF, NC, NF).transpose(4, 2, 0, 1, 3).reshape(128, 2, B, NC)
    L["box_row"] = np.repeat(both.transpose(0, 3, 1, 2), NPF, axis=1)
    order = [0, 1, 4, 5, 2, 3, 6, 7]
    L["wg"] = np.repeat(a["L0_xattn_Wg"][:, order].T, NPF, axis=0)
    L["delta"] = np.tile(np.eye(NPF, dtype=f32), (NF, 1))
    cos = np.repeat(np.array([0, 0, 1, 1, 0, 0, 1, 1], f32), NPF)
    bias = (cos * f32(math.pi / 2)).astype(f32)
    L["phase"] = np.stack([cos * f32(0.25), bias, -f32(PI_SAFE) - bias, f32(PI_SAFE) - bias], 1).astype(f32)
    L["bg"] = np.repeat(a["L0_xattn_bg"].reshape(2, 8).T, NPF, axis=0)
    for n in "qkv":
        L[f"W{n}T"] = a[f"L0_xattn_W{n}"].T
    L["WoT"] = a["L0_xattn_Wo"].T.reshape(PAIRS, 128, 128).transpose(1, 0, 2)
    L["bq"] = a["L0_xattn_bq"].reshape(PAIRS, 128).T
    L["bk"] = a["L0_xattn_bk"].reshape(PAIRS, 128).T
    L["bv"] = a["L0_xattn_bv"]
    L["bo"] = a["L0_xattn_bo"]
    for n, w, src in (("nest", 16, "L0_ffn_{}_{}"), ("rel", 8, "L1_xattn_{}{}")):
        for x in "qkvo":
            name, bname = (src.format(x, "w"), src.format(x, "b")) if n == "nest" else (src.format("W", x), src.format("b", x))
            L[f"W{x}_{n}"] = a[name].T
            L[f"b{x}_{n}"] = a[bname].reshape(128, 1) if x in "qk" else a[bname]
        L[f"hm_{n}"] = np.repeat(np.eye(128 // w, dtype=f32), w, axis=0)
    L["norm_wb"] = np.stack([a["L0_ffn_norm_w"], a["L0_ffn_norm_b"]], 1)
    experts = a["L0_ffn_router_prob"].shape[2]
    reach = D // 2 ** (np.arange(S) // (S // experts))
    L["wide"] = (np.arange(D)[None, :] < reach[:, None]).astype(f32)
    L["wideT"] = L["wide"].T
    L["mask"] = a["mask_Bx1x1xS2_ik0"].reshape(B, S)
    rel = a["L1_xattn_rel_emb"]
    most = (rel.shape[0] - 1) // 2
    at = np.clip(np.arange(S)[None, :] - np.arange(S)[:, None], -most, most) + most
    L["rel_bias"] = rel[at].transpose(0, 2, 1)
    L["W_e"] = a["L1_ffn_W"].transpose(1, 0, 2).reshape(D, 2 * NE, 128)
    L["V_e"] = a["L1_ffn_V"].transpose(1, 0, 2).reshape(D, 2 * NE, 128)
    L["W_out"] = a["L1_ffn_W_out"].reshape(NE, 2, 128, D).transpose(2, 0, 1, 3)
    L["rwT"] = a["L1_ffn_router_w"].T
    L["rb"] = a["L1_ffn_router_b"]
    L["iota8"] = np.arange(NE, dtype=f32)
    L["token"] = (np.arange(B)[None, :] * S + np.arange(S)[:, None]).astype(np.int32)
    L["owner"] = (np.arange(SLOTS // 128) * 128 // CAP).astype(f32)
    L["blank"] = np.array([0] * (ROW - 1) + [1 << 20], np.int32)
    L["ustrict"] = np.triu(np.ones((128, 128), f32), 1)
    return {k: np.ascontiguousarray(v) for k, v in L.items()}


def kernel(**inputs):
    import concourse.bacc as bacc
    from concourse.bass_utils import run_bass_kernel_spmd

    L = layouts(inputs)
    nc = bacc.Bacc("TRN2", target_bir_lowering=False, num_devices=1)
    A = {n: nc.dram_tensor(n + "_dram", L[n].shape, mybir.dt.from_np(L[n].dtype), kind="ExternalInput").ap()
         for n in NAMES}
    out = nc.dram_tensor("out_dram", (B, S, D), F32, kind="ExternalOutput").ap()
    build_program(nc, A, out)
    r = run_bass_kernel_spmd(nc, [{n + "_dram": L[n] for n in NAMES}], core_ids=[0])
    return r.results[0]["out_dram"]
```
